# Optimizing a Trainium2 kernel written in Bass

```python
import numpy as np
import jax
import jax.numpy as jnp

def _softmax(x, axis=-1):
    return jax.nn.softmax(x, axis=axis)

def _gelu(x):
    return jax.nn.gelu(x, approximate=True)

def _silu(x):
    return jax.nn.silu(x)

def _sigmoid(x):
    return jax.nn.sigmoid(x)

def _layernorm(x, axis=-1, eps=1e-05):
    m = jnp.mean(x, axis=axis, keepdims=True)
    v = jnp.var(x, axis=axis, keepdims=True)
    return (x - m) / jnp.sqrt(v + eps)

def _scatter_add(tgt, idx, src, axis=0):
    return tgt.at[idx].add(src)

def _segment_sum(src, seg, n):
    return jax.ops.segment_sum(src, seg, n)
kernel_name = 'mk_seq_postln_d1_jaxref_r8_7db3f8'

def setup_inputs(seed: int=0):
    np.random.seed(seed)
    _w = jnp.asarray

    def _L0_attn_setup():
        import jax, jax.numpy as jnp
        import numpy as np
        N_HEADS = 16
        key = jax.random.key(seed)
        ks = jax.random.split(key, 8)
        B, T, D = (2, 256, 128)
        hd, rank = (D // N_HEADS, 32)
        std = 0.02
        inp = {'x': jax.random.normal(ks[0], (B, T, D), jnp.float32), 'Wq': jax.random.normal(ks[1], (D, D), jnp.float32) * std, 'bq': jnp.zeros((D,), jnp.float32), 'Wk': jax.random.normal(ks[2], (D, D), jnp.float32) * std, 'bk': jnp.zeros((D,), jnp.float32), 'Wv': jax.random.normal(ks[3], (D, D), jnp.float32) * std, 'bv': jnp.zeros((D,), jnp.float32), 'Wo': jax.random.normal(ks[4], (D, D), jnp.float32) * std, 'bo': jnp.zeros((D,), jnp.float32), 'U': jnp.linalg.qr(jax.random.normal(ks[5], (hd, rank), jnp.float32))[0], 'V': jnp.linalg.qr(jax.random.normal(ks[6], (hd, rank), jnp.float32))[0]}
        return inp
    _L0_attn_in = _L0_attn_setup()

    def _L0_ffn_setup():
        import jax, jax.numpy as jnp
        import numpy as np
        D_MODEL = 128
        NUM_EXPERTS = 8
        HIDDEN = 512
        TOP_K = 2
        key = jax.random.key(seed)
        ks = jax.random.split(key, 6)
        x = jax.random.normal(ks[0], (2, 128, D_MODEL), dtype=jnp.float32)
        gate_w = jax.random.normal(ks[1], (NUM_EXPERTS, D_MODEL), dtype=jnp.float32) * (1.0 / np.sqrt(D_MODEL))
        w1 = jax.random.normal(ks[2], (NUM_EXPERTS, HIDDEN, D_MODEL), dtype=jnp.float32) * (1.0 / np.sqrt(D_MODEL))
        b1 = jax.random.normal(ks[3], (NUM_EXPERTS, HIDDEN), dtype=jnp.float32) * 0.01
        w2 = jax.random.normal(ks[4], (NUM_EXPERTS, D_MODEL, HIDDEN), dtype=jnp.float32) * (1.0 / np.sqrt(HIDDEN))
        b2 = jax.random.normal(ks[5], (NUM_EXPERTS, D_MODEL), dtype=jnp.float32) * 0.01
        return {'x': x, 'gate_w': gate_w, 'w1': w1, 'b1': b1, 'w2': w2, 'b2': b2}
    _L0_ffn_in = _L0_ffn_setup()
    _d = {'L0_attn_x': _L0_attn_in['x'], 'L0_attn_Wq': _L0_attn_in['Wq'], 'L0_attn_bq': _L0_attn_in['bq'], 'L0_attn_Wk': _L0_attn_in['Wk'], 'L0_attn_bk': _L0_attn_in['bk'], 'L0_attn_Wv': _L0_attn_in['Wv'], 'L0_attn_bv': _L0_attn_in['bv'], 'L0_attn_Wo': _L0_attn_in['Wo'], 'L0_attn_bo': _L0_attn_in['bo'], 'L0_attn_U': _L0_attn_in['U'], 'L0_attn_V': _L0_attn_in['V'], 'L0_ffn_gate_w': _L0_ffn_in['gate_w'], 'L0_ffn_w1': _L0_ffn_in['w1'], 'L0_ffn_b1': _L0_ffn_in['b1'], 'L0_ffn_w2': _L0_ffn_in['w2'], 'L0_ffn_b2': _L0_ffn_in['b2']}
    _x0 = _d['L0_attn_x']
    _d['L0_attn_x'] = jax.random.normal(jax.random.fold_in(jax.random.key(seed), 1), (16, 512, 128), dtype=_x0.dtype)
    del _x0
    return _d

def reference(L0_attn_x, L0_attn_Wq, L0_attn_bq, L0_attn_Wk, L0_attn_bk, L0_attn_Wv, L0_attn_bv, L0_attn_Wo, L0_attn_bo, L0_attn_U, L0_attn_V, L0_ffn_gate_w, L0_ffn_w1, L0_ffn_b1, L0_ffn_w2, L0_ffn_b2):

    def _L0_attn_ref(x, Wq, bq, Wk, bk, Wv, bv, Wo, bo, U, V):
        import jax, jax.numpy as jnp
        import numpy as np
        N_HEADS = 16
        B, T, D = x.shape
        H = N_HEADS
        hd = D // H
        rank = V.shape[1]
        q = (x @ Wq.T + bq).reshape(B, T, H, hd).transpose(0, 2, 1, 3)
        k = (x @ Wk.T + bk).reshape(B, T, H, hd).transpose(0, 2, 1, 3)
        v = (x @ Wv.T + bv).reshape(B, T, H, hd).transpose(0, 2, 1, 3)
        zq = q @ V
        zk = k @ V
        zv = v @ V
        att = jnp.einsum('bhqr,bhkr->bhqk', zq, zk) / jnp.sqrt(jnp.float32(max(rank, 1)))
        att = jax.nn.softmax(att, axis=-1)
        y_r = jnp.einsum('bhqk,bhkr->bhqr', att, zv)
        y = y_r @ U.T
        y = y.transpose(0, 2, 1, 3).reshape(B, T, D)
        return y @ Wo.T + bo

    def _L0_ffn_ref(x, gate_w, w1, b1, w2, b2):
        import jax, jax.numpy as jnp
        import numpy as np
        D_MODEL = 128
        NUM_EXPERTS = 8
        HIDDEN = 512
        TOP_K = 2
        B, S, D = x.shape
        xf = x.reshape(-1, D)
        T = xf.shape[0]
        gate_logits = xf @ gate_w.T
        gate_probs = jax.nn.softmax(gate_logits, axis=-1)
        topk_scores, topk_idx = jax.lax.top_k(gate_probs, TOP_K)
        topk_scores = topk_scores / jnp.sum(topk_scores, axis=-1, keepdims=True)
        combine = jnp.zeros((T, NUM_EXPERTS), dtype=x.dtype)
        combine = combine.at[jnp.arange(T)[:, None], topk_idx].set(topk_scores)
        h = jax.nn.relu(jnp.einsum('td,ehd->teh', xf, w1) + b1)
        expert_out = jnp.einsum('teh,edh->ted', h, w2) + b2
        out = jnp.einsum('ted,te->td', expert_out, combine)
        return out.reshape(B, S, D)
    x = L0_attn_x
    x = _layernorm(x + _L0_attn_ref(x, L0_attn_Wq, L0_attn_bq, L0_attn_Wk, L0_attn_bk, L0_attn_Wv, L0_attn_bv, L0_attn_Wo, L0_attn_bo, L0_attn_U, L0_attn_V), axis=-1)
    x = _layernorm(x + _L0_ffn_ref(x, L0_ffn_gate_w, L0_ffn_w1, L0_ffn_b1, L0_ffn_w2, L0_ffn_b2), axis=-1)
    return x

_drawn_inputs = setup_inputs


def setup_inputs(seed=0):
    import zlib

    import numpy as np

    out = dict(_drawn_inputs(seed))
    spreads = {'L0_attn_bq': (0.0, 0.8),
     'L0_attn_bk': (0.0, 0.8),
     'L0_attn_bv': (0.0, 0.1),
     'L0_attn_bo': (0.0, 0.1)}
    factors = {'L0_attn_Wq': 8.0,
     'L0_attn_Wk': 8.0,
     'L0_attn_Wv': 3.771,
     'L0_ffn_b1': 8.0,
     'L0_ffn_b2': 8.0}
    for name, (base, spread) in spreads.items():
        noise = np.random.default_rng([zlib.crc32(name.encode()), seed]).standard_normal(out[name].shape)
        drawn = base * np.exp(spread * noise) if base else spread * noise
        out[name] = jnp.asarray(drawn.astype(out[name].dtype))
    for name, factor in factors.items():
        out[name] = (out[name] * factor).astype(out[name].dtype)
    return out
```

```python
import concourse.bass as bass
from concourse import mybir
from contextlib import ExitStack

B, T, D = 16, 512, 128
H, R = 16, 8
E, HID = 8, 512
P = 128
QT = T // P
HB = HID // P
EPS = 1e-5

HG = 4
UNITS = H * QT
GROUP = UNITS // HG
SLOTS = 6
PROD_ROWS = SLOTS * R
MAX_ROW = 96
STACK = MAX_ROW + 3
P_RING = 16
AV_LAG = 6
V_COLS = R + 1
Q_RUNS = ((0, 0, 3), (3, 0, 2), (5, 0, 1))
K_PARTS = (0, 0, 0, 1, 1, 2)


class Batch:

    def __init__(self, i, c):
        self.i, self.c = i, c
        self.parity = c % 2

    def __add__(self, d):
        return Batch(self.i, self.c + d)

    def count(self, per_batch, events):
        return self.i * (2 * per_batch) + (self.c * per_batch + events)

    def count_parity(self, per_batch, events):
        return self.i * per_batch + ((self.c // 2) * per_batch + events)

    def row(self):
        return self.i * (2 * T) + self.c * T


def wait(engine, sem, value):
    if isinstance(value, int) and value <= 0:
        return
    engine.wait_ge(sem, value)


def build_layer(nc, x, wq, bq, wk, bk, wv, bv, wo, bo, u, v, gate_w, w1, b1, w2, b2, out):
    fp32, bf16 = mybir.dt.float32, mybir.dt.bfloat16
    ALU, ACT, AX = mybir.AluOpType, mybir.ActivationFunctionType, mybir.AxisListType
    SCALE = float(v.shape[1]) ** -0.5

    x_rows = x.rearrange("b t d -> (b t) d")
    out_rows = out.rearrange("b t d -> (b t) d")
    q_parts_d = [nc.dram_tensor(f"q_parts_d{n}", (3 * R, H, T), bf16, kind="Internal").ap() for n in range(2)]
    k_parts_d = [nc.dram_tensor(f"k_parts_d{n}", (3 * R, H, T), bf16, kind="Internal").ap() for n in range(2)]
    x1_d = nc.dram_tensor("x1_d", (B * T, D), fp32, kind="Internal").ap()

    top = ExitStack()

    def sem(name):
        return top.enter_context(nc.semaphore(name))

    with top:
        def sb(name, shape, dt=fp32):
            return top.enter_context(nc.sbuf_tensor(name, shape, dt))

        ident = sb("ident", [P, P])
        eps_t = sb("eps_t", [P, QT])
        neg_half = sb("neg_half", [P, QT])
        wq_t = sb("wq_t", [P, P])
        wk_t = sb("wk_t", [P, P])
        wv_t = sb("wv_t", [P, P])
        wo_t = sb("wo_t", [P, P])
        bq_c = sb("bq_c", [P, 1])
        bk_c = sb("bk_c", [P, 1])
        bv_b = sb("bv_b", [P, P])
        bo_b = sb("bo_b", [P, P])

        att = ExitStack()
        with att:
            def asb(name, shape, dt=fp32):
                return att.enter_context(nc.sbuf_tensor(name, shape, dt))

            k_stack = [asb(f"k_stack{n}", [P, H, T], bf16) for n in range(2)]
            q_stack = [asb(f"q_stack{n}", [P, H, T], bf16) for n in range(2)]
            probs = asb("probs", [P, P_RING, T])
            v_one = [asb(f"v_one{n}", [P, QT, H, V_COLS]) for n in range(2)]
            x_in = [asb(f"x_in{n}", [P, QT, D]) for n in range(2)]
            x_res = [asb(f"x_res{n}", [P, QT, D]) for n in range(2)]
            x_bo = asb("x_bo", [P, QT, D])
            x_t = [asb(f"x_t{n}", [P, T]) for n in range(2)]
            q_f = asb("q_f", [P, T])
            k_f = asb("k_f", [P, T])
            rest = asb("rest", [P, T])
            zeros = asb("zeros", [P, T])
            q_parts = asb("q_parts", [P, 3, T], bf16)
            k_parts = asb("k_parts", [P, 3, T], bf16)
            row_max = asb("row_max", [P, UNITS])
            HALF = UNITS // 2
            neg_max = [asb(f"neg_max{n}", [HALF, P]) for n in range(2)]
            max_rest = asb("max_rest", [HALF, P])
            max_parts = [asb(f"max_parts{n}", [HALF, 3, P], bf16) for n in range(2)]
            y_sb = [asb(f"y_sb{n}", [P, T]) for n in range(2)]
            inv_sum = asb("inv_sum", [P, HG, QT, HG])
            y_norm = asb("y_norm", [P, QT, H, R])
            y_t = asb("y_t", [P, T])
            res = asb("res", [P, QT, D])
            stats = asb("stats", [P, QT, 6])
            mean_var = asb("mean_var", [P, QT, 2])
            var_eps = asb("var_eps", [P, QT])
            rstd = asb("rstd", [P, QT])
            x1_sb = asb("x1_sb", [P, QT, D])
            w_nat = asb("w_nat", [P, 4, P])
            vu = asb("vu", [R, 2, R])
            bcols = asb("bcols", [P, 3])
            rep = asb("rep", [R, H, R])
            head_mask = asb("head_mask", [P, H])
            vu_rep = asb("vu_rep", [P, 2, R])
            v_rh = asb("v_rh", [P, R, H])
            v_hr = asb("v_hr", [P, H, R])
            u_hr = asb("u_hr", [P, H, R])
            wo_nt = asb("wo_nt", [P, P])
            bv_wide = asb("bv_wide", [P, P])

            st_ps = [att.enter_context(nc.psum_tensor(f"st_ps{n}", [P, T], fp32)) for n in range(2)]
            sm_ps = [att.enter_context(nc.psum_tensor(f"sm_ps{n}", [P, 2, T], fp32)) for n in range(2)]
            av_ps = att.enter_context(nc.psum_tensor("av_ps", [P, T], fp32))
            misc_ps = att.enter_context(nc.psum_tensor("misc_ps", [P, T], fp32))

            w_loaded, vu_loaded, b_loaded, bo_loaded = (sem(n) for n in ("w_loaded", "vu_loaded", "b_loaded", "bo_loaded"))
            const_ready, pool_setup = sem("const_ready"), sem("pool_setup")
            pe_setup, dve_setup = sem("pe_setup"), sem("dve_setup")
            with nc.Block() as block:
                @block.sync
                def _(sp):
                    for n, w in enumerate((wq, wk, wv, wo)):
                        sp.dma_start(w_nat[:, n, :], w).then_inc(w_loaded, 16)
                    for n, w in enumerate((v, u)):
                        sp.dma_start(vu[:, n, :], w).then_inc(vu_loaded, 16)
                    for n, w in enumerate((bq, bk, bv)):
                        sp.dma_start(bcols[:, n:n + 1], w.rearrange("(p a) -> p a", a=1)).then_inc(b_loaded, 16)
                    sp.dma_start(bo_b[:, :], bo.rearrange("(a n) -> a n", a=1).to_broadcast([P, D])).then_inc(bo_loaded, 16)
                    sp.wait_ge(bo_loaded, 16)

                @block.gpsimd
                def _(pool):
                    nc.gpsimd.memset(ident[:, :], 0.0).then_inc(pool_setup, 1)
                    nc.gpsimd.memset(rep[:, :, :], 0.0).then_inc(pool_setup, 1)
                    nc.gpsimd.memset(head_mask[:, :], 1.0).then_inc(pool_setup, 1)
                    pool.wait_ge(pool_setup, 3)
                    nc.gpsimd.affine_select(out=ident[:, :], in_=ident[:, :], compare_op=ALU.not_equal, fill=1.0,
                                            base=0, pattern=[[-1, P]], channel_multiplier=1).then_inc(const_ready, 1)
                    nc.gpsimd.affine_select(out=rep[:, :, :], in_=rep[:, :, :], compare_op=ALU.not_equal, fill=1.0,
                                            base=0, pattern=[[0, H], [-1, R]], channel_multiplier=1).then_inc(const_ready, 1)
                    nc.gpsimd.affine_select(out=head_mask[:, :], in_=head_mask[:, :], compare_op=ALU.is_ge, fill=0.0,
                                            base=0, pattern=[[-R, H]], channel_multiplier=1).then_inc(pool_setup, 1)
                    pool.wait_ge(pool_setup, 4)
                    nc.gpsimd.affine_select(out=head_mask[:, :], in_=head_mask[:, :], compare_op=ALU.is_ge, fill=0.0,
                                            base=R - 1, pattern=[[R, H]], channel_multiplier=-1).then_inc(const_ready, 1)
                    nc.gpsimd.memset(eps_t[:, :], EPS).then_inc(const_ready, 1)
                    nc.gpsimd.memset(neg_half[:, :], -0.5).then_inc(const_ready, 1)
                    nc.gpsimd.memset(zeros[:, :], 0.0).then_inc(const_ready, 1)
                    for n in range(2):
                        nc.gpsimd.memset(v_one[n][:, :, :, R:R + 1], 1.0).then_inc(const_ready, 1)

                @block.tensor
                def _(pe):
                    pe.wait_ge(const_ready, 3)
                    pe.wait_ge(vu_loaded, 32)
                    for n in range(2):
                        last = nc.tensor.matmul(misc_ps[:, n * R:(n + 1) * R], rep[:, :, :].rearrange("p h d -> p (h d)"),
                                                vu[:, n, :], start=True, stop=True)
                    last.then_inc(pe_setup, 1)
                    pe.wait_ge(w_loaded, 64)
                    nc.tensor.transpose(st_ps[0][:, 0:P], w_nat[:, 3, :], ident[:, :]).then_inc(pe_setup, 1)
                    pe.wait_ge(dve_setup, 5)
                    pe.wait_ge(b_loaded, 48)
                    vrh = v_rh[:, :, :].rearrange("p r h -> p (r h)")
                    vhr = v_hr[:, :, :].rearrange("p h r -> p (h r)")
                    nc.tensor.matmul(sm_ps[0][:, 0, 0:P], w_nat[:, 0, :], vrh, start=True, stop=True)
                    nc.tensor.matmul(sm_ps[0][:, 0, P:2 * P], w_nat[:, 1, :], vrh, start=True, stop=True)
                    nc.tensor.matmul(sm_ps[0][:, 0, 2 * P:3 * P], w_nat[:, 2, :], vhr, start=True, stop=True).then_inc(pe_setup, 1)
                    nc.tensor.matmul(sm_ps[1][:, 0, 0:1], vrh, bcols[:, 0:1], start=True, stop=True)
                    nc.tensor.matmul(sm_ps[1][:, 0, 1:2], vrh, bcols[:, 1:2], start=True, stop=True)
                    nc.tensor.matmul(sm_ps[1][:, 0, P:2 * P], bv_wide[:, :], vhr, start=True, stop=True).then_inc(pe_setup, 1)
                    pe.wait_ge(dve_setup, 6)
                    nc.tensor.matmul(sm_ps[1][:, 1, 0:P], u_hr[:, :, :].rearrange("p h r -> p (h r)"), wo_nt[:, :],
                                     start=True, stop=True).then_inc(pe_setup, 1)

                @block.vector
                def _(dve):
                    dve.wait_ge(pe_setup, 1)
                    nc.vector.tensor_copy(vu_rep[:, :, :].rearrange("p a r -> p (a r)"), misc_ps[:, 0:2 * R]).then_inc(dve_setup, 1)
                    dve.wait_ge(dve_setup, 1)
                    dve.wait_ge(const_ready, 3)
                    mask_h = head_mask[:, :].unsqueeze(1).to_broadcast([P, R, H])
                    mask_r = head_mask[:, :].unsqueeze(2).to_broadcast([P, H, R])
                    nc.vector.tensor_tensor(v_rh[:, :, :], vu_rep[:, 0, :].unsqueeze(2).to_broadcast([P, R, H]), mask_h, ALU.mult).then_inc(dve_setup, 1)
                    nc.vector.tensor_tensor(v_hr[:, :, :], vu_rep[:, 0, :].unsqueeze(1).to_broadcast([P, H, R]), mask_r, ALU.mult).then_inc(dve_setup, 1)
                    nc.vector.tensor_tensor(u_hr[:, :, :], vu_rep[:, 1, :].unsqueeze(1).to_broadcast([P, H, R]), mask_r, ALU.mult).then_inc(dve_setup, 1)
                    dve.wait_ge(b_loaded, 48)
                    nc.vector.tensor_copy(bv_wide[:, :], bcols[:, 2:3].to_broadcast([P, P])).then_inc(dve_setup, 1)
                    dve.wait_ge(pe_setup, 2)
                    nc.vector.tensor_copy(wo_nt[:, :], st_ps[0][:, 0:P]).then_inc(dve_setup, 1)
                    for n in range(2):
                        for s in (q_stack[n], k_stack[n]):
                            nc.vector.memset(s[0:MAX_ROW, :, :].rearrange("p h t -> p (h t)").bitcast(fp32), 0.0).then_inc(dve_setup, 1)
                        nc.vector.memset(k_stack[n][MAX_ROW:STACK, :, :], 1.0).then_inc(dve_setup, 1)
                    nc.vector.memset(av_ps[:, :], 0.0).then_inc(dve_setup, 1)

                @block.scalar
                def _(act):
                    act.wait_ge(pe_setup, 3)
                    for n, w in enumerate((wq_t, wk_t, wv_t)):
                        nc.scalar.activation(w[:, :], sm_ps[0][:, 0, n * P:(n + 1) * P], ACT.Copy)
                    act.wait_ge(pe_setup, 4)
                    nc.scalar.activation(bq_c[:, :], sm_ps[1][:, 0, 0:1], ACT.Copy, scale=SCALE)
                    nc.scalar.activation(bk_c[:, :], sm_ps[1][:, 0, 1:2], ACT.Copy)
                    nc.scalar.activation(bv_b[:, :], sm_ps[1][:, 0, P:2 * P], ACT.Copy)
                    act.wait_ge(pe_setup, 5)
                    nc.scalar.activation(wo_t[:, :], sm_ps[1][:, 1, 0:P], ACT.Copy)

            names = ("xt_done q_done k_done v_done maxt_done yt_done ynt_done wo_done st_done sm_done av_done "
                     "xt_sb q_sb k_sb ynt_sb y_ready exp_done "
                     "red_done negmax_sb yn_inv yn_sb v_sb res_ready stats_ready mv_ready x1_ready "
                     "qpart_ready kpart_ready maxpart_ready vareps_ready split_done maxsplit_done xbo_ready rstd_ready "
                     "parts_stored x1_stored")
            S = {n: sem(n) for n in names.split()}
            x_loaded = [sem(f"x_loaded{n}") for n in range(2)]
            xres_loaded = [sem(f"xres_loaded{n}") for n in range(2)]
            stack_loaded = [sem(f"stack_loaded{n}") for n in range(HG)]
            maxrow_loaded = [sem(f"maxrow_loaded{n}") for n in range(2)]
            LOADS = (SLOTS + len(Q_RUNS)) * 16

            def schedule(engine, body):
                def flags(n):
                    return 0 <= n < B, 0 <= n + 1 < B, n + 2 < B, 0 <= n - 1 < B
                for n in range(-2, 2):
                    body(Batch(0, n), *flags(n))
                with engine.Fori(1, B // 2 - 1) as i:
                    for c in range(2):
                        body(Batch(i, c), *flags(2 + c))
                for n in range(B - 2, B + 1):
                    body(Batch(0, n), *flags(n))

            with nc.Block() as block:
                @block.tensor
                def _(pe):
                    def body(b, cur, nxt, proj, prev):
                        n1, n2, p1 = b + 1, b + 2, b + -1

                        def misc(s):
                            if s == 2 and cur:
                                wait(pe, S["red_done"], b.count(32, 32))
                                wait(pe, S["negmax_sb"], b.count(2, 1))
                                wait(pe, S["yn_sb"], p1.count(HG, 3))
                                nc.tensor.transpose(misc_ps[0:HALF, 0:P], row_max[:, HALF:UNITS], ident[:, :]).then_inc(S["maxt_done"], 1)
                            if s == 5 and proj:
                                pe.wait_ge(x_loaded[n2.parity], n2.count_parity(16, 16))
                                wait(pe, S["negmax_sb"], b.count(2, 2) if cur else 0)
                                wait(pe, S["k_sb"], n1.count(1, 1))
                                for t in range(QT):
                                    last = nc.tensor.transpose(misc_ps[:, t * P:(t + 1) * P], x_in[n2.parity][:, t, :], ident[:, :])
                                last.then_inc(S["xt_done"], 1)
                            if s == 8 and proj:
                                pe.wait_ge(S["xt_sb"], n2.count(1, 1))
                                nc.tensor.matmul(misc_ps[:, :], wq_t[:, :], x_t[n2.parity][:, :], start=True, stop=True).then_inc(S["q_done"], 1)
                            if s == 11 and proj:
                                pe.wait_ge(S["q_sb"], n2.count(1, 1))
                                nc.tensor.matmul(misc_ps[:, :], wk_t[:, :], x_t[n2.parity][:, :], start=True, stop=True).then_inc(S["k_done"], 1)
                            if s == 14 and prev:
                                wait(pe, S["k_sb"], n2.count(1, 1) if proj else 0)
                                wait(pe, S["negmax_sb"], b.count(2, 2) if cur else 0)
                                wait(pe, S["yn_sb"], p1.count(HG, 3))
                                y_transpose(p1, 3)
                            if s == 17 and prev:
                                pe.wait_ge(S["yn_sb"], p1.count(HG, 4))
                                for t in range(QT):
                                    last = nc.tensor.transpose(misc_ps[:, t * P:(t + 1) * P], y_norm[:, t, :, :].rearrange("p h r -> p (h r)"), ident[:, :])
                                last.then_inc(S["ynt_done"], 1)
                            if s == 20 and prev:
                                pe.wait_ge(S["ynt_sb"], p1.count(1, 1))
                                for t in range(QT):
                                    last = nc.tensor.matmul(misc_ps[:, t * P:(t + 1) * P], y_t[:, t * P:(t + 1) * P], wo_t[:, :], start=True, stop=True)
                                last.then_inc(S["wo_done"], 1)
                            if s == 26 and cur:
                                wait(pe, S["res_ready"], p1.count(1, 1) if prev else 0)
                                wait(pe, S["k_sb"], n2.count(1, 1) if proj else 0)
                                y_transpose(b, 0)
                            if s == 30 and nxt:
                                wait(pe, S["yn_sb"], b.count(HG, 1) if cur else 0)
                                wait(pe, S["k_sb"], n2.count(1, 1) if proj else 0)
                                wait(pe, S["xt_sb"], n1.count(1, 1))
                                for t in range(QT):
                                    last = nc.tensor.matmul(misc_ps[:, t * P:(t + 1) * P], x_t[n1.parity][:, t * P:(t + 1) * P], wv_t[:, :], start=True, stop=True)
                                last.then_inc(S["v_done"], 1)
                            if s == 36 and nxt:
                                pe.wait_ge(S["red_done"], n1.count(32, 16))
                                pe.wait_ge(S["v_sb"], n1.count(1, 1))
                                nc.tensor.transpose(misc_ps[0:HALF, 0:P], row_max[:, 0:HALF], ident[:, :]).then_inc(S["maxt_done"], 1)
                            if s == 42 and cur:
                                wait(pe, S["negmax_sb"], n1.count(2, 1) if nxt else 0)
                                wait(pe, S["yn_sb"], b.count(HG, 1))
                                y_transpose(b, 1)
                            if s == 58 and cur:
                                pe.wait_ge(S["yn_sb"], b.count(HG, 2))
                                y_transpose(b, 2)

                        def y_transpose(n, hg):
                            pe.wait_ge(S["y_ready"], n.count(HG, hg + 1))
                            for t in range(QT):
                                last = nc.tensor.transpose(misc_ps[:, t * P:(t + 1) * P], y_sb[hg % 2][:, t * P:(t + 1) * P], ident[:, :])
                            last.then_inc(S["yt_done"], 1)

                        def av(n, j):
                            hg, kb = divmod(j, QT)
                            if j == 0:
                                wait(pe, S["v_sb"], n.count(1, 1))
                            if kb == 0:
                                wait(pe, S["y_ready"], n.count(HG, hg))
                            pe.wait_ge(S["exp_done"], n.count(UNITS, 4 * j + 4))
                            for g in range(HG):
                                last = nc.tensor.matmul(av_ps[32 * g:32 * g + V_COLS, :], v_one[n.parity][:, kb, HG * hg + g, :],
                                                        probs[:, (4 * j + g) % P_RING, :], start=(kb == 0), stop=(kb == QT - 1),
                                                        tile_position=(0, 32 * g))
                            last.then_inc(S["av_done"], 1)

                        for s in range(UNITS):
                            misc(s)
                            hg, k, g = s // GROUP, (s % GROUP) // HG, s % HG
                            if cur:
                                h = HG * hg + g
                                wait(pe, S["exp_done"], b.count(UNITS, s - 1))
                                if s % HALF == 0:
                                    pe.wait_ge(maxrow_loaded[s // HALF], b.count(48, 48))
                                nc.tensor.matmul(st_ps[s % 2][:, :], k_stack[b.parity][0:STACK, h, k * P:(k + 1) * P],
                                                 q_stack[b.parity][0:STACK, h, :], start=True, stop=True).then_inc(S["st_done"], 1)
                            if nxt:
                                h = HG * hg + k
                                if s % GROUP == 0:
                                    pe.wait_ge(stack_loaded[hg], n1.count(LOADS, LOADS))
                                if s % 2 == 0:
                                    wait(pe, S["red_done"], n1.count(32, s // 2 - 1))
                                last = nc.tensor.matmul(sm_ps[(s // 2) % 2][:, s % 2, :], q_stack[n1.parity][0:MAX_ROW, h, g * P:(g + 1) * P],
                                                        k_stack[n1.parity][0:MAX_ROW, h, :], start=True, stop=True)
                                if s % 2 == 1:
                                    last.then_inc(S["sm_done"], 1)
                            j, off = divmod(s - AV_LAG, 4)
                            if off == 0:
                                if j >= 0 and cur:
                                    av(b, j)
                                if j < 0 and prev:
                                    av(p1, j + 16)

                    schedule(pe, body)

                @block.scalar
                def _(act):
                    def body(b, cur, nxt, proj, prev):
                        n1, n2, p1 = b + 1, b + 2, b + -1

                        def y_out(n, hg):
                            act.wait_ge(S["av_done"], n.count(16, 4 * hg + 4))
                            wait(act, S["yt_done"], n.count(HG, hg - 1))
                            nc.scalar.activation(y_sb[hg % 2][:, :], av_ps[:, :], ACT.Copy).then_inc(S["y_ready"], 1)

                        for s in range(UNITS):
                            if s == 3 and prev:
                                y_out(p1, 3)
                            if s == 6 and proj:
                                act.wait_ge(S["xt_done"], n2.count(1, 1))
                                wait(act, S["v_done"], b.count(1, 1))
                                nc.scalar.activation(x_t[n2.parity][:, :], misc_ps[:, :], ACT.Copy).then_inc(S["xt_sb"], 1)
                            if s == 9 and proj:
                                act.wait_ge(S["q_done"], n2.count(1, 1))
                                wait(act, S["split_done"], n1.count(2, 1))
                                nc.scalar.activation(q_f[:, :], misc_ps[:, :], ACT.Identity, bias=bq_c[:, :], scale=SCALE).then_inc(S["q_sb"], 1)
                            if s == 12 and proj:
                                act.wait_ge(S["k_done"], n2.count(1, 1))
                                wait(act, S["split_done"], n1.count(2, 2))
                                nc.scalar.activation(k_f[:, :], misc_ps[:, :], ACT.Identity, bias=bk_c[:, :]).then_inc(S["k_sb"], 1)
                            if s == 18 and prev:
                                act.wait_ge(S["ynt_done"], p1.count(1, 1))
                                wait(act, S["wo_done"], p1.count(1, 0))
                                nc.scalar.activation(y_t[:, :], misc_ps[:, :], ACT.Copy).then_inc(S["ynt_sb"], 1)
                            if s >= GROUP and s % GROUP == 3 and cur:
                                y_out(b, s // GROUP - 1)
                            if cur:
                                act.wait_ge(S["st_done"], b.count(UNITS, s + 1))
                                if s % 4 == 0:
                                    wait(act, S["av_done"], b.count(16, s // 4 - P_RING // 4 + 1))
                                nc.scalar.activation(probs[:, s % P_RING, :], st_ps[s % 2][:, :], ACT.Exp).then_inc(S["exp_done"], 1)

                    schedule(act, body)

                @block.vector
                def _(dve):
                    def body(b, cur, nxt, proj, prev):
                        n1, n2, p1 = b + 1, b + 2, b + -1

                        def neg(n, half):
                            dve.wait_ge(S["maxt_done"], n.count(2, half + 1))
                            wait(dve, S["maxsplit_done"], n.count(2, half - 1))
                            nc.vector.tensor_scalar(neg_max[half][:, :], misc_ps[0:HALF, 0:P], -1.0, None, ALU.mult).then_inc(S["negmax_sb"], 1)

                        def y_normalise(n, hg):
                            dve.wait_ge(S["yt_done"], n.count(HG, hg + 1))
                            ps = misc_ps[:, :].rearrange("p (t g c) -> p t g c", t=QT, g=HG)
                            nc.vector.reciprocal(inv_sum[:, hg, :, :], ps[:, :, :, R]).then_inc(S["yn_inv"], 1)
                            dve.wait_ge(S["yn_inv"], n.count(HG, hg + 1))
                            wait(dve, S["ynt_done"], n.count(1, 0))
                            nc.vector.tensor_tensor(y_norm[:, :, HG * hg:HG * hg + HG, :], ps[:, :, :, 0:R],
                                                    inv_sum[:, hg, :, :].unsqueeze(3).to_broadcast([P, QT, HG, R]), ALU.mult).then_inc(S["yn_sb"], 1)

                        def layernorm(n):
                            dve.wait_ge(S["wo_done"], n.count(1, 1))
                            dve.wait_ge(S["xbo_ready"], n.count(1, 1))
                            nc.vector.tensor_tensor(res[:, :, :].rearrange("p t d -> p (t d)"), misc_ps[:, :],
                                                    x_bo[:, :, :].rearrange("p t d -> p (t d)"), ALU.add).then_inc(S["res_ready"], 1)
                            dve.wait_ge(S["res_ready"], n.count(1, 1))
                            for t in range(QT):
                                nc.vector.bn_stats(stats[:, t, :], res[:, t, :]).then_inc(S["stats_ready"], 1)

                        def moments(n):
                            for t in range(QT):
                                nc.vector.bn_aggr(mean_var[:, t, :], stats[:, t, :]).then_inc(S["mv_ready"], 1)

                        def scale_out(n):
                            dve.wait_ge(S["rstd_ready"], n.count(1, 1))
                            wait(dve, S["x1_stored"], n.count(16, 0))
                            for t in range(QT):
                                nc.vector.tensor_scalar(x1_sb[:, t, :], res[:, t, :], mean_var[:, t, 0:1], rstd[:, t:t + 1],
                                                        ALU.subtract, ALU.mult).then_inc(S["x1_ready"], 1)

                        for s in range(UNITS):
                            if s == 3 and cur:
                                neg(b, 1)
                            if s == 15 and prev:
                                y_normalise(p1, 3)
                            if s == 21 and prev:
                                layernorm(p1)
                            if s == 27 and cur:
                                y_normalise(b, 0)
                            if s == 31 and nxt:
                                dve.wait_ge(S["v_done"], n1.count(1, 1))
                                wait(dve, S["av_done"], b.count(16, 0))
                                nc.vector.tensor_tensor(v_one[n1.parity][:, :, :, 0:R], misc_ps[:, :].rearrange("p (t h r) -> p t h r", t=QT, h=H),
                                                        bv_b[:, :].rearrange("p (h r) -> p h r", h=H).unsqueeze(1).to_broadcast([P, QT, H, R]),
                                                        ALU.add).then_inc(S["v_sb"], 1)
                            if s == 33 and prev:
                                scale_out(p1)
                            if s == 37 and nxt:
                                neg(n1, 0)
                            if s == 43 and cur:
                                y_normalise(b, 1)
                            if s == 59 and cur:
                                y_normalise(b, 2)
                            if s == 23 and prev:
                                dve.wait_ge(S["stats_ready"], p1.count(QT, QT))
                            if nxt and s % 2 == 1:
                                dve.wait_ge(S["sm_done"], n1.count(32, s // 2 + 1))
                                if s % HALF == 1:
                                    wait(dve, S["maxt_done"], b.count(2, s // HALF + 1))
                                nc.vector.tensor_reduce(row_max[:, s - 1:s + 1], sm_ps[(s // 2) % 2][:, :, :], AX.X, ALU.max).then_inc(S["red_done"], 1)
                            if s == 23 and prev:
                                moments(p1)

                    schedule(dve, body)

                @block.gpsimd
                def _(pool):
                    def body(b, cur, nxt, proj, prev):
                        n1, n2, p1 = b + 1, b + 2, b + -1

                        def split(full, parts, rest_t, zeros, part_ready, value, last_sem):
                            nc.gpsimd.tensor_tensor(parts[:, 0, :], full, zeros, ALU.add).then_inc(part_ready, 1)
                            pool.wait_ge(part_ready, value(1))
                            nc.gpsimd.tensor_tensor(rest_t, full, parts[:, 0, :], ALU.subtract).then_inc(part_ready, 1)
                            pool.wait_ge(part_ready, value(2))
                            nc.gpsimd.tensor_tensor(parts[:, 1, :], rest_t, zeros, ALU.add).then_inc(part_ready, 1)
                            pool.wait_ge(part_ready, value(3))
                            nc.gpsimd.tensor_tensor(parts[:, 2, :], rest_t, parts[:, 1, :], ALU.subtract).then_inc(last_sem, 1)

                        def split_max(n, half):
                            pool.wait_ge(S["negmax_sb"], n.count(2, half + 1))
                            wait(pool, maxrow_loaded[half], n.count(48, 0))
                            wait(pool, S["maxsplit_done"], n.count(2, half))
                            split(neg_max[half][:, :], max_parts[half], max_rest[:, :], zeros[0:HALF, 0:P], S["maxpart_ready"],
                                  lambda k: n.count(6, 3 * half + k), S["maxsplit_done"])

                        if cur:
                            split_max(b, 1)
                        if prev:
                            pool.wait_ge(xres_loaded[p1.parity], p1.count_parity(16, 16))
                            wait(pool, S["res_ready"], p1.count(1, 0))
                            nc.gpsimd.tensor_tensor(x_bo[:, :, :], x_res[p1.parity][:, :, :], bo_b[:, :].unsqueeze(1).to_broadcast([P, QT, D]),
                                                    ALU.add).then_inc(S["xbo_ready"], 1)
                        if proj:
                            pool.wait_ge(S["q_sb"], n2.count(1, 1))
                            wait(pool, S["parts_stored"], n2.count(32, 0))
                            wait(pool, S["split_done"], n2.count(2, 0))
                            split(q_f[:, :], q_parts, rest[:, :], zeros[:, :], S["qpart_ready"], lambda k: n2.count(3, k), S["split_done"])
                        if prev:
                            pool.wait_ge(S["mv_ready"], p1.count(QT, QT))
                            nc.gpsimd.tensor_tensor(var_eps[:, :], mean_var[:, :, 1], eps_t[:, :], ALU.add).then_inc(S["vareps_ready"], 1)
                            pool.wait_ge(S["vareps_ready"], p1.count(1, 1))
                            wait(pool, S["x1_ready"], p1.count(QT, 0))
                            nc.gpsimd.tensor_tensor(rstd[:, :], var_eps[:, :], neg_half[:, :], ALU.pow).then_inc(S["rstd_ready"], 1)
                        if proj:
                            pool.wait_ge(S["k_sb"], n2.count(1, 1))
                            pool.wait_ge(S["split_done"], n2.count(2, 1))
                            split(k_f[:, :], k_parts, rest[:, :], zeros[:, :], S["kpart_ready"], lambda k: n2.count(3, k), S["split_done"])
                        if nxt:
                            split_max(n1, 0)

                    schedule(pool, body)

                @block.sync
                def _(sp):
                    def body(b, cur, nxt, proj, prev):
                        n1, n2, p1 = b + 1, b + 2, b + -1

                        rows = {n: sp.snap(n.row()) if not isinstance(n.i, int) else n.row() for n in (n2, b, p1)}

                        def tokens(dram, n):
                            return dram[bass.ds(rows[n], T), :].rearrange("(t p) d -> p t d", p=P)

                        def max_rows(n, half):
                            sp.wait_ge(S["maxsplit_done"], n.count(2, half + 1))
                            for part in range(3):
                                sp.dma_start(q_stack[n.parity][MAX_ROW + part:MAX_ROW + part + 1, half * H // 2:(half + 1) * H // 2, :].rearrange("a h (t p) -> a (h t) p", p=P),
                                             max_parts[half][:, part, :]).then_inc(maxrow_loaded[half], 16)

                        def stacks(n, hg):
                            heads = slice(HG * hg, HG * hg + HG)
                            for slot, part in enumerate(K_PARTS):
                                sp.dma_start(k_stack[n.parity][slot * R:(slot + 1) * R, heads, :],
                                             k_parts_d[n.parity][part * R:(part + 1) * R, heads, :]).then_inc(stack_loaded[hg], 16)
                            for slot, part, count in Q_RUNS:
                                sp.dma_start(q_stack[n.parity][slot * R:(slot + count) * R, heads, :],
                                             q_parts_d[n.parity][part * R:(part + count) * R, heads, :]).then_inc(stack_loaded[hg], 16)

                        if proj:
                            wait(sp, S["xt_done"], b.count(1, 1))
                            sp.dma_start(x_in[n2.parity][:, :, :], tokens(x_rows, n2)).then_inc(x_loaded[n2.parity], 16)
                        if nxt:
                            wait(sp, S["sm_done"], b.count(32, 32))
                            stacks(n1, HG - 1)
                        if cur:
                            wait(sp, S["xbo_ready"], p1.count(1, 0))
                            sp.dma_start(x_res[b.parity][:, :, :], tokens(x_rows, b)).then_inc(xres_loaded[b.parity], 16)
                            max_rows(b, 1)
                        if proj:
                            for parts_d, parts, done in ((q_parts_d, q_parts, 1), (k_parts_d, k_parts, 2)):
                                sp.wait_ge(S["split_done"], n2.count(2, done))
                                sp.dma_start(parts_d[n2.parity].rearrange("(s r) h t -> s (r h) t", r=R).rearrange("s p t -> p s t"),
                                             parts[:, :, :]).then_inc(S["parts_stored"], 16)
                        if prev:
                            sp.wait_ge(S["x1_ready"], p1.count(QT, QT))
                            sp.dma_start(tokens(x1_d, p1), x1_sb[:, :, :]).then_inc(S["x1_stored"], 16)
                        if nxt:
                            max_rows(n1, 0)
                        if proj:
                            sp.wait_ge(S["parts_stored"], n2.count(32, 32))
                            stacks(n2, 0)
                            stacks(n2, 1)
                            wait(sp, S["sm_done"], n1.count(32, 24))
                            stacks(n2, 2)


                    schedule(sp, body)
                    sp.wait_ge(S["x1_stored"], 16 * B)

        moe = ExitStack()
        with moe:
            def msb(name, shape, dt=fp32):
                return moe.enter_context(nc.sbuf_tensor(name, shape, dt))

            w1_n = msb("w1_n", [P, E * HB, D])
            w2_n = msb("w2_n", [P, E, HID])
            w1_t = msb("w1_t", [P, E, HID])
            w2_t = msb("w2_t", [P, E, HB, D])
            gate_n = msb("gate_n", [E, D])
            gate_t = msb("gate_t", [P, E])
            b1_n = msb("b1_n", [E * HB, P])
            b1_c = msb("b1_c", [P, E * HB])
            b2_b = msb("b2_b", [P, E, D])
            earlier = msb("earlier", [P, E, E])
            x1 = msb("x1", [P, QT, D])
            x1_t = msb("x1_t", [P, T])
            logits = msb("logits", [P, QT, E])
            top_l = msb("top_l", [P, QT])
            ex = msb("ex", [P, QT, E])
            pr = msb("pr", [P, QT, E])
            s4 = msb("s4", [P, QT])
            i4 = msb("i4", [P, QT])
            gt = msb("gt", [P, E, E])
            eq = msb("eq", [P, E, E])
            rank = msb("rank", [P, QT, E])
            comb = msb("comb", [P, QT, E])
            h_sb = msb("h_sb", [P, 2, HB, T])
            tmp = msb("tmp", [P, QT, D])
            acc = msb("acc", [P, QT, D])
            st2 = msb("st2", [P, QT, 6])
            mv2 = msb("mv2", [P, QT, 2])
            ve2 = msb("ve2", [P, QT])
            rs2 = msb("rs2", [P, QT])
            y2 = msb("y2", [P, QT, D])
            hp = [moe.enter_context(nc.psum_tensor(f"hp{n}", [P, T], fp32)) for n in range(4)]
            op = [moe.enter_context(nc.psum_tensor(f"op{n}", [P, QT, D], fp32)) for n in range(2)]
            mp = [moe.enter_context(nc.psum_tensor(f"mp{n}", [P, T], fp32)) for n in range(2)]

            w_in, pe_w, ev_w, ev_a, c_w = sem("w_in"), sem("pe_w"), sem("ev_w"), sem("ev_a"), sem("c_w")
            with nc.Block() as block:
                @block.sync
                def _(sp):
                    sp.dma_start(w1_n[:, :, :], w1.rearrange("e (h p) d -> p (e h) d", p=P)).then_inc(w_in, 16)
                    sp.dma_start(w2_n[:, :, :], w2.rearrange("e d h -> d e h")).then_inc(w_in, 16)
                    sp.dma_start(gate_n[:, :], gate_w).then_inc(w_in, 16)
                    sp.dma_start(b1_n[:, :], b1.rearrange("e (h p) -> (e h) p", p=P)).then_inc(w_in, 16)
                    sp.dma_start(b2_b[:, :, :].rearrange("p e d -> p (e d)"), b2.rearrange("(a e) d -> a (e d)", a=1).to_broadcast([P, E * D])).then_inc(w_in, 16)
                    sp.wait_ge(w_in, 80)

                @block.gpsimd
                def _(pool):
                    nc.gpsimd.memset(earlier[:, :, :], 1.0).then_inc(c_w, 1)
                    pool.wait_ge(c_w, 1)
                    nc.gpsimd.affine_select(out=earlier[:, :, :], in_=earlier[:, :, :], compare_op=ALU.is_gt, fill=0.0,
                                            base=0, pattern=[[1, E], [-1, E]], channel_multiplier=0).then_inc(c_w, 1)

                @block.tensor
                def _(pe):
                    pe.wait_ge(w_in, 80)
                    for e in range(E):
                        if e >= 2:
                            pe.wait_ge(ev_w, e - 1)
                            pe.wait_ge(ev_a, e - 1)
                        for h in range(HB):
                            nc.tensor.transpose(hp[e % 2][:, h * P:(h + 1) * P], w1_n[:, e * HB + h, :], ident[:, :])
                            last = nc.tensor.transpose(hp[2 + e % 2][:, h * P:(h + 1) * P], w2_n[:, e, h * P:(h + 1) * P], ident[:, :])
                        last.then_inc(pe_w, 1)
                    nc.tensor.transpose(mp[0][:, 0:E], gate_n[:, :], ident[0:E, 0:E])
                    nc.tensor.transpose(mp[1][:, 0:E * HB], b1_n[:, :], ident[0:E * HB, 0:E * HB]).then_inc(pe_w, 1)

                @block.vector
                def _(dve):
                    for e in range(E):
                        dve.wait_ge(pe_w, e + 1)
                        nc.vector.tensor_copy(w1_t[:, e, :], hp[e % 2][:, :]).then_inc(ev_w, 1)
                    dve.wait_ge(pe_w, E + 1)
                    nc.vector.tensor_copy(gate_t[:, :], mp[0][:, 0:E]).then_inc(ev_w, 1)

                @block.scalar
                def _(act):
                    for e in range(E):
                        act.wait_ge(pe_w, e + 1)
                        nc.scalar.activation(w2_t[:, e, :, :].rearrange("p h d -> p (h d)"), hp[2 + e % 2][:, :], ACT.Copy).then_inc(ev_a, 1)
                    act.wait_ge(pe_w, E + 1)
                    nc.scalar.activation(b1_c[:, :], mp[1][:, 0:E * HB], ACT.Copy).then_inc(ev_a, 1)

            M = {n: sem("m_" + n) for n in "x1 x1t_ps x1t lg_ps lg exps rout hps h ops comb1 acc xv dv rs y outd".split()}
            with nc.Block() as block:
                @block.sync
                def _(sp):
                    with sp.Fori(0, B) as i:
                        row = sp.snap(i * T)
                        sp.dma_start(x1[:, :, :], x1_d[bass.ds(row, T), :].rearrange("(t p) d -> p t d", p=P)).then_inc(M["x1"], 16)
                        sp.wait_ge(M["y"], i * QT + QT)
                        sp.dma_start(out_rows[bass.ds(row, T), :].rearrange("(t p) d -> p t d", p=P), y2[:, :, :]).then_inc(M["outd"], 16)
                    sp.wait_ge(M["outd"], 16 * B)

                @block.tensor
                def _(pe):
                    with pe.Fori(0, B) as i:
                        pe.wait_ge(M["x1"], i * 16 + 16)
                        for t in range(QT):
                            last = nc.tensor.transpose(mp[0][:, t * P:(t + 1) * P], x1[:, t, :], ident[:, :])
                        last.then_inc(M["x1t_ps"], 1)
                        pe.wait_ge(M["x1t"], i + 1)
                        for t in range(QT):
                            last = nc.tensor.matmul(mp[1][:, t * E:(t + 1) * E], x1_t[:, t * P:(t + 1) * P], gate_t[:, :], start=True, stop=True)
                        last.then_inc(M["lg_ps"], 1)
                        for e in range(E + 1):
                            if e < E:
                                for h in range(HB):
                                    pe.wait_ge(M["h"], i * E * HB + (e * HB + h - 3)) if e * HB + h - 3 > 0 else None
                                    nc.tensor.matmul(hp[h][:, :], w1_t[:, e, h * P:(h + 1) * P], x1_t[:, :], start=True, stop=True).then_inc(M["hps"], 1)
                            if e >= 1:
                                f = e - 1
                                pe.wait_ge(M["h"], i * E * HB + (f + 1) * HB)
                                if f >= 2:
                                    pe.wait_ge(M["comb1"], i * E + (f - 1))
                                for t in range(QT):
                                    for h in range(HB):
                                        last = nc.tensor.matmul(op[f % 2][:, t, :], h_sb[:, f % 2, h, t * P:(t + 1) * P], w2_t[:, f, h, :], start=(h == 0), stop=(h == HB - 1))
                                last.then_inc(M["ops"], 1)
                        pe.wait_ge(M["y"], i * QT + QT)

                @block.scalar
                def _(act):
                    with act.Fori(0, B) as i:
                        act.wait_ge(M["x1t_ps"], i + 1)
                        nc.scalar.activation(x1_t[:, :], mp[0][:, :], ACT.Copy).then_inc(M["x1t"], 1)
                        act.wait_ge(M["lg"], i + 1)
                        nc.scalar.activation(ex[:, :, :], logits[:, :, :], ACT.Exp).then_inc(M["exps"], 1)
                        for e in range(E):
                            for h in range(HB):
                                act.wait_ge(M["hps"], i * E * HB + (e * HB + h + 1))
                                if e >= 2 and h == 0:
                                    act.wait_ge(M["ops"], i * E + (e - 1))
                                nc.scalar.activation(h_sb[:, e % 2, h, :], hp[h][:, :], ACT.Relu, bias=b1_c[:, e * HB + h:e * HB + h + 1]).then_inc(M["h"], 1)

                @block.gpsimd
                def _(pool):
                    with pool.Fori(0, B) as i:
                        pool.wait_ge(M["xv"], i * 2 * QT + 2 * QT)
                        nc.gpsimd.tensor_tensor(ve2[:, :], mv2[:, :, 1], eps_t[:, :], ALU.add).then_inc(M["rs"], 1)
                        pool.wait_ge(M["rs"], i * 2 + 1)
                        nc.gpsimd.tensor_tensor(rs2[:, :], ve2[:, :], neg_half[:, :], ALU.pow).then_inc(M["rs"], 1)

                @block.vector
                def _(dve):
                    STEPS = 1 + 3 + 5 * QT + 6 + E * QT + 1
                    with dve.Fori(0, B) as i:
                        k = [0]

                        def link(instruction):
                            k[0] += 1
                            instruction.then_inc(M["dv"], 1)
                            dve.wait_ge(M["dv"], i * STEPS + k[0])

                        dve.wait_ge(M["lg_ps"], i + 1)
                        lg = mp[1][:, 0:QT * E].rearrange("p (t e) -> p t e", e=E)
                        link(nc.vector.tensor_reduce(top_l[:, :], lg, AX.X, ALU.max))
                        nc.vector.tensor_tensor(logits[:, :, :], lg, top_l[:, :].unsqueeze(2).to_broadcast([P, QT, E]), ALU.subtract).then_inc(M["lg"], 1)
                        dve.wait_ge(M["exps"], i + 1)
                        link(nc.vector.tensor_reduce(s4[:, :], ex[:, :, :], AX.X, ALU.add))
                        link(nc.vector.reciprocal(i4[:, :], s4[:, :]))
                        link(nc.vector.tensor_tensor(pr[:, :, :], ex[:, :, :], i4[:, :].unsqueeze(2).to_broadcast([P, QT, E]), ALU.mult))
                        for t in range(QT):
                            pf = pr[:, t, :].unsqueeze(1).to_broadcast([P, E, E])
                            pe_ = pr[:, t, :].unsqueeze(2).to_broadcast([P, E, E])
                            link(nc.vector.tensor_tensor(gt[:, :, :], pf, pe_, ALU.is_gt))
                            link(nc.vector.tensor_tensor(eq[:, :, :], pf, pe_, ALU.is_equal))
                            link(nc.vector.tensor_tensor(eq[:, :, :], eq[:, :, :], earlier[:, :, :], ALU.mult))
                            link(nc.vector.tensor_tensor(gt[:, :, :], gt[:, :, :], eq[:, :, :], ALU.add))
                            link(nc.vector.tensor_reduce(rank[:, t, :], gt[:, :, :], AX.X, ALU.add))
                        link(nc.vector.tensor_scalar(rank[:, :, :], rank[:, :, :], 1.5, None, ALU.is_lt))
                        link(nc.vector.tensor_tensor(comb[:, :, :], rank[:, :, :], pr[:, :, :], ALU.mult))
                        link(nc.vector.tensor_reduce(s4[:, :], comb[:, :, :], AX.X, ALU.add))
                        link(nc.vector.reciprocal(i4[:, :], s4[:, :]))
                        link(nc.vector.tensor_tensor(comb[:, :, :], comb[:, :, :], i4[:, :].unsqueeze(2).to_broadcast([P, QT, E]), ALU.mult))
                        link(nc.vector.tensor_copy(acc[:, :, :], x1[:, :, :]))
                        for e in range(E):
                            dve.wait_ge(M["ops"], i * E + (e + 1))
                            nc.vector.tensor_tensor(tmp[:, :, :], op[e % 2][:, :, :], b2_b[:, e, :].unsqueeze(1).to_broadcast([P, QT, D]), ALU.add).then_inc(M["comb1"], 1)
                            dve.wait_ge(M["comb1"], i * E + (e + 1))
                            for t in range(QT):
                                link(nc.vector.scalar_tensor_tensor(acc[:, t, :], tmp[:, t, :], comb[:, t, e:e + 1], acc[:, t, :], ALU.mult, ALU.add))
                        for t in range(QT):
                            nc.vector.bn_stats(st2[:, t, :], acc[:, t, :]).then_inc(M["xv"], 1)
                        dve.wait_ge(M["xv"], i * 2 * QT + QT)
                        nc.vector.memset(s4[:, 0:1], 0.0).then_inc(M["dv"], 1)
                        for t in range(QT):
                            nc.vector.bn_aggr(mv2[:, t, :], st2[:, t, :]).then_inc(M["xv"], 1)
                        dve.wait_ge(M["rs"], i * 2 + 2)
                        for t in range(QT):
                            nc.vector.tensor_scalar(y2[:, t, :], acc[:, t, :], mv2[:, t, 0:1], rs2[:, t:t + 1], ALU.subtract, ALU.mult).then_inc(M["y"], 1)
                        dve.wait_ge(M["outd"], i * 16 + 16)



_INS = ["L0_attn_x", "L0_attn_Wq", "L0_attn_bq", "L0_attn_Wk", "L0_attn_bk", "L0_attn_Wv", "L0_attn_bv", "L0_attn_Wo",
        "L0_attn_bo", "L0_attn_U", "L0_attn_V", "L0_ffn_gate_w", "L0_ffn_w1", "L0_ffn_b1", "L0_ffn_w2", "L0_ffn_b2"]


def kernel(**inputs):
    import numpy as np
    import concourse.bacc as bacc
    from concourse.bass_utils import run_bass_kernel_spmd

    nc = bacc.Bacc("TRN2", target_bir_lowering=False, num_devices=1)
    arrays, args = {}, []
    for name in _INS:
        a = np.ascontiguousarray(inputs[name])
        arrays[name] = a
        args.append(nc.dram_tensor(name, a.shape, mybir.dt.from_np(a.dtype), kind="ExternalInput").ap())
    args.append(nc.dram_tensor("out", (B, T, D), mybir.dt.float32, kind="ExternalOutput").ap())
    build_layer(nc, *args)
    return run_bass_kernel_spmd(nc, [arrays], core_ids=[0]).results[0]["out"]
```

```python
import concourse.bass as bass
from concourse import mybir
from contextlib import ExitStack

B, T, D = 16, 512, 128
H, R = 16, 8
E, HID = 8, 512
P = 128
QT = T // P
HB = HID // P
EPS = 1e-5

HG = 4
UNITS = H * QT
GROUP = UNITS // HG
SLOTS = 6
PROD_ROWS = SLOTS * R
MAX_ROW = 96
STACK = MAX_ROW + 3
P_RING = 16
AV_LAG = 6
CAP = B * T + P
TILES = 2 * B * T // P + E
ROW = D + 2
TOP_STEPS = 19
V_COLS = R + 1
Q_RUNS = ((0, 0, 3), (3, 0, 2), (5, 0, 1))
K_PARTS = (0, 0, 0, 1, 1, 2)


class Batch:

    def __init__(self, i, c):
        self.i, self.c = i, c
        self.parity = c % 2

    def __add__(self, d):
        return Batch(self.i, self.c + d)

    def count(self, per_batch, events):
        return self.i * (2 * per_batch) + (self.c * per_batch + events)

    def count_parity(self, per_batch, events):
        return self.i * per_batch + ((self.c // 2) * per_batch + events)

    def row(self):
        return self.i * (2 * T) + self.c * T


def wait(engine, sem, value):
    if isinstance(value, int) and value <= 0:
        return
    engine.wait_ge(sem, value)


def build_layer(nc, x, wq, bq, wk, bk, wv, bv, wo, bo, u, v, gate_w, w1, b1, w2, b2, out):
    fp32, bf16 = mybir.dt.float32, mybir.dt.bfloat16
    ALU, ACT, AX = mybir.AluOpType, mybir.ActivationFunctionType, mybir.AxisListType
    SCALE = float(v.shape[1]) ** -0.5

    x_rows = x.rearrange("b t d -> (b t) d")
    out_rows = out.rearrange("b t d -> (b t) d")
    q_parts_d = [nc.dram_tensor(f"q_parts_d{n}", (3 * R, H, T), bf16, kind="Internal").ap() for n in range(2)]
    k_parts_d = [nc.dram_tensor(f"k_parts_d{n}", (3 * R, H, T), bf16, kind="Internal").ap() for n in range(2)]
    x1_d = nc.dram_tensor("x1_d", (B * T, D), fp32, kind="Internal").ap()
    routed_d = nc.dram_tensor("routed_d", (E * CAP + P, ROW), fp32, kind="Internal").ap()
    y_d = nc.dram_tensor("y_d", (2 * B * T, D), fp32, kind="Internal").ap()
    i32 = mybir.dt.int32

    top = ExitStack()

    def sem(name):
        return top.enter_context(nc.semaphore(name))

    with top:
        def sb(name, shape, dt=fp32):
            return top.enter_context(nc.sbuf_tensor(name, shape, dt))

        ident = sb("ident", [P, P])
        eps_t = sb("eps_t", [P, QT])
        neg_half = sb("neg_half", [P, QT])
        wq_t = sb("wq_t", [P, P])
        wk_t = sb("wk_t", [P, P])
        wv_t = sb("wv_t", [P, P])
        wo_t = sb("wo_t", [P, P])
        bq_c = sb("bq_c", [P, 1])
        bk_c = sb("bk_c", [P, 1])
        bv_b = sb("bv_b", [P, P])
        bo_b = sb("bo_b", [P, P])
        next_row = sb("next_row", [P, E])
        pad_rows = sb("pad_rows", [P, ROW])
        row_base = sb("row_base", [1, E])
        tile_no = sb("tile_no", [1, TILES])
        next_row_i = sb("next_row_i", [1, E], i32)
        tile_expert = sb("tile_expert", [1, TILES], i32)
        tile_row = sb("tile_row", [1, TILES], i32)

        att = ExitStack()
        with att:
            def asb(name, shape, dt=fp32):
                return att.enter_context(nc.sbuf_tensor(name, shape, dt))

            k_stack = [asb(f"k_stack{n}", [P, H, T], bf16) for n in range(2)]
            q_stack = [asb(f"q_stack{n}", [P, H, T], bf16) for n in range(2)]
            probs = asb("probs", [P, P_RING, T])
            v_one = [asb(f"v_one{n}", [P, QT, H, V_COLS]) for n in range(2)]
            x_in = [asb(f"x_in{n}", [P, QT, D]) for n in range(2)]
            x_res = [asb(f"x_res{n}", [P, QT, D]) for n in range(2)]
            x_bo = asb("x_bo", [P, QT, D])
            x_t = [asb(f"x_t{n}", [P, T]) for n in range(2)]
            q_f = asb("q_f", [P, T])
            k_f = asb("k_f", [P, T])
            rest = asb("rest", [P, T])
            zeros = asb("zeros", [P, T])
            q_parts = asb("q_parts", [P, 3, T], bf16)
            k_parts = asb("k_parts", [P, 3, T], bf16)
            row_max = asb("row_max", [P, UNITS])
            HALF = UNITS // 2
            neg_max = [asb(f"neg_max{n}", [HALF, P]) for n in range(2)]
            max_rest = asb("max_rest", [HALF, P])
            max_parts = [asb(f"max_parts{n}", [HALF, 3, P], bf16) for n in range(2)]
            y_sb = [asb(f"y_sb{n}", [P, T]) for n in range(2)]
            inv_sum = asb("inv_sum", [P, HG, QT, HG])
            y_norm = asb("y_norm", [P, QT, H, R])
            y_t = asb("y_t", [P, T])
            res = asb("res", [P, QT, D])
            stats = asb("stats", [P, QT, 6])
            mean_var = asb("mean_var", [P, QT, 2])
            var_eps = asb("var_eps", [P, QT])
            rstd = asb("rstd", [P, QT])
            rows = [[asb(f"rows{n}_{w}", [P, QT, ROW]) for w in range(2)] for n in range(2)]
            x1_t = asb("x1_t", [P, T])
            gate_t = asb("gate_t", [P, E])
            prefer = asb("prefer", [P, QT, E])
            before = asb("before", [P, P], bf16)
            ones = asb("ones", [P, P], bf16)
            top_logit = asb("top_logit", [P, QT])
            logits = asb("logits", [P, QT, E])
            exps = asb("exps", [P, QT, E])
            gate_sum = asb("gate_sum", [P, QT])
            gate_inv = asb("gate_inv", [P, QT])
            gate_p = asb("gate_p", [P, QT, E])
            best = [asb(f"best{w}", [P, QT]) for w in range(2)]
            tied = asb("tied", [P, QT, E])
            tied_w = asb("tied_w", [P, QT, E])
            first = asb("first", [P, QT])
            others = asb("others", [P, QT, E])
            chosen = [[asb(f"chosen{n}_{w}", [P, QT, E]) for w in range(2)] for n in range(2)]
            pair_sum = asb("pair_sum", [P, QT])
            pair_inv = asb("pair_inv", [P, QT])
            chosen_any = [asb(f"chosen_any{n}", [P, QT, E], bf16) for n in range(2)]
            slot = asb("slot", [P, QT, E])
            slot_of = asb("slot_of", [P, QT, E])
            slot_f = asb("slot_f", [P, 2, QT])
            slot_i = [asb(f"slot_i{n}", [P, 2, QT], i32) for n in range(2)]
            place_i = asb("place_i", [P, 2, QT], i32)
            place_f = asb("place_f", [P, 2, QT])
            gate_n = asb("gate_n", [E, P])
            tile_no_i = asb("tile_no_i", [1, TILES], i32)
            tiles_i = asb("tiles_i", [1, 2, E], i32)
            tiles_of = asb("tiles_of", [1, E])
            last_tile = asb("last_tile", [1, E])
            jump = asb("jump", [1, E])
            one_row = asb("one_row", [1, E])
            count_e = asb("count_e", [1, E])
            past = asb("past", [1, TILES, E])
            past_jump = asb("past_jump", [1, TILES, E])
            table_f = asb("table_f", [1, 3, TILES])
            w_nat = asb("w_nat", [P, 4, P])
            vu = asb("vu", [R, 2, R])
            bcols = asb("bcols", [P, 3])
            rep = asb("rep", [R, H, R])
            head_mask = asb("head_mask", [P, H])
            vu_rep = asb("vu_rep", [P, 2, R])
            v_rh = asb("v_rh", [P, R, H])
            v_hr = asb("v_hr", [P, H, R])
            u_hr = asb("u_hr", [P, H, R])
            wo_nt = asb("wo_nt", [P, P])
            bv_wide = asb("bv_wide", [P, P])

            st_ps = [att.enter_context(nc.psum_tensor(f"st_ps{n}", [P, T], fp32)) for n in range(2)]
            sm_ps = [att.enter_context(nc.psum_tensor(f"sm_ps{n}", [P, 2, T], fp32)) for n in range(2)]
            av_ps = att.enter_context(nc.psum_tensor("av_ps", [P, T], fp32))
            misc_ps = att.enter_context(nc.psum_tensor("misc_ps", [P, T], fp32))

            w_loaded, vu_loaded, b_loaded, bo_loaded = (sem(n) for n in ("w_loaded", "vu_loaded", "b_loaded", "bo_loaded"))
            const_ready, pool_setup = sem("const_ready"), sem("pool_setup")
            table_step, table_ready = sem("table_step"), sem("table_ready")
            gate_loaded, pads_ready, pads_stored = sem("gate_loaded"), sem("pads_ready"), sem("pads_stored")
            pe_setup, dve_setup, place_ready = sem("pe_setup"), sem("dve_setup"), sem("place_ready")
            with nc.Block() as block:
                @block.sync
                def _(sp):
                    for n, w in enumerate((wq, wk, wv, wo)):
                        sp.dma_start(w_nat[:, n, :], w).then_inc(w_loaded, 16)
                    for n, w in enumerate((v, u)):
                        sp.dma_start(vu[:, n, :], w).then_inc(vu_loaded, 16)
                    for n, w in enumerate((bq, bk, bv)):
                        sp.dma_start(bcols[:, n:n + 1], w.rearrange("(p a) -> p a", a=1)).then_inc(b_loaded, 16)
                    sp.dma_start(bo_b[:, :], bo.rearrange("(a n) -> a n", a=1).to_broadcast([P, D])).then_inc(bo_loaded, 16)
                    sp.dma_start(gate_n[:, :], gate_w).then_inc(gate_loaded, 16)
                    sp.wait_ge(bo_loaded, 16)
                    sp.wait_ge(pads_ready, 2)
                    sp.dma_start(routed_d[E * CAP:E * CAP + P, :], pad_rows[:, :]).then_inc(pads_stored, 16)
                    sp.wait_ge(pads_stored, 16)

                @block.gpsimd
                def _(pool):
                    nc.gpsimd.memset(ident[:, :], 0.0).then_inc(pool_setup, 1)
                    nc.gpsimd.memset(rep[:, :, :], 0.0).then_inc(pool_setup, 1)
                    nc.gpsimd.memset(head_mask[:, :], 1.0).then_inc(pool_setup, 1)
                    pool.wait_ge(pool_setup, 3)
                    nc.gpsimd.affine_select(out=ident[:, :], in_=ident[:, :], compare_op=ALU.not_equal, fill=1.0,
                                            base=0, pattern=[[-1, P]], channel_multiplier=1).then_inc(const_ready, 1)
                    nc.gpsimd.affine_select(out=rep[:, :, :], in_=rep[:, :, :], compare_op=ALU.not_equal, fill=1.0,
                                            base=0, pattern=[[0, H], [-1, R]], channel_multiplier=1).then_inc(const_ready, 1)
                    nc.gpsimd.affine_select(out=head_mask[:, :], in_=head_mask[:, :], compare_op=ALU.is_ge, fill=0.0,
                                            base=0, pattern=[[-R, H]], channel_multiplier=1).then_inc(pool_setup, 1)
                    pool.wait_ge(pool_setup, 4)
                    nc.gpsimd.affine_select(out=head_mask[:, :], in_=head_mask[:, :], compare_op=ALU.is_ge, fill=0.0,
                                            base=R - 1, pattern=[[R, H]], channel_multiplier=-1).then_inc(const_ready, 1)
                    nc.gpsimd.memset(eps_t[:, :], EPS).then_inc(const_ready, 1)
                    nc.gpsimd.memset(neg_half[:, :], -0.5).then_inc(const_ready, 1)
                    nc.gpsimd.memset(zeros[:, :], 0.0).then_inc(const_ready, 1)
                    for n in range(2):
                        nc.gpsimd.memset(v_one[n][:, :, :, R:R + 1], 1.0).then_inc(const_ready, 1)
                    nc.gpsimd.memset(pad_rows[:, 0:ROW - 1], 0.0).then_inc(pads_ready, 1)
                    nc.gpsimd.memset(pad_rows[:, ROW - 1:ROW].bitcast(i32), 2 * B * T).then_inc(pads_ready, 1)
                    for e in range(E):
                        nc.gpsimd.memset(prefer[:, :, e:e + 1], float(E - e)).then_inc(const_ready, 1)
                        nc.gpsimd.memset(next_row[:, e:e + 1], float(e * CAP)).then_inc(const_ready, 1)
                        nc.gpsimd.memset(row_base[:, e:e + 1], float(e * CAP)).then_inc(const_ready, 1)
                    nc.gpsimd.memset(ones[:, :], 1.0).then_inc(const_ready, 1)
                    nc.gpsimd.memset(before[:, :], 1.0).then_inc(pool_setup, 1)
                    pool.wait_ge(pool_setup, 5)
                    nc.gpsimd.affine_select(out=before[:, :], in_=before[:, :], compare_op=ALU.is_gt, fill=0.0,
                                            base=0, pattern=[[1, P]], channel_multiplier=-1).then_inc(const_ready, 1)
                    nc.gpsimd.iota(place_i[:, :, :], pattern=[[B * T, 2], [P, QT]], base=0, channel_multiplier=1).then_inc(place_ready, 1)
                    nc.gpsimd.iota(tile_no_i[:, :], pattern=[[1, TILES]], base=0, channel_multiplier=0).then_inc(place_ready, 1)

                @block.tensor
                def _(pe):
                    pe.wait_ge(const_ready, 3)
                    pe.wait_ge(vu_loaded, 32)
                    for n in range(2):
                        last = nc.tensor.matmul(misc_ps[:, n * R:(n + 1) * R], rep[:, :, :].rearrange("p h d -> p (h d)"),
                                                vu[:, n, :], start=True, stop=True)
                    last.then_inc(pe_setup, 1)
                    pe.wait_ge(w_loaded, 64)
                    pe.wait_ge(gate_loaded, 16)
                    nc.tensor.transpose(st_ps[1][:, 0:E], gate_n[:, :], ident[0:E, 0:E])
                    nc.tensor.transpose(st_ps[0][:, 0:P], w_nat[:, 3, :], ident[:, :]).then_inc(pe_setup, 1)
                    pe.wait_ge(dve_setup, 5)
                    pe.wait_ge(b_loaded, 48)
                    vrh = v_rh[:, :, :].rearrange("p r h -> p (r h)")
                    vhr = v_hr[:, :, :].rearrange("p h r -> p (h r)")
                    nc.tensor.matmul(sm_ps[0][:, 0, 0:P], w_nat[:, 0, :], vrh, start=True, stop=True)
                    nc.tensor.matmul(sm_ps[0][:, 0, P:2 * P], w_nat[:, 1, :], vrh, start=True, stop=True)
                    nc.tensor.matmul(sm_ps[0][:, 0, 2 * P:3 * P], w_nat[:, 2, :], vhr, start=True, stop=True).then_inc(pe_setup, 1)
                    nc.tensor.matmul(sm_ps[1][:, 0, 0:1], vrh, bcols[:, 0:1], start=True, stop=True)
                    nc.tensor.matmul(sm_ps[1][:, 0, 1:2], vrh, bcols[:, 1:2], start=True, stop=True)
                    nc.tensor.matmul(sm_ps[1][:, 0, P:2 * P], bv_wide[:, :], vhr, start=True, stop=True).then_inc(pe_setup, 1)
                    pe.wait_ge(dve_setup, 6)
                    nc.tensor.matmul(sm_ps[1][:, 1, 0:P], u_hr[:, :, :].rearrange("p h r -> p (h r)"), wo_nt[:, :],
                                     start=True, stop=True).then_inc(pe_setup, 1)

                @block.vector
                def _(dve):
                    dve.wait_ge(pe_setup, 1)
                    nc.vector.tensor_copy(vu_rep[:, :, :].rearrange("p a r -> p (a r)"), misc_ps[:, 0:2 * R]).then_inc(dve_setup, 1)
                    dve.wait_ge(dve_setup, 1)
                    dve.wait_ge(const_ready, 3)
                    mask_h = head_mask[:, :].unsqueeze(1).to_broadcast([P, R, H])
                    mask_r = head_mask[:, :].unsqueeze(2).to_broadcast([P, H, R])
                    nc.vector.tensor_tensor(v_rh[:, :, :], vu_rep[:, 0, :].unsqueeze(2).to_broadcast([P, R, H]), mask_h, ALU.mult).then_inc(dve_setup, 1)
                    nc.vector.tensor_tensor(v_hr[:, :, :], vu_rep[:, 0, :].unsqueeze(1).to_broadcast([P, H, R]), mask_r, ALU.mult).then_inc(dve_setup, 1)
                    nc.vector.tensor_tensor(u_hr[:, :, :], vu_rep[:, 1, :].unsqueeze(1).to_broadcast([P, H, R]), mask_r, ALU.mult).then_inc(dve_setup, 1)
                    dve.wait_ge(b_loaded, 48)
                    nc.vector.tensor_copy(bv_wide[:, :], bcols[:, 2:3].to_broadcast([P, P])).then_inc(dve_setup, 1)
                    dve.wait_ge(pe_setup, 2)
                    nc.vector.tensor_copy(wo_nt[:, :], st_ps[0][:, 0:P]).then_inc(dve_setup, 1)
                    nc.vector.tensor_copy(gate_t[:, :], st_ps[1][:, 0:E]).then_inc(dve_setup, 1)
                    dve.wait_ge(place_ready, 2)
                    nc.vector.tensor_copy(tile_no[:, :], tile_no_i[:, :]).then_inc(dve_setup, 1)
                    nc.vector.memset(one_row[:, :], 1.0).then_inc(dve_setup, 1)
                    nc.vector.tensor_copy(place_f[:, :, :], place_i[:, :, :]).then_inc(dve_setup, 1)
                    for n in range(2):
                        for s in (q_stack[n], k_stack[n]):
                            nc.vector.memset(s[0:MAX_ROW, :, :].rearrange("p h t -> p (h t)").bitcast(fp32), 0.0).then_inc(dve_setup, 1)
                        nc.vector.memset(k_stack[n][MAX_ROW:STACK, :, :], 1.0).then_inc(dve_setup, 1)
                    nc.vector.memset(av_ps[:, :], 0.0).then_inc(dve_setup, 1)

                @block.scalar
                def _(act):
                    act.wait_ge(pe_setup, 3)
                    for n, w in enumerate((wq_t, wk_t, wv_t)):
                        nc.scalar.activation(w[:, :], sm_ps[0][:, 0, n * P:(n + 1) * P], ACT.Copy)
                    act.wait_ge(pe_setup, 4)
                    nc.scalar.activation(bq_c[:, :], sm_ps[1][:, 0, 0:1], ACT.Copy, scale=SCALE)
                    nc.scalar.activation(bk_c[:, :], sm_ps[1][:, 0, 1:2], ACT.Copy)
                    nc.scalar.activation(bv_b[:, :], sm_ps[1][:, 0, P:2 * P], ACT.Copy)
                    act.wait_ge(pe_setup, 5)
                    nc.scalar.activation(wo_t[:, :], sm_ps[1][:, 1, 0:P], ACT.Copy)

            names = ("xt_done q_done k_done v_done maxt_done yt_done ynt_done wo_done st_done sm_done av_done "
                     "xt_sb q_sb k_sb ynt_sb y_ready exp_done "
                     "x1t_done x1t_sb logits_done logits_sb exps_sb top_step choice_done rank_done slot_step place_out place_next copied "
                     "red_done negmax_sb yn_inv yn_sb v_sb res_ready stats_ready mv_ready x1_ready "
                     "qpart_ready kpart_ready maxpart_ready vareps_ready split_done maxsplit_done xbo_ready rstd_ready "
                     "parts_stored")
            S = {n: sem(n) for n in names.split()}
            x_loaded = [sem(f"x_loaded{n}") for n in range(2)]
            xres_loaded = [sem(f"xres_loaded{n}") for n in range(2)]
            stack_loaded = [sem(f"stack_loaded{n}") for n in range(HG)]
            x1_stored = [sem(f"x1_stored{n}") for n in range(2)]
            scattered = [sem(f"scattered{n}") for n in range(2)]
            maxrow_loaded = [sem(f"maxrow_loaded{n}") for n in range(2)]
            LOADS = (SLOTS + len(Q_RUNS)) * 16

            def schedule(engine, body):
                def flags(n):
                    return 0 <= n < B, 0 <= n + 1 < B, n + 2 < B, 0 <= n - 1 < B, 0 <= n - 2 < B
                for n in range(-2, 3):
                    body(Batch(0, n), *flags(n))
                with engine.Fori(1, B // 2 - 2) as i:
                    for c in (1, 2):
                        body(Batch(i, c), *flags(2 + c))
                for n in range(B - 3, B + 2):
                    body(Batch(0, n), *flags(n))

            with nc.Block() as block:
                @block.tensor
                def _(pe):
                    def body(b, cur, nxt, proj, prev, prev2):
                        n1, n2, p1, p2 = b + 1, b + 2, b + -1, b + -2

                        def misc(s):
                            if s == 2 and cur:
                                wait(pe, S["red_done"], b.count(32, 32))
                                wait(pe, S["negmax_sb"], b.count(2, 1))
                                wait(pe, S["yn_sb"], p1.count(HG, 3))
                                nc.tensor.transpose(misc_ps[0:HALF, 0:P], row_max[:, HALF:UNITS], ident[:, :]).then_inc(S["maxt_done"], 1)
                            if s == 5 and proj:
                                pe.wait_ge(x_loaded[n2.parity], n2.count_parity(16, 16))
                                wait(pe, S["negmax_sb"], b.count(2, 2) if cur else 0)
                                wait(pe, S["k_sb"], n1.count(1, 1))
                                for t in range(QT):
                                    last = nc.tensor.transpose(misc_ps[:, t * P:(t + 1) * P], x_in[n2.parity][:, t, :], ident[:, :])
                                last.then_inc(S["xt_done"], 1)
                            if s == 8 and proj:
                                pe.wait_ge(S["xt_sb"], n2.count(1, 1))
                                nc.tensor.matmul(misc_ps[:, :], wq_t[:, :], x_t[n2.parity][:, :], start=True, stop=True).then_inc(S["q_done"], 1)
                            if s == 11 and proj:
                                pe.wait_ge(S["q_sb"], n2.count(1, 1))
                                nc.tensor.matmul(misc_ps[:, :], wk_t[:, :], x_t[n2.parity][:, :], start=True, stop=True).then_inc(S["k_done"], 1)
                            if s == 14 and prev:
                                wait(pe, S["k_sb"], n2.count(1, 1) if proj else 0)
                                wait(pe, S["negmax_sb"], b.count(2, 2) if cur else 0)
                                wait(pe, S["yn_sb"], p1.count(HG, 3))
                                y_transpose(p1, 3)
                            if s == 17 and prev:
                                pe.wait_ge(S["yn_sb"], p1.count(HG, 4))
                                for t in range(QT):
                                    last = nc.tensor.transpose(misc_ps[:, t * P:(t + 1) * P], y_norm[:, t, :, :].rearrange("p h r -> p (h r)"), ident[:, :])
                                last.then_inc(S["ynt_done"], 1)
                            if s == 20 and prev:
                                pe.wait_ge(S["ynt_sb"], p1.count(1, 1))
                                for t in range(QT):
                                    last = nc.tensor.matmul(misc_ps[:, t * P:(t + 1) * P], y_t[:, t * P:(t + 1) * P], wo_t[:, :], start=True, stop=True)
                                last.then_inc(S["wo_done"], 1)
                            if s == 23 and prev2:
                                wait(pe, S["res_ready"], p1.count(1, 1) if prev else 0)
                                wait(pe, S["logits_sb"], p2.count(1, 1))
                                pe.wait_ge(S["choice_done"], p2.count(1, 1))
                                for t in range(QT + 1):
                                    for k in range(t):
                                        last = nc.tensor.matmul(misc_ps[:, t * E:(t + 1) * E], ones[:, :], chosen_any[p2.parity][:, k, :],
                                                                start=(k == 0), stop=(t == QT and k == t - 1))
                                    if t < QT:
                                        nc.tensor.matmul(misc_ps[:, t * E:(t + 1) * E], before[:, :], chosen_any[p2.parity][:, t, :],
                                                         start=(t == 0), stop=True)
                                last.then_inc(S["rank_done"], 1)
                            if s == 26 and cur:
                                wait(pe, S["res_ready"], p1.count(1, 1) if prev else 0)
                                wait(pe, S["slot_step"], p2.count(8, 2) if prev2 else 0)
                                wait(pe, S["k_sb"], n2.count(1, 1) if proj else 0)
                                y_transpose(b, 0)
                            if s == 30 and nxt:
                                wait(pe, S["yn_sb"], b.count(HG, 1) if cur else 0)
                                wait(pe, S["k_sb"], n2.count(1, 1) if proj else 0)
                                wait(pe, S["xt_sb"], n1.count(1, 1))
                                for t in range(QT):
                                    last = nc.tensor.matmul(misc_ps[:, t * P:(t + 1) * P], x_t[n1.parity][:, t * P:(t + 1) * P], wv_t[:, :], start=True, stop=True)
                                last.then_inc(S["v_done"], 1)
                            if s == 36 and nxt:
                                pe.wait_ge(S["red_done"], n1.count(32, 16))
                                pe.wait_ge(S["v_sb"], n1.count(1, 1))
                                nc.tensor.transpose(misc_ps[0:HALF, 0:P], row_max[:, 0:HALF], ident[:, :]).then_inc(S["maxt_done"], 1)
                            if s == 42 and cur:
                                wait(pe, S["negmax_sb"], n1.count(2, 1) if nxt else 0)
                                wait(pe, S["yn_sb"], b.count(HG, 1))
                                y_transpose(b, 1)
                            if s == 46 and prev:
                                wait(pe, S["yn_sb"], b.count(HG, 2) if cur else 0)
                                wait(pe, S["slot_step"], p2.count(8, 2) if prev2 else 0)
                                pe.wait_ge(S["x1_ready"], p1.count(QT, QT))
                                for t in range(QT):
                                    last = nc.tensor.transpose(misc_ps[:, t * P:(t + 1) * P], rows[p1.parity][0][:, t, 0:D], ident[:, :])
                                last.then_inc(S["x1t_done"], 1)
                            if s == 50 and prev:
                                pe.wait_ge(S["x1t_sb"], p1.count(1, 1))
                                for t in range(QT):
                                    last = nc.tensor.matmul(misc_ps[:, t * E:(t + 1) * E], x1_t[:, t * P:(t + 1) * P], gate_t[:, :], start=True, stop=True)
                                last.then_inc(S["logits_done"], 1)
                            if s == 58 and cur:
                                pe.wait_ge(S["yn_sb"], b.count(HG, 2))
                                wait(pe, S["logits_sb"], p1.count(1, 1) if prev else 0)
                                y_transpose(b, 2)

                        def y_transpose(n, hg):
                            pe.wait_ge(S["y_ready"], n.count(HG, hg + 1))
                            for t in range(QT):
                                last = nc.tensor.transpose(misc_ps[:, t * P:(t + 1) * P], y_sb[hg % 2][:, t * P:(t + 1) * P], ident[:, :])
                            last.then_inc(S["yt_done"], 1)

                        def av(n, j):
                            hg, kb = divmod(j, QT)
                            if j == 0:
                                wait(pe, S["v_sb"], n.count(1, 1))
                            if kb == 0:
                                wait(pe, S["y_ready"], n.count(HG, hg))
                            pe.wait_ge(S["exp_done"], n.count(UNITS, 4 * j + 4))
                            for g in range(HG):
                                last = nc.tensor.matmul(av_ps[32 * g:32 * g + V_COLS, :], v_one[n.parity][:, kb, HG * hg + g, :],
                                                        probs[:, (4 * j + g) % P_RING, :], start=(kb == 0), stop=(kb == QT - 1),
                                                        tile_position=(0, 32 * g))
                            last.then_inc(S["av_done"], 1)

                        for s in range(UNITS):
                            misc(s)
                            hg, k, g = s // GROUP, (s % GROUP) // HG, s % HG
                            if cur:
                                h = HG * hg + g
                                wait(pe, S["exp_done"], b.count(UNITS, s - 1))
                                if s % HALF == 0:
                                    pe.wait_ge(maxrow_loaded[s // HALF], b.count(48, 48))
                                nc.tensor.matmul(st_ps[s % 2][:, :], k_stack[b.parity][0:STACK, h, k * P:(k + 1) * P],
                                                 q_stack[b.parity][0:STACK, h, :], start=True, stop=True).then_inc(S["st_done"], 1)
                            if nxt:
                                h = HG * hg + k
                                if s % GROUP == 0:
                                    pe.wait_ge(stack_loaded[hg], n1.count(LOADS, LOADS))
                                if s % 2 == 0:
                                    wait(pe, S["red_done"], n1.count(32, s // 2 - 1))
                                last = nc.tensor.matmul(sm_ps[(s // 2) % 2][:, s % 2, :], q_stack[n1.parity][0:MAX_ROW, h, g * P:(g + 1) * P],
                                                        k_stack[n1.parity][0:MAX_ROW, h, :], start=True, stop=True)
                                if s % 2 == 1:
                                    last.then_inc(S["sm_done"], 1)
                            j, off = divmod(s - AV_LAG, 4)
                            if off == 0:
                                if j >= 0 and cur:
                                    av(b, j)
                                if j < 0 and prev:
                                    av(p1, j + 16)

                    schedule(pe, body)

                @block.scalar
                def _(act):
                    def body(b, cur, nxt, proj, prev, prev2):
                        n1, n2, p1, p2 = b + 1, b + 2, b + -1, b + -2

                        def y_out(n, hg):
                            act.wait_ge(S["av_done"], n.count(16, 4 * hg + 4))
                            wait(act, S["yt_done"], n.count(HG, hg - 1))
                            nc.scalar.activation(y_sb[hg % 2][:, :], av_ps[:, :], ACT.Copy).then_inc(S["y_ready"], 1)

                        for s in range(UNITS):
                            if s == 3 and prev:
                                y_out(p1, 3)
                            if s == 6 and proj:
                                act.wait_ge(S["xt_done"], n2.count(1, 1))
                                wait(act, S["v_done"], b.count(1, 1))
                                nc.scalar.activation(x_t[n2.parity][:, :], misc_ps[:, :], ACT.Copy).then_inc(S["xt_sb"], 1)
                            if s == 9 and proj:
                                act.wait_ge(S["q_done"], n2.count(1, 1))
                                wait(act, S["split_done"], n1.count(2, 1))
                                nc.scalar.activation(q_f[:, :], misc_ps[:, :], ACT.Identity, bias=bq_c[:, :], scale=SCALE).then_inc(S["q_sb"], 1)
                            if s == 12 and proj:
                                act.wait_ge(S["k_done"], n2.count(1, 1))
                                wait(act, S["split_done"], n1.count(2, 2))
                                nc.scalar.activation(k_f[:, :], misc_ps[:, :], ACT.Identity, bias=bk_c[:, :]).then_inc(S["k_sb"], 1)
                            if s == 18 and prev:
                                act.wait_ge(S["ynt_done"], p1.count(1, 1))
                                wait(act, S["wo_done"], p1.count(1, 0))
                                nc.scalar.activation(y_t[:, :], misc_ps[:, :], ACT.Copy).then_inc(S["ynt_sb"], 1)
                            if s == 35 and prev:
                                act.wait_ge(S["x1_ready"], p1.count(QT, QT))
                                nc.scalar.activation(rows[p1.parity][1][:, :, 0:D], rows[p1.parity][0][:, :, 0:D], ACT.Copy).then_inc(S["copied"], 1)
                            if s == 47 and prev:
                                act.wait_ge(S["x1t_done"], p1.count(1, 1))
                                wait(act, S["logits_done"], p1.count(1, 0))
                                nc.scalar.activation(x1_t[:, :], misc_ps[:, :], ACT.Copy).then_inc(S["x1t_sb"], 1)
                            if s == 52 and prev:
                                act.wait_ge(S["logits_sb"], p1.count(1, 1))
                                nc.scalar.activation(exps[:, :, :], logits[:, :, :], ACT.Exp).then_inc(S["exps_sb"], 1)
                            if s >= GROUP and s % GROUP == 3 and cur:
                                y_out(b, s // GROUP - 1)
                            if cur:
                                act.wait_ge(S["st_done"], b.count(UNITS, s + 1))
                                if s % 4 == 0:
                                    wait(act, S["av_done"], b.count(16, s // 4 - P_RING // 4 + 1))
                                nc.scalar.activation(probs[:, s % P_RING, :], st_ps[s % 2][:, :], ACT.Exp).then_inc(S["exp_done"], 1)

                    schedule(act, body)

                @block.vector
                def _(dve):
                    def body(b, cur, nxt, proj, prev, prev2):
                        n1, n2, p1, p2 = b + 1, b + 2, b + -1, b + -2

                        def neg(n, half):
                            dve.wait_ge(S["maxt_done"], n.count(2, half + 1))
                            wait(dve, S["maxsplit_done"], n.count(2, half - 1))
                            nc.vector.tensor_scalar(neg_max[half][:, :], misc_ps[0:HALF, 0:P], -1.0, None, ALU.mult).then_inc(S["negmax_sb"], 1)

                        def y_normalise(n, hg):
                            dve.wait_ge(S["yt_done"], n.count(HG, hg + 1))
                            ps = misc_ps[:, :].rearrange("p (t g c) -> p t g c", t=QT, g=HG)
                            nc.vector.reciprocal(inv_sum[:, hg, :, :], ps[:, :, :, R]).then_inc(S["yn_inv"], 1)
                            dve.wait_ge(S["yn_inv"], n.count(HG, hg + 1))
                            wait(dve, S["ynt_done"], n.count(1, 0))
                            nc.vector.tensor_tensor(y_norm[:, :, HG * hg:HG * hg + HG, :], ps[:, :, :, 0:R],
                                                    inv_sum[:, hg, :, :].unsqueeze(3).to_broadcast([P, QT, HG, R]), ALU.mult).then_inc(S["yn_sb"], 1)

                        def layernorm(n):
                            dve.wait_ge(S["wo_done"], n.count(1, 1))
                            dve.wait_ge(S["xbo_ready"], n.count(1, 1))
                            nc.vector.tensor_tensor(res[:, :, :].rearrange("p t d -> p (t d)"), misc_ps[:, :],
                                                    x_bo[:, :, :].rearrange("p t d -> p (t d)"), ALU.add).then_inc(S["res_ready"], 1)
                            dve.wait_ge(S["res_ready"], n.count(1, 1))
                            for t in range(QT):
                                nc.vector.bn_stats(stats[:, t, :], res[:, t, :]).then_inc(S["stats_ready"], 1)

                        def moments(n):
                            for t in range(QT):
                                nc.vector.bn_aggr(mean_var[:, t, :], stats[:, t, :]).then_inc(S["mv_ready"], 1)

                        def scale_out(n):
                            dve.wait_ge(S["rstd_ready"], n.count(1, 1))
                            wait(dve, x1_stored[n.parity], n.count_parity(16, 0))
                            wait(dve, scattered[n.parity], n.count_parity(8 * 16, 0))
                            for t in range(QT):
                                nc.vector.tensor_scalar(rows[n.parity][0][:, t, 0:D], res[:, t, :], mean_var[:, t, 0:1], rstd[:, t:t + 1],
                                                        ALU.subtract, ALU.mult).then_inc(S["x1_ready"], 1)

                        def choose(n, k):
                            lg = misc_ps[:, 0:QT * E].rearrange("p (t e) -> p t e", e=E)
                            wide = lambda t: t[:, :].unsqueeze(2).to_broadcast([P, QT, E])
                            ch, rw = chosen[n.parity], rows[n.parity]
                            if k == 0:
                                dve.wait_ge(S["logits_done"], n.count(1, 1))
                            else:
                                dve.wait_ge(S["top_step"], n.count(TOP_STEPS, max(k - 1, 1)))
                            if k == 0:
                                step = nc.vector.tensor_reduce(top_logit[:, :], lg, AX.X, ALU.max)
                            elif k == 1:
                                step = nc.vector.tensor_tensor(logits[:, :, :], lg, wide(top_logit), ALU.subtract)
                                step.then_inc(S["logits_sb"], 1)
                                return
                            elif k == 2:
                                step = nc.vector.tensor_reduce(gate_sum[:, :], exps[:, :, :], AX.X, ALU.add)
                            elif k == 3:
                                step = nc.vector.reciprocal(gate_inv[:, :], gate_sum[:, :])
                            elif k == 4:
                                step = nc.vector.tensor_tensor(gate_p[:, :, :], exps[:, :, :], wide(gate_inv), ALU.mult)
                            elif k in (5, 11):
                                w = k // 11
                                step = nc.vector.tensor_reduce(best[w][:, :], (gate_p, others)[w][:, :, :], AX.X, ALU.max)
                            elif k in (6, 12):
                                w = k // 12
                                step = nc.vector.tensor_tensor(tied[:, :, :], (gate_p, others)[w][:, :, :], wide(best[w]), ALU.is_equal)
                            elif k in (7, 13):
                                step = nc.vector.tensor_tensor(tied_w[:, :, :], tied[:, :, :], prefer[:, :, :], ALU.mult)
                            elif k in (8, 14):
                                step = nc.vector.tensor_reduce(first[:, :], tied_w[:, :, :], AX.X, ALU.max)
                            elif k in (9, 15):
                                step = nc.vector.tensor_tensor(ch[k // 15][:, :, :], tied_w[:, :, :], wide(first), ALU.is_equal)
                            elif k == 10:
                                step = nc.vector.scalar_tensor_tensor(others[:, :, :], ch[0][:, :, :], -2.0, gate_p[:, :, :], ALU.mult, ALU.add)
                            elif k == 16:
                                step = nc.vector.tensor_tensor(pair_sum[:, :], best[0][:, :], best[1][:, :], ALU.add)
                            elif k == 17:
                                step = nc.vector.reciprocal(pair_inv[:, :], pair_sum[:, :])
                            elif k in (18, 19):
                                step = nc.vector.tensor_tensor(rw[k - 18][:, :, D], best[k - 18][:, :], pair_inv[:, :], ALU.mult)
                            elif k == 20:
                                step = nc.vector.tensor_tensor(chosen_any[n.parity][:, :, :], ch[0][:, :, :], ch[1][:, :, :], ALU.add)
                                step.then_inc(S["choice_done"], 1)
                                return
                            step.then_inc(S["top_step"], 1)

                        def route(n, k):
                            ch, rw = chosen[n.parity], rows[n.parity]
                            before_tile = misc_ps[:, 0:QT * E].rearrange("p (t e) -> p t e", e=E)
                            if k == 0:
                                dve.wait_ge(S["rank_done"], n.count(1, 1))
                            if k > 0:
                                dve.wait_ge(S["slot_step"], n.count(8, k))
                            if k == 7:
                                wait(dve, S["place_next"], n.count(1, 0))
                            if k == 0:
                                step = nc.vector.tensor_tensor(slot[:, :, :], before_tile, next_row[:, :].unsqueeze(1).to_broadcast([P, QT, E]), ALU.add)
                            elif k == 1:
                                step = nc.vector.tensor_tensor(next_row[:, :], misc_ps[:, QT * E:(QT + 1) * E], next_row[:, :], ALU.add)
                            elif k in (2, 4):
                                step = nc.vector.tensor_tensor(slot_of[:, :, :], slot[:, :, :], ch[k // 4][:, :, :], ALU.mult)
                            elif k in (3, 5):
                                step = nc.vector.tensor_reduce(slot_f[:, k // 5, :], slot_of[:, :, :], AX.X, ALU.add)
                            elif k == 6:
                                step = nc.vector.tensor_copy(slot_i[n.parity][:, :, :], slot_f[:, :, :])
                            elif k == 7:
                                for w in range(2):
                                    step = nc.vector.tensor_copy(rw[w][:, :, D + 1].bitcast(i32), place_f[:, w, :])
                                    if w == 0:
                                        step.then_inc(S["place_out"], 1)
                            elif k == 8:
                                step = nc.vector.tensor_scalar(place_f[:, :, :], place_f[:, :, :], float(T), None, ALU.add)
                                step.then_inc(S["place_next"], 1)
                                return
                            step.then_inc(S["slot_step"], 1)

                        for s in range(UNITS):
                            if s == 3 and cur:
                                neg(b, 1)
                            if 24 <= s <= 32 and prev2:
                                route(p2, s - 24)
                            if s == 51 and prev:
                                choose(p1, 0)
                                choose(p1, 1)
                            if s == 54 and prev:
                                dve.wait_ge(S["exps_sb"], p1.count(1, 1))
                            if 54 <= s <= 63 and prev:
                                choose(p1, 2 * (s - 53))
                                if s < 63:
                                    choose(p1, 2 * (s - 53) + 1)
                            if s == 15 and prev:
                                y_normalise(p1, 3)
                            if s == 21 and prev:
                                layernorm(p1)
                            if s == 27 and cur:
                                y_normalise(b, 0)
                            if s == 31 and nxt:
                                dve.wait_ge(S["v_done"], n1.count(1, 1))
                                wait(dve, S["av_done"], b.count(16, 0))
                                nc.vector.tensor_tensor(v_one[n1.parity][:, :, :, 0:R], misc_ps[:, :].rearrange("p (t h r) -> p t h r", t=QT, h=H),
                                                        bv_b[:, :].rearrange("p (h r) -> p h r", h=H).unsqueeze(1).to_broadcast([P, QT, H, R]),
                                                        ALU.add).then_inc(S["v_sb"], 1)
                            if s == 33 and prev:
                                scale_out(p1)
                            if s == 37 and nxt:
                                neg(n1, 0)
                            if s == 43 and cur:
                                y_normalise(b, 1)
                            if s == 59 and cur:
                                y_normalise(b, 2)
                            if s == 23 and prev:
                                dve.wait_ge(S["stats_ready"], p1.count(QT, QT))
                            if nxt and s % 2 == 1:
                                dve.wait_ge(S["sm_done"], n1.count(32, s // 2 + 1))
                                if s % HALF == 1:
                                    wait(dve, S["maxt_done"], b.count(2, s // HALF + 1))
                                nc.vector.tensor_reduce(row_max[:, s - 1:s + 1], sm_ps[(s // 2) % 2][:, :, :], AX.X, ALU.max).then_inc(S["red_done"], 1)
                            if s == 23 and prev:
                                moments(p1)

                    schedule(dve, body)

                    def step(n, instruction):
                        instruction.then_inc(table_step, 1)
                        dve.wait_ge(table_step, n)

                    step(1, nc.vector.tensor_copy(next_row_i[:, :], next_row[0:1, :]))
                    step(2, nc.vector.tensor_tensor(count_e[:, :], next_row[0:1, :], row_base[:, :], ALU.subtract))
                    step(3, nc.vector.tensor_scalar(tiles_i[:, 0, :], count_e[:, :], float(P - 1), None, ALU.add))
                    step(4, nc.vector.tensor_scalar(tiles_i[:, 1, :], tiles_i[:, 0, :], P.bit_length() - 1, None, ALU.arith_shift_right))
                    step(5, nc.vector.tensor_copy(tiles_of[:, :], tiles_i[:, 1, :]))
                    step(6, nc.vector.tensor_tensor_scan(last_tile[:, :], one_row[:, :], tiles_of[:, :], 0.0, ALU.mult, ALU.add))
                    step(7, nc.vector.tensor_scalar(jump[:, :], tiles_of[:, :], float(-P), float(CAP), ALU.mult, ALU.add))
                    step(8, nc.vector.tensor_tensor(past[:, :, :], last_tile[:, :].unsqueeze(1).to_broadcast([1, TILES, E]),
                                                    tile_no[:, :].unsqueeze(2).to_broadcast([1, TILES, E]), ALU.is_le))
                    step(9, nc.vector.tensor_reduce(table_f[:, 0, :], past[:, :, :], AX.X, ALU.add))
                    step(10, nc.vector.tensor_scalar(tile_expert[:, :], table_f[:, 0, :], float(E - 1), None, ALU.min))
                    step(11, nc.vector.tensor_tensor(past_jump[:, :, :], past[:, :, :], jump[:, :].unsqueeze(1).to_broadcast([1, TILES, E]), ALU.mult))
                    step(12, nc.vector.tensor_reduce(table_f[:, 1, :], past_jump[:, :, :], AX.X, ALU.add))
                    step(13, nc.vector.scalar_tensor_tensor(table_f[:, 2, :], tile_no[:, :], float(P), table_f[:, 1, :], ALU.mult, ALU.add))
                    nc.vector.tensor_scalar(tile_row[:, :], table_f[:, 2, :], float(E * CAP), None, ALU.min).then_inc(table_ready, 1)

                @block.gpsimd
                def _(pool):
                    def body(b, cur, nxt, proj, prev, prev2):
                        n1, n2, p1, p2 = b + 1, b + 2, b + -1, b + -2

                        def split(full, parts, rest_t, zeros, part_ready, value, last_sem):
                            nc.gpsimd.tensor_tensor(parts[:, 0, :], full, zeros, ALU.add).then_inc(part_ready, 1)
                            pool.wait_ge(part_ready, value(1))
                            nc.gpsimd.tensor_tensor(rest_t, full, parts[:, 0, :], ALU.subtract).then_inc(part_ready, 1)
                            pool.wait_ge(part_ready, value(2))
                            nc.gpsimd.tensor_tensor(parts[:, 1, :], rest_t, zeros, ALU.add).then_inc(part_ready, 1)
                            pool.wait_ge(part_ready, value(3))
                            nc.gpsimd.tensor_tensor(parts[:, 2, :], rest_t, parts[:, 1, :], ALU.subtract).then_inc(last_sem, 1)

                        def split_max(n, half):
                            pool.wait_ge(S["negmax_sb"], n.count(2, half + 1))
                            wait(pool, maxrow_loaded[half], n.count(48, 0))
                            wait(pool, S["maxsplit_done"], n.count(2, half))
                            split(neg_max[half][:, :], max_parts[half], max_rest[:, :], zeros[0:HALF, 0:P], S["maxpart_ready"],
                                  lambda k: n.count(6, 3 * half + k), S["maxsplit_done"])

                        if cur:
                            split_max(b, 1)
                        if prev:
                            pool.wait_ge(xres_loaded[p1.parity], p1.count_parity(16, 16))
                            wait(pool, S["res_ready"], p1.count(1, 0))
                            nc.gpsimd.tensor_tensor(x_bo[:, :, :], x_res[p1.parity][:, :, :], bo_b[:, :].unsqueeze(1).to_broadcast([P, QT, D]),
                                                    ALU.add).then_inc(S["xbo_ready"], 1)
                        if proj:
                            pool.wait_ge(S["q_sb"], n2.count(1, 1))
                            wait(pool, S["parts_stored"], n2.count(32, 0))
                            wait(pool, S["split_done"], n2.count(2, 0))
                            split(q_f[:, :], q_parts, rest[:, :], zeros[:, :], S["qpart_ready"], lambda k: n2.count(3, k), S["split_done"])
                        if prev:
                            pool.wait_ge(S["mv_ready"], p1.count(QT, QT))
                            nc.gpsimd.tensor_tensor(var_eps[:, :], mean_var[:, :, 1], eps_t[:, :], ALU.add).then_inc(S["vareps_ready"], 1)
                            pool.wait_ge(S["vareps_ready"], p1.count(1, 1))
                            wait(pool, S["x1_ready"], p1.count(QT, 0))
                            nc.gpsimd.tensor_tensor(rstd[:, :], var_eps[:, :], neg_half[:, :], ALU.pow).then_inc(S["rstd_ready"], 1)
                        if proj:
                            pool.wait_ge(S["k_sb"], n2.count(1, 1))
                            pool.wait_ge(S["split_done"], n2.count(2, 1))
                            split(k_f[:, :], k_parts, rest[:, :], zeros[:, :], S["kpart_ready"], lambda k: n2.count(3, k), S["split_done"])
                        if prev2:
                            pool.wait_ge(S["place_out"], p2.count(1, 1))
                            pool.wait_ge(S["slot_step"], p2.count(8, 8))
                            pool.wait_ge(S["copied"], p2.count(1, 1))
                        if nxt:
                            split_max(n1, 0)
                        if prev2:
                            for w in range(2):
                                for t in range(QT):
                                    nc.gpsimd.indirect_dma_start(
                                        routed_d, bass.IndirectOffsetOnAxis(ap=slot_i[p2.parity][:, w, t:t + 1], axis=0),
                                        rows[p2.parity][w][:, t, :], None).then_inc(scattered[p2.parity], 16)

                    schedule(pool, body)

                @block.sync
                def _(sp):
                    def body(b, cur, nxt, proj, prev, prev2):
                        n1, n2, p1, p2 = b + 1, b + 2, b + -1, b + -2

                        row_of = {n: sp.snap(n.row()) if not isinstance(n.i, int) else n.row() for n in (n2, b, p1)}

                        def tokens(dram, n):
                            return dram[bass.ds(row_of[n], T), :].rearrange("(t p) d -> p t d", p=P)

                        def max_rows(n, half):
                            sp.wait_ge(S["maxsplit_done"], n.count(2, half + 1))
                            for part in range(3):
                                sp.dma_start(q_stack[n.parity][MAX_ROW + part:MAX_ROW + part + 1, half * H // 2:(half + 1) * H // 2, :].rearrange("a h (t p) -> a (h t) p", p=P),
                                             max_parts[half][:, part, :]).then_inc(maxrow_loaded[half], 16)

                        def stacks(n, hg):
                            heads = slice(HG * hg, HG * hg + HG)
                            for slot, part in enumerate(K_PARTS):
                                sp.dma_start(k_stack[n.parity][slot * R:(slot + 1) * R, heads, :],
                                             k_parts_d[n.parity][part * R:(part + 1) * R, heads, :]).then_inc(stack_loaded[hg], 16)
                            for slot, part, count in Q_RUNS:
                                sp.dma_start(q_stack[n.parity][slot * R:(slot + count) * R, heads, :],
                                             q_parts_d[n.parity][part * R:(part + count) * R, heads, :]).then_inc(stack_loaded[hg], 16)

                        if proj:
                            wait(sp, S["xt_done"], b.count(1, 1))
                            sp.dma_start(x_in[n2.parity][:, :, :], tokens(x_rows, n2)).then_inc(x_loaded[n2.parity], 16)
                        if nxt:
                            wait(sp, S["sm_done"], b.count(32, 32))
                            stacks(n1, HG - 1)
                        if cur:
                            wait(sp, S["xbo_ready"], p1.count(1, 0))
                            sp.dma_start(x_res[b.parity][:, :, :], tokens(x_rows, b)).then_inc(xres_loaded[b.parity], 16)
                            max_rows(b, 1)
                        if proj:
                            for parts_d, parts, done in ((q_parts_d, q_parts, 1), (k_parts_d, k_parts, 2)):
                                sp.wait_ge(S["split_done"], n2.count(2, done))
                                sp.dma_start(parts_d[n2.parity].rearrange("(s r) h t -> s (r h) t", r=R).rearrange("s p t -> p s t"),
                                             parts[:, :, :]).then_inc(S["parts_stored"], 16)
                        if prev:
                            sp.wait_ge(S["x1_ready"], p1.count(QT, QT))
                            sp.dma_start(tokens(x1_d, p1), rows[p1.parity][0][:, :, 0:D]).then_inc(x1_stored[p1.parity], 16)
                        if nxt:
                            max_rows(n1, 0)
                        if proj:
                            sp.wait_ge(S["parts_stored"], n2.count(32, 32))
                            stacks(n2, 0)
                            stacks(n2, 1)
                            wait(sp, S["sm_done"], n1.count(32, 24))
                            stacks(n2, 2)


                    schedule(sp, body)
                    for n in range(2):
                        sp.wait_ge(x1_stored[n], 16 * (B // 2))
                        sp.wait_ge(scattered[n], B // 2 * 8 * 16)
                    sp.wait_ge(table_ready, 1)
                    for e in range(E):
                        end = sp.value_load(next_row_i[0:1, e:e + 1], min_val=e * CAP, max_val=e * CAP + B * T)
                        sp.dma_start(routed_d[bass.ds(end, P), :], pad_rows[:, :]).then_inc(pads_stored, 16)
                    sp.wait_ge(pads_stored, 16 + 16 * E)

        moe = ExitStack()
        with moe:
            def msb(name, shape, dt=fp32):
                return moe.enter_context(nc.sbuf_tensor(name, shape, dt))

            RING = 8
            w1_n = msb("w1_n", [P, E * HB, D])
            w2_n = msb("w2_n", [P, E, HID])
            w1_t = msb("w1_t", [P, E, HID])
            w2_t = msb("w2_t", [P, E, HB, D])
            b1_b = msb("b1_b", [P, E, HID])
            b2_b = msb("b2_b", [P, E, D])
            x_rows_sb = [msb(f"x_rows_sb{n}", [P, ROW]) for n in range(RING)]
            xt_sb = [msb(f"xt_sb{n}", [P, P]) for n in range(2)]
            hidden = [msb(f"hidden{n}", [P, HID]) for n in range(2)]
            hidden_t = [msb(f"hidden_t{n}", [P, HID]) for n in range(2)]
            y_bias = [msb(f"y_bias{n}", [P, D]) for n in range(2)]
            y_out = [msb(f"y_out{n}", [P, D]) for n in range(RING)]
            up_ps = [moe.enter_context(nc.psum_tensor(f"up_ps{n}", [P, HID], fp32)) for n in range(2)]
            ht_ps = [moe.enter_context(nc.psum_tensor(f"ht_ps{n}", [P, HID], fp32)) for n in range(2)]
            down_ps = [moe.enter_context(nc.psum_tensor(f"down_ps{n}", [P, D], fp32)) for n in range(2)]
            xt_ps = [moe.enter_context(nc.psum_tensor(f"xt_ps{n}", [P, P], fp32)) for n in range(2)]

            w_loaded, b_loaded2 = sem("w12_loaded"), sem("b12_loaded")
            w_ps, w1_done, w2_done = sem("w_ps"), sem("w1_done"), sem("w2_done")
            with nc.Block() as block:
                @block.sync
                def _(sp):
                    sp.dma_start(w1_n[:, :, :], w1.rearrange("e (h p) d -> p (e h) d", p=P)).then_inc(w_loaded, 16)
                    sp.dma_start(w2_n[:, :, :], w2.rearrange("e d h -> d e h")).then_inc(w_loaded, 16)
                    sp.dma_start(b1_b[:, :, :].rearrange("p e h -> p (e h)"), b1.rearrange("(a e) h -> a (e h)", a=1).to_broadcast([P, E * HID])).then_inc(b_loaded2, 16)
                    sp.dma_start(b2_b[:, :, :].rearrange("p e d -> p (e d)"), b2.rearrange("(a e) d -> a (e d)", a=1).to_broadcast([P, E * D])).then_inc(b_loaded2, 16)
                    sp.wait_ge(b_loaded2, 32)

                @block.tensor
                def _(pe):
                    pe.wait_ge(w_loaded, 32)
                    for e in range(E):
                        if e >= 2:
                            pe.wait_ge(w1_done, e - 1)
                            pe.wait_ge(w2_done, e - 1)
                        for h in range(HB):
                            nc.tensor.transpose(up_ps[e % 2][:, h * P:(h + 1) * P], w1_n[:, e * HB + h, :], ident[:, :])
                            last = nc.tensor.transpose(ht_ps[e % 2][:, h * P:(h + 1) * P], w2_n[:, e, h * P:(h + 1) * P], ident[:, :])
                        last.then_inc(w_ps, 1)

                @block.vector
                def _(dve):
                    for e in range(E):
                        dve.wait_ge(w_ps, e + 1)
                        nc.vector.tensor_copy(w1_t[:, e, :], up_ps[e % 2][:, :]).then_inc(w1_done, 1)

                @block.scalar
                def _(act):
                    for e in range(E):
                        act.wait_ge(w_ps, e + 1)
                        nc.scalar.activation(w2_t[:, e, :, :].rearrange("p h d -> p (h d)"), ht_ps[e % 2][:, :], ACT.Copy).then_inc(w2_done, 1)

            names = "xt_done xt_out up_done biased ht_done relu_out down_done y_bias_done y_done"
            M = {n: sem("moe_" + n) for n in names.split()}
            rows_loaded = [sem(f"rows_loaded{n}") for n in range(RING)]
            y_scattered = [sem(f"y_scattered{n}") for n in range(RING)]

            def loop_tiles(engine, step):
                for u in range(RING):
                    step(0, u)
                with engine.Fori(1, TILES // RING - 1) as i:
                    for u in range(RING):
                        step(i, u)
                for u in range(RING):
                    step(TILES // RING - 1, u)

            with nc.Block() as block:
                @block.sync
                def _(sp):
                    def load(i, u):
                        row = sp.value_load(tile_row[0:1, bass.ds(i * RING + u, 1)], min_val=0, max_val=E * CAP)
                        wait(sp, y_scattered[u], i * 16)
                        sp.dma_start(x_rows_sb[u][:, :], routed_d[bass.ds(row, P), :]).then_inc(rows_loaded[u], 16)
                    loop_tiles(sp, load)
                    for n in range(RING):
                        sp.wait_ge(y_scattered[n], 16 * (TILES // RING))

                @block.tensor
                def _(pe):
                    def x_transpose(i, u):
                        pe.wait_ge(rows_loaded[u], i * 16 + 16)
                        wait(pe, M["xt_out"], i * RING + (u - 1))
                        nc.tensor.transpose(xt_ps[u % 2][:, :], x_rows_sb[u][:, 0:D], ident[:, :]).then_inc(M["xt_done"], 1)

                    def hidden_transpose(i, u):
                        pe.wait_ge(M["biased"], i * RING + (u + 1))
                        wait(pe, M["relu_out"], i * RING + (u - 1))
                        for h in range(HB):
                            last = nc.tensor.transpose(ht_ps[u % 2][:, h * P:(h + 1) * P], hidden[u % 2][:, h * P:(h + 1) * P], ident[:, :])
                        last.then_inc(M["ht_done"], 1)

                    def up(i, u, e):
                        pe.wait_ge(M["xt_out"], i * RING + (u + 1))
                        wait(pe, M["biased"], i * RING + (u - 1))
                        nc.tensor.matmul(up_ps[u % 2][:, :], xt_sb[u % 2][:, :], w1_t[:, bass.ds(e, 1), :].rearrange("p a h -> p (a h)"),
                                         start=True, stop=True).then_inc(M["up_done"], 1)

                    def down(i, u, e):
                        pe.wait_ge(M["relu_out"], i * RING + (u + 1))
                        wait(pe, M["y_bias_done"], i * RING + (u - 1))
                        for h in range(HB):
                            last = nc.tensor.matmul(down_ps[u % 2][:, :], hidden_t[u % 2][:, h * P:(h + 1) * P],
                                                    w2_t[:, bass.ds(e, 1), h, :].rearrange("p a d -> p (a d)"),
                                                    start=(h == 0), stop=(h == HB - 1))
                        last.then_inc(M["down_done"], 1)

                    def expert(i, u):
                        return pe.value_load(tile_expert[0:1, bass.ds(i * RING + u, 1)], min_val=0, max_val=E - 1)

                    def step(i, u):
                        pi, pu = (i, u - 1) if u else (i - 1, RING - 1)
                        ni, nu = (i, u + 1) if u < RING - 1 else (i + 1, 0)
                        has_last = not (isinstance(i, int) and i == 0 and u == 0)
                        has_next = not (isinstance(i, int) and i == TILES // RING - 1 and u == RING - 1)
                        e = expert(i, u)
                        if has_last:
                            e_last = expert(pi, pu)
                            hidden_transpose(pi, pu)
                        up(i, u, e)
                        if has_next:
                            x_transpose(ni, nu)
                        if has_last:
                            down(pi, pu, e_last)

                    x_transpose(0, 0)
                    loop_tiles(pe, step)
                    last_i, last_u = TILES // RING - 1, RING - 1
                    e = expert(last_i, last_u)
                    hidden_transpose(last_i, last_u)
                    down(last_i, last_u, e)

                @block.scalar
                def _(act):
                    def step(i, u):
                        act.wait_ge(M["ht_done"], i * RING + (u + 1))
                        wait(act, M["down_done"], i * RING + (u - 1))
                        nc.scalar.activation(hidden_t[u % 2][:, :], ht_ps[u % 2][:, :], ACT.Relu).then_inc(M["relu_out"], 1)
                    loop_tiles(act, step)

                @block.vector
                def _(dve):
                    def x_out(i, u):
                        dve.wait_ge(M["xt_done"], i * RING + (u + 1))
                        wait(dve, M["up_done"], i * RING + (u - 1))
                        nc.vector.tensor_copy(xt_sb[u % 2][:, :], xt_ps[u % 2][:, :]).then_inc(M["xt_out"], 1)

                    def y(i, u, e):
                        dve.wait_ge(M["down_done"], i * RING + (u + 1))
                        wait(dve, M["y_done"], i * RING + (u - 1))
                        nc.vector.tensor_tensor(y_bias[u % 2][:, :], down_ps[u % 2][:, :], b2_b[:, bass.ds(e, 1), :].rearrange("p a d -> p (a d)"),
                                                ALU.add).then_inc(M["y_bias_done"], 1)

                    def expert(i, u):
                        return dve.value_load(tile_expert[0:1, bass.ds(i * RING + u, 1)], min_val=0, max_val=E - 1)

                    def step(i, u):
                        pi, pu = (i, u - 1) if u else (i - 1, RING - 1)
                        ni, nu = (i, u + 1) if u < RING - 1 else (i + 1, 0)
                        e = expert(i, u)
                        has_last = not (isinstance(i, int) and i == 0 and u == 0)
                        has_next = not (isinstance(i, int) and i == TILES // RING - 1 and u == RING - 1)
                        if has_last:
                            e_last = expert(pi, pu)
                        if has_next:
                            x_out(ni, nu)
                        dve.wait_ge(M["up_done"], i * RING + (u + 1))
                        wait(dve, M["ht_done"], i * RING + (u - 1))
                        nc.vector.tensor_tensor(hidden[u % 2][:, :], up_ps[u % 2][:, :], b1_b[:, bass.ds(e, 1), :].rearrange("p a h -> p (a h)"),
                                                ALU.add).then_inc(M["biased"], 1)
                        if has_last:
                            y(pi, pu, e_last)

                    x_out(0, 0)
                    loop_tiles(dve, step)
                    last_i, last_u = TILES // RING - 1, RING - 1
                    y(last_i, last_u, expert(last_i, last_u))

                @block.gpsimd
                def _(pool):
                    def weight(i, u):
                        pool.wait_ge(M["y_bias_done"], i * RING + (u + 1))
                        wait(pool, y_scattered[u], i * 16)
                        wait(pool, M["y_done"], i * RING + u)
                        nc.gpsimd.tensor_tensor(y_out[u][:, :], y_bias[u % 2][:, :], x_rows_sb[u][:, D:D + 1].to_broadcast([P, D]),
                                                ALU.mult).then_inc(M["y_done"], 1)

                    def scatter(u):
                        nc.gpsimd.indirect_dma_start(y_d, bass.IndirectOffsetOnAxis(ap=x_rows_sb[u][:, D + 1:D + 2].bitcast(i32), axis=0),
                                                     y_out[u][:, :], None, bounds_check=2 * B * T - 1, oob_is_err=False).then_inc(y_scattered[u], 16)

                    def step(i, u):
                        weight(i, u)
                        if not (isinstance(i, int) and i == 0 and u == 0):
                            scatter((u - 1) % RING)

                    loop_tiles(pool, step)
                    pool.wait_ge(M["y_done"], TILES)
                    scatter(RING - 1)

        fin = ExitStack()
        with fin:
            def fsb(name, shape, dt=fp32):
                return fin.enter_context(nc.sbuf_tensor(name, shape, dt))
            a_in = [[fsb(f"a_in{n}_{w}", [P, QT, D]) for w in range(3)] for n in range(4)]
            f_res = [fsb(f"f_res{n}", [P, QT, D]) for n in range(2)]
            f_sum = [fsb(f"f_sum{n}", [P, QT, D]) for n in range(2)]
            f_stats = fsb("f_stats", [P, QT, 6])
            f_mv = [fsb(f"f_mv{n}", [P, QT, 2]) for n in range(2)]
            f_ve = [fsb(f"f_ve{n}", [P, QT]) for n in range(2)]
            f_rstd = [fsb(f"f_rstd{n}", [P, QT]) for n in range(2)]
            f_out = [fsb(f"f_out{n}", [P, QT, D]) for n in range(4)]
            F = {n: sem("fin_" + n) for n in "sum res stats mv ve rstd out".split()}
            f_loaded = [sem(f"f_loaded{n}") for n in range(4)]
            f_stored = [sem(f"f_stored{n}") for n in range(4)]

            def loop_batches(engine, step):
                for u in range(5):
                    step(u // 4, u % 4)
                with engine.Fori(1, B // 4 - 1) as i:
                    for u in range(1, 5):
                        step(i + u // 4 if u > 3 else i, u % 4)
                for u in range(1, 4):
                    step(B // 4 - 1, u)

            def batch_rows(dram, first, engine):
                if not isinstance(first, int):
                    first = engine.snap(first)
                return dram[bass.ds(first, T), :].rearrange("(t p) d -> p t d", p=P)

            with nc.Block() as block:
                @block.sync
                def _(sp):
                    def load(i, u):
                        sources = [batch_rows(dram, (i * 4 + u) * T + first, sp) for dram, first in ((x1_d, 0), (y_d, 0), (y_d, B * T))]
                        wait(sp, F["out"], (i * 4 + (u - 3)) * QT)
                        for w in range(3):
                            sp.dma_start(a_in[u][w][:, :, :], sources[w]).then_inc(f_loaded[u], 16)
                    loop_batches(sp, load)

                @block.scalar
                def _(act):
                    def store(i, u):
                        rows = batch_rows(out_rows, (i * 4 + u) * T, act)
                        act.wait_ge(F["out"], (i * 4 + (u + 1)) * QT)
                        act.dma_start(rows, f_out[u][:, :, :]).then_inc(f_stored[u], 16)
                    loop_batches(act, store)
                    for n in range(4):
                        act.wait_ge(f_stored[n], 16 * (B // 4))

                @block.gpsimd
                def _(pool):
                    def rstd_of(i, u):
                        pool.wait_ge(F["mv"], (i * 4 + (u + 1)) * QT)
                        nc.gpsimd.tensor_tensor(f_ve[u % 2][:, :], f_mv[u % 2][:, :, 1], eps_t[:, :], ALU.add).then_inc(F["ve"], 1)
                        pool.wait_ge(F["ve"], i * 4 + (u + 1))
                        wait(pool, F["out"], (i * 4 + (u - 1)) * QT)
                        nc.gpsimd.tensor_tensor(f_rstd[u % 2][:, :], f_ve[u % 2][:, :], neg_half[:, :], ALU.pow).then_inc(F["rstd"], 1)

                    def step(i, u):
                        pool.wait_ge(f_loaded[u], i * 48 + 48)
                        wait(pool, F["res"], i * 4 + (u - 1))
                        nc.gpsimd.tensor_tensor(f_sum[u % 2][:, :, :], a_in[u][0][:, :, :], a_in[u][1][:, :, :], ALU.add).then_inc(F["sum"], 1)
                        if u or not isinstance(i, int):
                            rstd_of(*((i, u - 1) if u else (i - 1, 3)))
                        elif i:
                            rstd_of(i - 1, 3)

                    loop_batches(pool, step)
                    rstd_of(B // 4 - 1, 3)

                @block.vector
                def _(dve):
                    def out_of(i, u):
                        dve.wait_ge(F["rstd"], i * 4 + (u + 1))
                        wait(dve, f_stored[u], i * 16)
                        for t in range(QT):
                            nc.vector.tensor_scalar(f_out[u][:, t, :], f_res[u % 2][:, t, :], f_mv[u % 2][:, t, 0:1], f_rstd[u % 2][:, t:t + 1],
                                                    ALU.subtract, ALU.mult).then_inc(F["out"], 1)

                    def step(i, u):
                        dve.wait_ge(F["sum"], i * 4 + (u + 1))
                        wait(dve, F["out"], (i * 4 + (u - 1)) * QT)
                        nc.vector.tensor_tensor(f_res[u % 2][:, :, :], f_sum[u % 2][:, :, :], a_in[u][2][:, :, :], ALU.add).then_inc(F["res"], 1)
                        dve.wait_ge(F["res"], i * 4 + (u + 1))
                        wait(dve, F["mv"], (i * 4 + u) * QT)
                        for t in range(QT):
                            nc.vector.bn_stats(f_stats[:, t, :], f_res[u % 2][:, t, :]).then_inc(F["stats"], 1)
                        dve.wait_ge(F["stats"], (i * 4 + (u + 1)) * QT)
                        if u or not isinstance(i, int):
                            out_of(*((i, u - 1) if u else (i - 1, 3)))
                        elif i:
                            out_of(i - 1, 3)
                        for t in range(QT):
                            nc.vector.bn_aggr(f_mv[u % 2][:, t, :], f_stats[:, t, :]).then_inc(F["mv"], 1)

                    loop_batches(dve, step)
                    out_of(B // 4 - 1, 3)


_INS = ["L0_attn_x", "L0_attn_Wq", "L0_attn_bq", "L0_attn_Wk", "L0_attn_bk", "L0_attn_Wv", "L0_attn_bv", "L0_attn_Wo",
        "L0_attn_bo", "L0_attn_U", "L0_attn_V", "L0_ffn_gate_w", "L0_ffn_w1", "L0_ffn_b1", "L0_ffn_w2", "L0_ffn_b2"]


def kernel(**inputs):
    import numpy as np
    import concourse.bacc as bacc
    from concourse.bass_utils import run_bass_kernel_spmd

    nc = bacc.Bacc("TRN2", target_bir_lowering=False, num_devices=1)
    arrays, args = {}, []
    for name in _INS:
        a = np.ascontiguousarray(inputs[name])
        arrays[name] = a
        args.append(nc.dram_tensor(name, a.shape, mybir.dt.from_np(a.dtype), kind="ExternalInput").ap())
    args.append(nc.dram_tensor("out", (B, T, D), mybir.dt.float32, kind="ExternalOutput").ap())
    build_layer(nc, *args)
    return run_bass_kernel_spmd(nc, [arrays], core_ids=[0]).results[0]["out"]
```

```python
import concourse.bass as bass
from concourse import mybir
import struct
from contextlib import ExitStack

B, T, D = 16, 512, 128
H, R = 16, 8
E, HID = 8, 512
P = 128
QT = T // P
HB = HID // P
EPS = 1e-5

HG = 4
UNITS = H * QT
GROUP = UNITS // HG
SLOTS = 6
MAX_ROW = 96
STACK = MAX_ROW + 3
P_RING = 16
AV_LAG = 7
CAP = B * T + P
TILES = 2 * B * T // P + E
ROW = D + 2
TOP_STEPS = 19
V_COLS = R + 1
Q_RUNS = ((0, 0, 3), (3, 0, 2), (5, 0, 1))
K_RUNS = ((0, 0, 3), (3, 1, 2), (5, 2, 1))


def av_schedule():
    at = {}
    for j in range(UNITS // 4):
        for half, off in enumerate((0, 2) if j % QT else (1, 3)):
            last, slot = divmod(4 * j + AV_LAG + off, UNITS)
            at.setdefault(slot, []).append((j, half, bool(last)))
    return at


AV_AT = av_schedule()
Y_OUT = AV_LAG + QT * 4 - GROUP
EXPERT_AT = [UNITS - 4 * (E - e) for e in range(E)]
SCALE_AT = 40
TWO_ONES = struct.unpack("<f", struct.pack("<I", 0x3F803F80))[0]


class Batch:

    def __init__(self, i, c):
        self.i, self.c = i, c
        self.parity = c % 2

    def __add__(self, d):
        return Batch(self.i, self.c + d)

    def count(self, per_batch, events):
        return self.i * (2 * per_batch) + (self.c * per_batch + events)

    def count_parity(self, per_batch, events):
        return self.i * per_batch + ((self.c // 2) * per_batch + events)

    def row(self):
        return self.i * (2 * T) + self.c * T


def is_first(b):
    return isinstance(b.i, int) and b.c == -2


def wait(engine, sem, value):
    if isinstance(value, int) and value <= 0:
        return
    engine.wait_ge(sem, value)


def build_layer(nc, x, wq, bq, wk, bk, wv, bv, wo, bo, u, v, gate_w, w1, b1, w2, b2, out):
    fp32, bf16 = mybir.dt.float32, mybir.dt.bfloat16
    ALU, ACT, AX = mybir.AluOpType, mybir.ActivationFunctionType, mybir.AxisListType
    SCALE = float(v.shape[1]) ** -0.5

    x_rows = x.rearrange("b t d -> (b t) d")
    out_rows = out.rearrange("b t d -> (b t) d")
    q_parts_d = [nc.dram_tensor(f"q_parts_d{n}", (3 * R, H, T), bf16, kind="Internal").ap() for n in range(2)]
    k_parts_d = [nc.dram_tensor(f"k_parts_d{n}", (3 * R, H, T), bf16, kind="Internal").ap() for n in range(2)]
    x1_d = nc.dram_tensor("x1_d", (B * T, D), fp32, kind="Internal").ap()
    routed_d = nc.dram_tensor("routed_d", (E * CAP + P, ROW), fp32, kind="Internal").ap()
    y_d = nc.dram_tensor("y_d", (2 * B * T, D), fp32, kind="Internal").ap()
    i32 = mybir.dt.int32

    top = ExitStack()

    def sem(name):
        return top.enter_context(nc.semaphore(name))

    with top:
        def sb(name, shape, dt=fp32):
            return top.enter_context(nc.sbuf_tensor(name, shape, dt))

        ident = sb("ident", [P, P])
        eps_t = sb("eps_t", [P, QT])
        neg_half = sb("neg_half", [P, QT])
        wq_t = sb("wq_t", [P, P])
        wk_t = sb("wk_t", [P, P])
        wv_t = sb("wv_t", [P, P])
        wo_t = sb("wo_t", [P, P])
        bq_c = sb("bq_c", [P, 1])
        bk_c = sb("bk_c", [P, 1])
        bv_b = sb("bv_b", [P, P])
        bo_b = sb("bo_b", [P, P])
        next_row = sb("next_row", [P, E])
        pad_rows = sb("pad_rows", [P, ROW])
        row_base = sb("row_base", [1, E])
        tile_no = sb("tile_no", [1, TILES])
        next_row_i = sb("next_row_i", [1, E], i32)
        tile_expert = sb("tile_expert", [1, TILES], i32)
        tile_row = sb("tile_row", [1, TILES], i32)

        W1, W2, B1, B2 = slice(0, HID), slice(HID, 2 * HID), slice(2 * HID, 2 * HID + HB), slice(2 * HID + HB, 2 * HID + HB + D)
        experts = sb("experts", [P, E, B2.stop])

        att = ExitStack()
        with att:
            def asb(name, shape, dt=fp32):
                return att.enter_context(nc.sbuf_tensor(name, shape, dt))

            k_stack = [asb(f"k_stack{n}", [P, H, T], bf16) for n in range(2)]
            q_stack = [asb(f"q_stack{n}", [P, H, T], bf16) for n in range(2)]
            probs = asb("probs", [P, P_RING, T])
            v_one = [asb(f"v_one{n}", [P, QT, H, V_COLS]) for n in range(2)]
            x_in = [asb(f"x_in{n}", [P, QT, D]) for n in range(2)]
            x_res = [asb(f"x_res{n}", [P, QT, D]) for n in range(2)]
            x_bo = asb("x_bo", [P, QT, D])
            x_t = [asb(f"x_t{n}", [P, T]) for n in range(2)]
            q_f = asb("q_f", [P, T])
            k_f = asb("k_f", [P, T])
            rest = asb("rest", [P, T])
            zeros = asb("zeros", [P, T])
            q_parts = asb("q_parts", [P, 3, T], bf16)
            k_parts = asb("k_parts", [P, 3, T], bf16)
            row_max = asb("row_max", [P, UNITS])
            HALF = UNITS // 2
            neg_max = [asb(f"neg_max{n}", [HALF, P]) for n in range(2)]
            max_rest = asb("max_rest", [HALF, P])
            max_parts = [asb(f"max_parts{n}", [HALF, 3, P], bf16) for n in range(2)]
            y_sb = [asb(f"y_sb{n}", [P, T]) for n in range(2)]
            inv_sum = asb("inv_sum", [P, HG, QT, HG])
            y_norm = asb("y_norm", [P, QT, H, R])
            y_t = asb("y_t", [P, T])
            res = asb("res", [P, QT, D])
            stats = asb("stats", [P, QT, 6])
            mean_var = asb("mean_var", [P, QT, 2])
            var_eps = asb("var_eps", [P, QT])
            rstd = asb("rstd", [P, QT])
            rows = [[asb(f"rows{n}_{w}", [P, QT, ROW]) for w in range(2)] for n in range(2)]
            x1_t = asb("x1_t", [P, T])
            gate_t = asb("gate_t", [P, E])
            prefer = asb("prefer", [P, QT, E])
            before = asb("before", [P, P], bf16)
            ones = asb("ones", [P, P], bf16)
            top_logit = asb("top_logit", [P, QT])
            logits = asb("logits", [P, QT, E])
            exps = asb("exps", [P, QT, E])
            gate_sum = asb("gate_sum", [P, QT])
            gate_inv = asb("gate_inv", [P, QT])
            gate_p = asb("gate_p", [P, QT, E])
            best = [asb(f"best{w}", [P, QT]) for w in range(2)]
            tied = asb("tied", [P, QT, E])
            tied_w = asb("tied_w", [P, QT, E])
            first = asb("first", [P, QT])
            others = asb("others", [P, QT, E])
            chosen = [[asb(f"chosen{n}_{w}", [P, QT, E]) for w in range(2)] for n in range(2)]
            pair_sum = asb("pair_sum", [P, QT])
            pair_inv = asb("pair_inv", [P, QT])
            chosen_any = [asb(f"chosen_any{n}", [P, QT, E], bf16) for n in range(2)]
            slot = asb("slot", [P, QT, E])
            slot_of = asb("slot_of", [P, QT, E])
            slot_f = asb("slot_f", [P, 2, QT])
            slot_i = [asb(f"slot_i{n}", [P, 2, QT], i32) for n in range(2)]
            place_i = asb("place_i", [P, 2, QT], i32)
            place_f = asb("place_f", [P, 2, QT])
            gate_n = asb("gate_n", [E, P])
            b1_n = asb("b1_n", [E * HB, P])
            w1_n = probs[:, 0:P_RING // 2, :].rearrange("p n (h d) -> p (n h) d", d=D)
            w2_n = probs[:, P_RING // 2:P_RING, :]
            tile_no_i = asb("tile_no_i", [1, TILES], i32)
            tiles_i = asb("tiles_i", [1, 2, E], i32)
            tiles_of = asb("tiles_of", [1, E])
            last_tile = asb("last_tile", [1, E])
            jump = asb("jump", [1, E])
            one_row = asb("one_row", [1, E])
            count_e = asb("count_e", [1, E])
            past, past_jump = (probs[0:1, n:n + 4, :].rearrange("p n t -> p (n t)")[:, 0:TILES * E].rearrange("p (t e) -> p t e", e=E) for n in (0, 4))
            table_f = asb("table_f", [1, 3, TILES])
            w_nat = probs[:, 0, :].rearrange("p (n d) -> p n d", d=P)
            vu = asb("vu", [R, 2, R])
            bcols = asb("bcols", [P, 3])
            rep = asb("rep", [R, H, R])
            head_mask = asb("head_mask", [P, H])
            vu_rep = asb("vu_rep", [P, 2, R])
            v_rh = asb("v_rh", [P, R, H])
            v_hr = asb("v_hr", [P, H, R])
            u_hr = asb("u_hr", [P, H, R])
            wo_nt = asb("wo_nt", [P, P])
            bv_wide = asb("bv_wide", [P, P])

            st_ps = [att.enter_context(nc.psum_tensor(f"st_ps{n}", [P, T], fp32)) for n in range(2)]
            sm_ps = [att.enter_context(nc.psum_tensor(f"sm_ps{n}", [P, 2, T], fp32)) for n in range(2)]
            av_ps = att.enter_context(nc.psum_tensor("av_ps", [P, T], fp32))
            misc_ps = att.enter_context(nc.psum_tensor("misc_ps", [P, T], fp32))

            w_loaded, vu_loaded, b_loaded, bo_loaded = (sem(n) for n in ("w_loaded", "vu_loaded", "b_loaded", "bo_loaded"))
            const_ready, pool_setup = sem("const_ready"), sem("pool_setup")
            b1_loaded, b2_loaded = sem("b1_loaded"), sem("b2_loaded")
            experts_loaded = [sem(f"experts_loaded{n}") for n in range(2)]
            experts_ps, experts_copied = sem("experts_ps"), sem("experts_copied")
            cleared, cleared_pool = sem("cleared"), sem("cleared_pool")
            x_loaded = [sem(f"x_loaded{n}") for n in range(2)]
            table_step = sem("table_step")
            gate_loaded, pads_ready, pads_stored = sem("gate_loaded"), sem("pads_ready"), sem("pads_stored")
            pe_setup, dve_setup, place_ready = sem("pe_setup"), sem("dve_setup"), sem("place_ready")
            def clear_q(engine, n):
                return engine.memset(q_stack[n][0:MAX_ROW, :, :].rearrange("p h t -> p (h t)").bitcast(fp32), 0.0)

            def clear_k(engine, n):
                return engine.memset(k_stack[n][0:MAX_ROW, :, :].rearrange("p h t -> p (h t)").bitcast(fp32), 0.0)

            def ones_k(engine, n):
                return engine.memset(k_stack[n][MAX_ROW:STACK, :, :].rearrange("p h t -> p (h t)").bitcast(fp32), TWO_ONES)

            with nc.Block() as block:
                @block.sync
                def _(sp):
                    for n, w in enumerate((wq, wk, wv, wo)):
                        sp.dma_start(w_nat[:, n, :], w).then_inc(w_loaded, 16)
                    for n, w in enumerate((v, u)):
                        sp.dma_start(vu[:, n, :], w).then_inc(vu_loaded, 16)
                    for n, w in enumerate((bq, bk, bv)):
                        sp.dma_start(bcols[:, n:n + 1], w.rearrange("(p a) -> p a", a=1)).then_inc(b_loaded, 16)
                    sp.dma_start(bo_b[:, :], bo.rearrange("(a n) -> a n", a=1).to_broadcast([P, D])).then_inc(bo_loaded, 16)
                    sp.dma_start(gate_n[:, :], gate_w).then_inc(gate_loaded, 16)
                    sp.dma_start(b1_n[:, :], b1.rearrange("e (h p) -> (e h) p", p=P)).then_inc(b1_loaded, 16)
                    for n in range(2):
                        sp.dma_start(x_in[n][:, :, :], x_rows[n * T:(n + 1) * T, :].rearrange("(t p) d -> p t d", p=P)).then_inc(x_loaded[n], 16)
                    sp.wait_ge(bo_loaded, 16)
                    sp.wait_ge(pads_ready, 2)
                    sp.dma_start(routed_d[E * CAP:E * CAP + P, :], pad_rows[:, :]).then_inc(pads_stored, 16)
                    sp.wait_ge(pads_stored, 16)

                @block.gpsimd
                def _(pool):
                    nc.gpsimd.memset(ident[:, :], 0.0).then_inc(pool_setup, 1)
                    nc.gpsimd.memset(rep[:, :, :], 0.0).then_inc(pool_setup, 1)
                    nc.gpsimd.memset(head_mask[:, :], 1.0).then_inc(pool_setup, 1)
                    pool.wait_ge(pool_setup, 3)
                    nc.gpsimd.affine_select(out=ident[:, :], in_=ident[:, :], compare_op=ALU.not_equal, fill=1.0,
                                            base=0, pattern=[[-1, P]], channel_multiplier=1).then_inc(const_ready, 1)
                    nc.gpsimd.affine_select(out=rep[:, :, :], in_=rep[:, :, :], compare_op=ALU.not_equal, fill=1.0,
                                            base=0, pattern=[[0, H], [-1, R]], channel_multiplier=1).then_inc(const_ready, 1)
                    nc.gpsimd.affine_select(out=head_mask[:, :], in_=head_mask[:, :], compare_op=ALU.is_ge, fill=0.0,
                                            base=0, pattern=[[-R, H]], channel_multiplier=1).then_inc(pool_setup, 1)
                    pool.wait_ge(pool_setup, 4)
                    nc.gpsimd.affine_select(out=head_mask[:, :], in_=head_mask[:, :], compare_op=ALU.is_ge, fill=0.0,
                                            base=R - 1, pattern=[[R, H]], channel_multiplier=-1).then_inc(const_ready, 1)
                    nc.gpsimd.memset(eps_t[:, :], EPS).then_inc(const_ready, 1)
                    nc.gpsimd.memset(neg_half[:, :], -0.5).then_inc(const_ready, 1)
                    nc.gpsimd.memset(zeros[:, :], 0.0).then_inc(const_ready, 1)
                    for n in range(2):
                        nc.gpsimd.memset(v_one[n][:, :, :, R:R + 1], 1.0).then_inc(const_ready, 1)
                    nc.gpsimd.memset(pad_rows[:, 0:ROW - 1], 0.0).then_inc(pads_ready, 1)
                    nc.gpsimd.memset(pad_rows[:, ROW - 1:ROW].bitcast(i32), 2 * B * T).then_inc(pads_ready, 1)
                    for e in range(E):
                        nc.gpsimd.memset(prefer[:, :, e:e + 1], float(E - e)).then_inc(const_ready, 1)
                        nc.gpsimd.memset(next_row[:, e:e + 1], float(e * CAP)).then_inc(const_ready, 1)
                        nc.gpsimd.memset(row_base[:, e:e + 1], float(e * CAP)).then_inc(const_ready, 1)
                    nc.gpsimd.memset(ones[:, :], 1.0).then_inc(const_ready, 1)
                    nc.gpsimd.memset(before[:, :], 1.0).then_inc(pool_setup, 1)
                    pool.wait_ge(pool_setup, 5)
                    nc.gpsimd.affine_select(out=before[:, :], in_=before[:, :], compare_op=ALU.is_gt, fill=0.0,
                                            base=0, pattern=[[1, P]], channel_multiplier=-1).then_inc(const_ready, 1)
                    nc.gpsimd.iota(place_i[:, :, :], pattern=[[B * T, 2], [P, QT]], base=0, channel_multiplier=1).then_inc(place_ready, 1)
                    nc.gpsimd.iota(tile_no_i[:, :], pattern=[[1, TILES]], base=0, channel_multiplier=0).then_inc(place_ready, 1)

                @block.tensor
                def _(pe):
                    pe.wait_ge(const_ready, 3)
                    pe.wait_ge(vu_loaded, 32)
                    for n in range(2):
                        last = nc.tensor.matmul(misc_ps[:, n * R:(n + 1) * R], rep[:, :, :].rearrange("p h d -> p (h d)"),
                                                vu[:, n, :], start=True, stop=True)
                    last.then_inc(pe_setup, 1)
                    pe.wait_ge(w_loaded, 64)
                    pe.wait_ge(gate_loaded, 16)
                    nc.tensor.transpose(st_ps[1][:, 0:E], gate_n[:, :], ident[0:E, 0:E])
                    pe.wait_ge(b1_loaded, 16)
                    nc.tensor.transpose(st_ps[1][:, E:E + E * HB], b1_n[:, :], ident[0:E * HB, 0:E * HB])
                    nc.tensor.transpose(st_ps[0][:, 0:P], w_nat[:, 3, :], ident[:, :]).then_inc(pe_setup, 1)
                    pe.wait_ge(dve_setup, 5)
                    pe.wait_ge(b_loaded, 48)
                    vrh = v_rh[:, :, :].rearrange("p r h -> p (r h)")
                    vhr = v_hr[:, :, :].rearrange("p h r -> p (h r)")
                    nc.tensor.matmul(sm_ps[0][:, 0, 0:P], w_nat[:, 0, :], vrh, start=True, stop=True)
                    nc.tensor.matmul(sm_ps[0][:, 0, P:2 * P], w_nat[:, 1, :], vrh, start=True, stop=True)
                    nc.tensor.matmul(sm_ps[0][:, 0, 2 * P:3 * P], w_nat[:, 2, :], vhr, start=True, stop=True).then_inc(pe_setup, 1)
                    nc.tensor.matmul(sm_ps[1][:, 0, 0:1], vrh, bcols[:, 0:1], start=True, stop=True)
                    nc.tensor.matmul(sm_ps[1][:, 0, 1:2], vrh, bcols[:, 1:2], start=True, stop=True)
                    nc.tensor.matmul(sm_ps[1][:, 0, P:2 * P], bv_wide[:, :], vhr, start=True, stop=True).then_inc(pe_setup, 1)
                    pe.wait_ge(dve_setup, 6)
                    nc.tensor.matmul(sm_ps[1][:, 1, 0:P], u_hr[:, :, :].rearrange("p h r -> p (h r)"), wo_nt[:, :],
                                     start=True, stop=True).then_inc(pe_setup, 1)

                @block.vector
                def _(dve):
                    dve.wait_ge(pe_setup, 1)
                    nc.vector.tensor_copy(vu_rep[:, :, :].rearrange("p a r -> p (a r)"), misc_ps[:, 0:2 * R]).then_inc(dve_setup, 1)
                    dve.wait_ge(dve_setup, 1)
                    dve.wait_ge(const_ready, 3)
                    mask_h = head_mask[:, :].unsqueeze(1).to_broadcast([P, R, H])
                    mask_r = head_mask[:, :].unsqueeze(2).to_broadcast([P, H, R])
                    nc.vector.tensor_tensor(v_rh[:, :, :], vu_rep[:, 0, :].unsqueeze(2).to_broadcast([P, R, H]), mask_h, ALU.mult).then_inc(dve_setup, 1)
                    nc.vector.tensor_tensor(v_hr[:, :, :], vu_rep[:, 0, :].unsqueeze(1).to_broadcast([P, H, R]), mask_r, ALU.mult).then_inc(dve_setup, 1)
                    nc.vector.tensor_tensor(u_hr[:, :, :], vu_rep[:, 1, :].unsqueeze(1).to_broadcast([P, H, R]), mask_r, ALU.mult).then_inc(dve_setup, 1)
                    dve.wait_ge(b_loaded, 48)
                    nc.vector.tensor_copy(bv_wide[:, :], bcols[:, 2:3].to_broadcast([P, P])).then_inc(dve_setup, 1)
                    dve.wait_ge(pe_setup, 2)
                    nc.vector.tensor_copy(wo_nt[:, :], st_ps[0][:, 0:P]).then_inc(dve_setup, 1)
                    nc.vector.tensor_copy(gate_t[:, :], st_ps[1][:, 0:E]).then_inc(dve_setup, 1)
                    nc.vector.tensor_copy(experts[:, :, B1], st_ps[1][:, E:E + E * HB].rearrange("p (e h) -> p e h", h=HB)).then_inc(dve_setup, 1)
                    dve.wait_ge(place_ready, 2)
                    nc.vector.tensor_copy(tile_no[:, :], tile_no_i[:, :]).then_inc(dve_setup, 1)
                    nc.vector.memset(one_row[:, :], 1.0).then_inc(dve_setup, 1)
                    nc.vector.tensor_copy(place_f[:, :, :], place_i[:, :, :]).then_inc(dve_setup, 1)
                    nc.vector.memset(av_ps[:, :], 0.0).then_inc(dve_setup, 1)

                @block.scalar
                def _(act):
                    act.wait_ge(pe_setup, 3)
                    for n, w in enumerate((wq_t, wk_t, wv_t)):
                        nc.scalar.activation(w[:, :], sm_ps[0][:, 0, n * P:(n + 1) * P], ACT.Copy)
                    act.wait_ge(pe_setup, 4)
                    nc.scalar.activation(bq_c[:, :], sm_ps[1][:, 0, 0:1], ACT.Copy, scale=SCALE)
                    nc.scalar.activation(bk_c[:, :], sm_ps[1][:, 0, 1:2], ACT.Copy)
                    nc.scalar.activation(bv_b[:, :], sm_ps[1][:, 0, P:2 * P], ACT.Copy)
                    act.wait_ge(pe_setup, 5)
                    nc.scalar.activation(wo_t[:, :], sm_ps[1][:, 1, 0:P], ACT.Copy)

            names = ("xt_done q_done k_done v_done maxt_done yt_done ynt_done wo_done st_done sm_done av_done "
                     "xt_sb q_sb k_sb ynt_sb y_ready exp_done "
                     "x1t_done x1t_sb logits_done logits_sb exps_sb top_step choice_done rank_done slot_step place_out place_next copied "
                     "red_done negmax_sb yn_inv yn_sb v_sb res_ready stats_ready mv_ready x1_ready "
                     "qpart_ready kpart_ready maxpart_ready vareps_ready split_done maxsplit_done xbo_ready rstd_ready "
                     "parts_stored")
            S = {n: sem(n) for n in names.split()}
            xres_loaded = [sem(f"xres_loaded{n}") for n in range(2)]
            stack_loaded = [sem(f"stack_loaded{n}") for n in range(HG)]
            x1_stored = [sem(f"x1_stored{n}") for n in range(2)]
            scattered = [sem(f"scattered{n}") for n in range(2)]
            maxrow_loaded = [sem(f"maxrow_loaded{n}") for n in range(2)]
            LOADS = (len(K_RUNS) + len(Q_RUNS)) * 16

            def split(engine, queue, full, parts, rest_t, zeros, part_ready, value, last_sem):
                engine.tensor_tensor(parts[:, 0, :], full, zeros, ALU.add).then_inc(part_ready, 1)
                queue.wait_ge(part_ready, value(1))
                engine.tensor_tensor(rest_t, full, parts[:, 0, :], ALU.subtract).then_inc(part_ready, 1)
                queue.wait_ge(part_ready, value(2))
                engine.tensor_tensor(parts[:, 1, :], rest_t, zeros, ALU.add).then_inc(part_ready, 1)
                queue.wait_ge(part_ready, value(3))
                engine.tensor_tensor(parts[:, 2, :], rest_t, parts[:, 1, :], ALU.subtract).then_inc(last_sem, 1)

            def split_q(engine, queue, n):
                queue.wait_ge(S["q_sb"], n.count(1, 1))
                wait(queue, S["parts_stored"], n.count(32, 0))
                wait(queue, S["split_done"], n.count(2, 0))
                split(engine, queue, q_f[:, :], q_parts, rest[:, :], zeros[:, :], S["qpart_ready"], lambda k: n.count(3, k), S["split_done"])

            def split_k(engine, queue, n):
                queue.wait_ge(S["k_sb"], n.count(1, 1))
                queue.wait_ge(S["split_done"], n.count(2, 1))
                split(engine, queue, k_f[:, :], k_parts, rest[:, :], zeros[:, :], S["kpart_ready"], lambda k: n.count(3, k), S["split_done"])

            def schedule(engine, body):
                def flags(n):
                    return 0 <= n < B, 0 <= n + 1 < B, n + 2 < B, 0 <= n - 1 < B, 0 <= n - 2 < B
                for n in range(-2, 3):
                    body(Batch(0, n), *flags(n))
                with engine.Fori(1, B // 2 - 2) as i:
                    for c in (1, 2):
                        body(Batch(i, c), *flags(2 + c))
                for n in range(B - 3, B + 2):
                    body(Batch(0, n), *flags(n))

            with nc.Block() as block:
                @block.tensor
                def _(pe):
                    def body(b, cur, nxt, proj, prev, prev2):
                        n1, n2, p1, p2 = b + 1, b + 2, b + -1, b + -2

                        def misc(s):
                            if s == 3 and cur:
                                wait(pe, S["red_done"], b.count(32, 32))
                                wait(pe, S["negmax_sb"], b.count(2, 1))
                                wait(pe, S["yn_sb"], p1.count(HG, 3))
                                nc.tensor.transpose(misc_ps[0:HALF, 0:P], row_max[:, HALF:UNITS], ident[:, :]).then_inc(S["maxt_done"], 1)
                            if s == 7 and proj:
                                pe.wait_ge(x_loaded[n2.parity], n2.count_parity(16, 16))
                                wait(pe, S["negmax_sb"], b.count(2, 2) if cur else 0)
                                wait(pe, S["k_sb"], n1.count(1, 1))
                                for t in range(QT):
                                    last = nc.tensor.transpose(misc_ps[:, t * P:(t + 1) * P], x_in[n2.parity][:, t, :], ident[:, :])
                                last.then_inc(S["xt_done"], 1)
                            if s == 10 and proj:
                                pe.wait_ge(S["xt_sb"], n2.count(1, 1))
                                nc.tensor.matmul(misc_ps[:, :], wq_t[:, :], x_t[n2.parity][:, :], start=True, stop=True).then_inc(S["q_done"], 1)
                            if s == 13 and proj:
                                pe.wait_ge(S["q_sb"], n2.count(1, 1))
                                nc.tensor.matmul(misc_ps[:, :], wk_t[:, :], x_t[n2.parity][:, :], start=True, stop=True).then_inc(S["k_done"], 1)
                            if s == 16 and prev:
                                wait(pe, S["k_sb"], n2.count(1, 1) if proj else 0)
                                wait(pe, S["negmax_sb"], b.count(2, 2) if cur else 0)
                                wait(pe, S["yn_sb"], p1.count(HG, 3))
                                y_transpose(p1, 3)
                            if s == 19 and prev:
                                pe.wait_ge(S["yn_sb"], p1.count(HG, 4))
                                for t in range(QT):
                                    last = nc.tensor.transpose(misc_ps[:, t * P:(t + 1) * P], y_norm[:, t, :, :].rearrange("p h r -> p (h r)"), ident[:, :])
                                last.then_inc(S["ynt_done"], 1)
                            if s == 22 and prev:
                                pe.wait_ge(S["ynt_sb"], p1.count(1, 1))
                                for t in range(QT):
                                    last = nc.tensor.matmul(misc_ps[:, t * P:(t + 1) * P], y_t[:, t * P:(t + 1) * P], wo_t[:, :], start=True, stop=True)
                                last.then_inc(S["wo_done"], 1)
                            if s == 25 and prev2:
                                wait(pe, S["res_ready"], p1.count(1, 1) if prev else 0)
                                wait(pe, S["logits_sb"], p2.count(1, 1))
                                pe.wait_ge(S["choice_done"], p2.count(1, 1))
                                for t in range(QT + 1):
                                    for k in range(t):
                                        last = nc.tensor.matmul(misc_ps[:, t * E:(t + 1) * E], ones[:, :], chosen_any[p2.parity][:, k, :],
                                                                start=(k == 0), stop=(t == QT and k == t - 1))
                                    if t < QT:
                                        nc.tensor.matmul(misc_ps[:, t * E:(t + 1) * E], before[:, :], chosen_any[p2.parity][:, t, :],
                                                         start=(t == 0), stop=True)
                                last.then_inc(S["rank_done"], 1)
                            if s == 29 and cur:
                                wait(pe, S["res_ready"], p1.count(1, 1) if prev else 0)
                                wait(pe, S["slot_step"], p2.count(8, 2) if prev2 else 0)
                                wait(pe, S["k_sb"], n2.count(1, 1) if proj else 0)
                                y_transpose(b, 0)
                            if s == 33 and nxt:
                                wait(pe, S["yn_sb"], b.count(HG, 1) if cur else 0)
                                wait(pe, S["k_sb"], n2.count(1, 1) if proj else 0)
                                wait(pe, S["xt_sb"], n1.count(1, 1))
                                for t in range(QT):
                                    last = nc.tensor.matmul(misc_ps[:, t * P:(t + 1) * P], x_t[n1.parity][:, t * P:(t + 1) * P], wv_t[:, :], start=True, stop=True)
                                last.then_inc(S["v_done"], 1)
                            if s == 38 and nxt:
                                pe.wait_ge(S["red_done"], n1.count(32, 16))
                                pe.wait_ge(S["v_sb"], n1.count(1, 1))
                                nc.tensor.transpose(misc_ps[0:HALF, 0:P], row_max[:, 0:HALF], ident[:, :]).then_inc(S["maxt_done"], 1)
                            if s == 43 and cur:
                                wait(pe, S["negmax_sb"], n1.count(2, 1) if nxt else 0)
                                wait(pe, S["yn_sb"], b.count(HG, 1))
                                y_transpose(b, 1)
                            if s == 47 and prev:
                                wait(pe, S["yn_sb"], b.count(HG, 2) if cur else 0)
                                wait(pe, S["slot_step"], p2.count(8, 2) if prev2 else 0)
                                pe.wait_ge(S["x1_ready"], p1.count(QT, QT))
                                for t in range(QT):
                                    last = nc.tensor.transpose(misc_ps[:, t * P:(t + 1) * P], rows[p1.parity][0][:, t, 0:D], ident[:, :])
                                last.then_inc(S["x1t_done"], 1)
                            if s == 51 and prev:
                                pe.wait_ge(S["x1t_sb"], p1.count(1, 1))
                                for t in range(QT):
                                    last = nc.tensor.matmul(misc_ps[:, t * E:(t + 1) * E], x1_t[:, t * P:(t + 1) * P], gate_t[:, :], start=True, stop=True)
                                last.then_inc(S["logits_done"], 1)
                            if s == 58 and cur:
                                pe.wait_ge(S["yn_sb"], b.count(HG, 2))
                                wait(pe, S["logits_sb"], p1.count(1, 1) if prev else 0)
                                y_transpose(b, 2)

                        def y_transpose(n, hg):
                            pe.wait_ge(S["y_ready"], n.count(HG, hg + 1))
                            for t in range(QT):
                                last = nc.tensor.transpose(misc_ps[:, t * P:(t + 1) * P], y_sb[hg % 2][:, t * P:(t + 1) * P], ident[:, :])
                            last.then_inc(S["yt_done"], 1)

                        def av(n, j, half):
                            queries = slice(half * T // 2, (half + 1) * T // 2)
                            hg, kb = divmod(j, QT)
                            if half == 0:
                                if j == 0:
                                    wait(pe, S["v_sb"], n.count(1, 1))
                                if kb == 0:
                                    wait(pe, S["y_ready"], n.count(HG, hg))
                                pe.wait_ge(S["exp_done"], n.count(UNITS, 4 * j + 4))
                            for g in range(HG):
                                last = nc.tensor.matmul(av_ps[32 * g:32 * g + V_COLS, queries], v_one[n.parity][:, kb, HG * hg + g, :],
                                                        probs[:, (4 * j + g) % P_RING, queries], start=(kb == 0 and half == 0), stop=(kb == QT - 1 and half == 1),
                                                        tile_position=(0, 32 * g))
                            if half == 1:
                                last.then_inc(S["av_done"], 1)

                        idle_scores = nxt and not cur
                        if not idle_scores and isinstance(b.i, int) and b.c == 0:
                            pe.wait_ge(experts_copied, 2 * E)

                        def transpose_expert(e):
                            if e % (E // 2) == 0:
                                pe.wait_ge(experts_loaded[e // (E // 2)], 32)
                            wait(pe, experts_copied, 2 * e)
                            for h in range(HB):
                                nc.tensor.transpose(st_ps[0][:, h * P:(h + 1) * P], w1_n[:, e * HB + h, :], ident[:, :])
                                last = nc.tensor.transpose(st_ps[1][:, h * P:(h + 1) * P], w2_n[:, e, h * P:(h + 1) * P], ident[:, :])
                            last.then_inc(experts_ps, 1)

                        for s in range(UNITS):
                            misc(s)
                            if idle_scores and s in EXPERT_AT:
                                transpose_expert(EXPERT_AT.index(s))
                            hg, k, g = s // GROUP, (s % GROUP) // HG, s % HG
                            if cur:
                                h = HG * hg + g
                                wait(pe, S["exp_done"], b.count(UNITS, s - 1))
                                if s % HALF == 0:
                                    pe.wait_ge(maxrow_loaded[s // HALF], b.count(48, 48))
                                nc.tensor.matmul(st_ps[s % 2][:, :], k_stack[b.parity][0:STACK, h, k * P:(k + 1) * P],
                                                 q_stack[b.parity][0:STACK, h, :], start=True, stop=True).then_inc(S["st_done"], 1)
                            if nxt:
                                h = HG * hg + k
                                if s % GROUP == 0:
                                    pe.wait_ge(stack_loaded[hg], n1.count(LOADS, LOADS))
                                if s % 2 == 0:
                                    wait(pe, S["red_done"], n1.count(32, s // 2 - 1))
                                last = nc.tensor.matmul(sm_ps[(s // 2) % 2][:, s % 2, :], q_stack[n1.parity][0:MAX_ROW, h, g * P:(g + 1) * P],
                                                        k_stack[n1.parity][0:MAX_ROW, h, :], start=True, stop=True)
                                if s % 2 == 1:
                                    last.then_inc(S["sm_done"], 1)
                            for j, half, of_last in AV_AT.get(s, []):
                                if prev if of_last else cur:
                                    av(p1 if of_last else b, j, half)

                    schedule(pe, body)

                @block.scalar
                def _(act):
                    def body(b, cur, nxt, proj, prev, prev2):
                        n1, n2, p1, p2 = b + 1, b + 2, b + -1, b + -2

                        def y_out(n, hg):
                            act.wait_ge(S["av_done"], n.count(16, 4 * hg + 4))
                            wait(act, S["yt_done"], n.count(HG, hg - 1))
                            nc.scalar.activation(y_sb[hg % 2][:, :], av_ps[:, :], ACT.Copy).then_inc(S["y_ready"], 1)

                        def copy_expert(e):
                            act.wait_ge(experts_ps, e + 1)
                            nc.scalar.activation(experts[:, e, W1], st_ps[0][:, :], ACT.Copy).then_inc(experts_copied, 1)
                            nc.scalar.activation(experts[:, e, W2], st_ps[1][:, :], ACT.Copy).then_inc(experts_copied, 1)

                        for s in range(UNITS):
                            if nxt and not cur and s in EXPERT_AT:
                                copy_expert(EXPERT_AT.index(s))
                            if s == Y_OUT and prev:
                                y_out(p1, 3)
                            if s == 8 and proj:
                                act.wait_ge(S["xt_done"], n2.count(1, 1))
                                wait(act, S["v_done"], b.count(1, 1))
                                nc.scalar.activation(x_t[n2.parity][:, :], misc_ps[:, :], ACT.Copy).then_inc(S["xt_sb"], 1)
                            if s == 11 and proj:
                                act.wait_ge(S["q_done"], n2.count(1, 1))
                                wait(act, S["split_done"], n1.count(2, 1))
                                nc.scalar.activation(q_f[:, :], misc_ps[:, :], ACT.Identity, bias=bq_c[:, :], scale=SCALE).then_inc(S["q_sb"], 1)
                            if s == 14 and proj:
                                act.wait_ge(S["k_done"], n2.count(1, 1))
                                wait(act, S["split_done"], n1.count(2, 2))
                                nc.scalar.activation(k_f[:, :], misc_ps[:, :], ACT.Identity, bias=bk_c[:, :]).then_inc(S["k_sb"], 1)
                            if s == 20 and prev:
                                act.wait_ge(S["ynt_done"], p1.count(1, 1))
                                wait(act, S["wo_done"], p1.count(1, 0))
                                nc.scalar.activation(y_t[:, :], misc_ps[:, :], ACT.Copy).then_inc(S["ynt_sb"], 1)
                            if s == 60 and prev:
                                act.wait_ge(S["x1_ready"], p1.count(QT, QT))
                                nc.scalar.activation(rows[p1.parity][1][:, :, 0:D], rows[p1.parity][0][:, :, 0:D], ACT.Copy).then_inc(S["copied"], 1)
                            if s == 48 and prev:
                                act.wait_ge(S["x1t_done"], p1.count(1, 1))
                                wait(act, S["logits_done"], p1.count(1, 0))
                                nc.scalar.activation(x1_t[:, :], misc_ps[:, :], ACT.Copy).then_inc(S["x1t_sb"], 1)
                            if s == 55 and prev:
                                act.wait_ge(S["logits_sb"], p1.count(1, 1))
                                nc.scalar.activation(exps[:, :, :], logits[:, :, :], ACT.Exp).then_inc(S["exps_sb"], 1)
                            if s >= GROUP and s % GROUP == Y_OUT and cur:
                                y_out(b, s // GROUP - 1)
                            if cur:
                                act.wait_ge(S["st_done"], b.count(UNITS, s + 1))
                                if s % 4 == 0:
                                    wait(act, S["av_done"], b.count(16, s // 4 - P_RING // 4 + 1))
                                nc.scalar.activation(probs[:, s % P_RING, :], st_ps[s % 2][:, :], ACT.Exp).then_inc(S["exp_done"], 1)

                    schedule(act, body)

                @block.vector
                def _(dve):
                    def body(b, cur, nxt, proj, prev, prev2):
                        n1, n2, p1, p2 = b + 1, b + 2, b + -1, b + -2

                        def neg(n, half):
                            dve.wait_ge(S["maxt_done"], n.count(2, half + 1))
                            wait(dve, S["maxsplit_done"], n.count(2, half - 1))
                            nc.vector.tensor_scalar(neg_max[half][:, :], misc_ps[0:HALF, 0:P], -1.0, None, ALU.mult).then_inc(S["negmax_sb"], 1)

                        def y_normalise(n, hg):
                            dve.wait_ge(S["yt_done"], n.count(HG, hg + 1))
                            ps = misc_ps[:, :].rearrange("p (t g c) -> p t g c", t=QT, g=HG)
                            nc.vector.reciprocal(inv_sum[:, hg, :, :], ps[:, :, :, R]).then_inc(S["yn_inv"], 1)
                            dve.wait_ge(S["yn_inv"], n.count(HG, hg + 1))
                            wait(dve, S["ynt_done"], n.count(1, 0))
                            nc.vector.tensor_tensor(y_norm[:, :, HG * hg:HG * hg + HG, :], ps[:, :, :, 0:R],
                                                    inv_sum[:, hg, :, :].unsqueeze(3).to_broadcast([P, QT, HG, R]), ALU.mult).then_inc(S["yn_sb"], 1)

                        def layernorm(n):
                            dve.wait_ge(S["wo_done"], n.count(1, 1))
                            dve.wait_ge(S["xbo_ready"], n.count(1, 1))
                            nc.vector.tensor_tensor(res[:, :, :].rearrange("p t d -> p (t d)"), misc_ps[:, :],
                                                    x_bo[:, :, :].rearrange("p t d -> p (t d)"), ALU.add).then_inc(S["res_ready"], 1)
                            dve.wait_ge(S["res_ready"], n.count(1, 1))
                            for t in range(QT):
                                nc.vector.bn_stats(stats[:, t, :], res[:, t, :]).then_inc(S["stats_ready"], 1)

                        def moments(n):
                            for t in range(QT):
                                nc.vector.bn_aggr(mean_var[:, t, :], stats[:, t, :]).then_inc(S["mv_ready"], 1)

                        def scale_out(n, t):
                            if t == 0:
                                dve.wait_ge(S["rstd_ready"], n.count(1, 1))
                                wait(dve, x1_stored[n.parity], n.count_parity(16, 0))
                                wait(dve, scattered[n.parity], n.count_parity(8 * 16, 0))
                            nc.vector.tensor_scalar(rows[n.parity][0][:, t, 0:D], res[:, t, :], mean_var[:, t, 0:1], rstd[:, t:t + 1],
                                                    ALU.subtract, ALU.mult).then_inc(S["x1_ready"], 1)

                        def choose(n, k):
                            lg = misc_ps[:, 0:QT * E].rearrange("p (t e) -> p t e", e=E)
                            wide = lambda t: t[:, :].unsqueeze(2).to_broadcast([P, QT, E])
                            ch, rw = chosen[n.parity], rows[n.parity]
                            if k == 0:
                                dve.wait_ge(S["logits_done"], n.count(1, 1))
                            else:
                                dve.wait_ge(S["top_step"], n.count(TOP_STEPS, max(k - 1, 1)))
                            if k == 0:
                                step = nc.vector.tensor_reduce(top_logit[:, :], lg, AX.X, ALU.max)
                            elif k == 1:
                                step = nc.vector.tensor_tensor(logits[:, :, :], lg, wide(top_logit), ALU.subtract)
                                step.then_inc(S["logits_sb"], 1)
                                return
                            elif k == 2:
                                step = nc.vector.tensor_reduce(gate_sum[:, :], exps[:, :, :], AX.X, ALU.add)
                            elif k == 3:
                                step = nc.vector.reciprocal(gate_inv[:, :], gate_sum[:, :])
                            elif k == 4:
                                step = nc.vector.tensor_tensor(gate_p[:, :, :], exps[:, :, :], wide(gate_inv), ALU.mult)
                            elif k in (5, 11):
                                w = k // 11
                                step = nc.vector.tensor_reduce(best[w][:, :], (gate_p, others)[w][:, :, :], AX.X, ALU.max)
                            elif k in (6, 12):
                                w = k // 12
                                step = nc.vector.tensor_tensor(tied[:, :, :], (gate_p, others)[w][:, :, :], wide(best[w]), ALU.is_equal)
                            elif k in (7, 13):
                                step = nc.vector.tensor_tensor(tied_w[:, :, :], tied[:, :, :], prefer[:, :, :], ALU.mult)
                            elif k in (8, 14):
                                step = nc.vector.tensor_reduce(first[:, :], tied_w[:, :, :], AX.X, ALU.max)
                            elif k in (9, 15):
                                step = nc.vector.tensor_tensor(ch[k // 15][:, :, :], tied_w[:, :, :], wide(first), ALU.is_equal)
                            elif k == 10:
                                step = nc.vector.scalar_tensor_tensor(others[:, :, :], ch[0][:, :, :], -2.0, gate_p[:, :, :], ALU.mult, ALU.add)
                            elif k == 16:
                                step = nc.vector.tensor_tensor(pair_sum[:, :], best[0][:, :], best[1][:, :], ALU.add)
                            elif k == 17:
                                step = nc.vector.reciprocal(pair_inv[:, :], pair_sum[:, :])
                            elif k in (18, 19):
                                step = nc.vector.tensor_tensor(rw[k - 18][:, :, D], best[k - 18][:, :], pair_inv[:, :], ALU.mult)
                            elif k == 20:
                                step = nc.vector.tensor_tensor(chosen_any[n.parity][:, :, :], ch[0][:, :, :], ch[1][:, :, :], ALU.add)
                                step.then_inc(S["choice_done"], 1)
                                return
                            step.then_inc(S["top_step"], 1)

                        def route(n, k):
                            ch, rw = chosen[n.parity], rows[n.parity]
                            before_tile = misc_ps[:, 0:QT * E].rearrange("p (t e) -> p t e", e=E)
                            if k == 0:
                                dve.wait_ge(S["rank_done"], n.count(1, 1))
                            if k > 0:
                                dve.wait_ge(S["slot_step"], n.count(8, k))
                            if k == 7:
                                wait(dve, S["place_next"], n.count(1, 0))
                            if k == 0:
                                step = nc.vector.tensor_tensor(slot[:, :, :], before_tile, next_row[:, :].unsqueeze(1).to_broadcast([P, QT, E]), ALU.add)
                            elif k == 1:
                                step = nc.vector.tensor_tensor(next_row[:, :], misc_ps[:, QT * E:(QT + 1) * E], next_row[:, :], ALU.add)
                            elif k in (2, 4):
                                step = nc.vector.tensor_tensor(slot_of[:, :, :], slot[:, :, :], ch[k // 4][:, :, :], ALU.mult)
                            elif k in (3, 5):
                                step = nc.vector.tensor_reduce(slot_f[:, k // 5, :], slot_of[:, :, :], AX.X, ALU.add)
                            elif k == 6:
                                step = nc.vector.tensor_copy(slot_i[n.parity][:, :, :], slot_f[:, :, :])
                            elif k == 7:
                                for w in range(2):
                                    step = nc.vector.tensor_copy(rw[w][:, :, D + 1].bitcast(i32), place_f[:, w, :])
                                    if w == 0:
                                        step.then_inc(S["place_out"], 1)
                            elif k == 8:
                                step = nc.vector.tensor_scalar(place_f[:, :, :], place_f[:, :, :], float(T), None, ALU.add)
                                step.then_inc(S["place_next"], 1)
                                return
                            step.then_inc(S["slot_step"], 1)

                        for s in range(UNITS):
                            if s == 4 and cur:
                                neg(b, 1)
                            if 26 <= s <= 34 and prev2:
                                route(p2, s - 26)
                            if s == 52 and prev:
                                choose(p1, 0)
                                choose(p1, 1)
                            if s == 56 and prev:
                                dve.wait_ge(S["exps_sb"], p1.count(1, 1))
                            if s >= 56 and prev:
                                choose(p1, s - 54)
                            if s <= 10 and prev2:
                                choose(p2, s + 10)
                            if s == 17 and prev:
                                y_normalise(p1, 3)
                            if s == 23 and prev:
                                layernorm(p1)
                            if s == 30 and cur:
                                y_normalise(b, 0)
                            if s == 34 and nxt:
                                dve.wait_ge(S["v_done"], n1.count(1, 1))
                                wait(dve, S["av_done"], b.count(16, 0))
                                nc.vector.tensor_tensor(v_one[n1.parity][:, :, :, 0:R], misc_ps[:, :].rearrange("p (t h r) -> p t h r", t=QT, h=H),
                                                        bv_b[:, :].rearrange("p (h r) -> p h r", h=H).unsqueeze(1).to_broadcast([P, QT, H, R]),
                                                        ALU.add).then_inc(S["v_sb"], 1)
                            if SCALE_AT <= s < SCALE_AT + QT and prev:
                                scale_out(p1, s - SCALE_AT)
                            if s == 39 and nxt:
                                neg(n1, 0)
                            if s == 44 and cur:
                                y_normalise(b, 1)
                            if s == 59 and cur:
                                y_normalise(b, 2)
                            if s == 25 and prev:
                                dve.wait_ge(S["stats_ready"], p1.count(QT, QT))
                            if nxt and s % 2 == 1:
                                dve.wait_ge(S["sm_done"], n1.count(32, s // 2 + 1))
                                if s % HALF == 1:
                                    wait(dve, S["maxt_done"], b.count(2, s // HALF + 1))
                                nc.vector.tensor_reduce(row_max[:, s - 1:s + 1], sm_ps[(s // 2) % 2][:, :, :], AX.X, ALU.max).then_inc(S["red_done"], 1)
                            if s == 25 and prev:
                                moments(p1)

                    clear_k(nc.vector, 0).then_inc(cleared, 1)
                    split_q(nc.vector, dve, Batch(0, 0))
                    split_k(nc.vector, dve, Batch(0, 0))
                    clear_k(nc.vector, 1).then_inc(cleared, 1)
                    schedule(dve, body)

                    def step(n, instruction):
                        instruction.then_inc(table_step, 1)
                        dve.wait_ge(table_step, n)

                    step(1, nc.vector.tensor_copy(next_row_i[:, :], next_row[0:1, :]))
                    step(2, nc.vector.tensor_tensor(count_e[:, :], next_row[0:1, :], row_base[:, :], ALU.subtract))
                    step(3, nc.vector.tensor_scalar(tiles_i[:, 0, :], count_e[:, :], float(P - 1), None, ALU.add))
                    step(4, nc.vector.tensor_scalar(tiles_i[:, 1, :], tiles_i[:, 0, :], P.bit_length() - 1, None, ALU.arith_shift_right))
                    step(5, nc.vector.tensor_copy(tiles_of[:, :], tiles_i[:, 1, :]))
                    step(6, nc.vector.tensor_tensor_scan(last_tile[:, :], one_row[:, :], tiles_of[:, :], 0.0, ALU.mult, ALU.add))
                    step(7, nc.vector.tensor_scalar(jump[:, :], tiles_of[:, :], float(-P), float(CAP), ALU.mult, ALU.add))
                    step(8, nc.vector.tensor_tensor(past[:, :, :], last_tile[:, :].unsqueeze(1).to_broadcast([1, TILES, E]),
                                                    tile_no[:, :].unsqueeze(2).to_broadcast([1, TILES, E]), ALU.is_le))
                    step(9, nc.vector.tensor_reduce(table_f[:, 0, :], past[:, :, :], AX.X, ALU.add))
                    step(10, nc.vector.tensor_scalar(tile_expert[:, :], table_f[:, 0, :], float(E - 1), None, ALU.min))
                    step(11, nc.vector.tensor_tensor(past_jump[:, :, :], past[:, :, :], jump[:, :].unsqueeze(1).to_broadcast([1, TILES, E]), ALU.mult))
                    step(12, nc.vector.tensor_reduce(table_f[:, 1, :], past_jump[:, :, :], AX.X, ALU.add))
                    step(13, nc.vector.scalar_tensor_tensor(table_f[:, 2, :], tile_no[:, :], float(P), table_f[:, 1, :], ALU.mult, ALU.add))
                    nc.vector.tensor_scalar(tile_row[:, :], table_f[:, 2, :], float(E * CAP), None, ALU.min).then_inc(table_step, 1)

                @block.gpsimd
                def _(pool):
                    def body(b, cur, nxt, proj, prev, prev2):
                        n1, n2, p1, p2 = b + 1, b + 2, b + -1, b + -2

                        def split_max(n, half):
                            pool.wait_ge(S["negmax_sb"], n.count(2, half + 1))
                            wait(pool, maxrow_loaded[half], n.count(48, 0))
                            wait(pool, S["maxsplit_done"], n.count(2, half))
                            split(nc.gpsimd, pool, neg_max[half][:, :], max_parts[half], max_rest[:, :], zeros[0:HALF, 0:P], S["maxpart_ready"],
                                  lambda k: n.count(6, 3 * half + k), S["maxsplit_done"])

                        if cur:
                            split_max(b, 1)
                        if prev:
                            pool.wait_ge(xres_loaded[p1.parity], p1.count_parity(16, 16))
                            wait(pool, S["res_ready"], p1.count(1, 0))
                            nc.gpsimd.tensor_tensor(x_bo[:, :, :], x_res[p1.parity][:, :, :], bo_b[:, :].unsqueeze(1).to_broadcast([P, QT, D]),
                                                    ALU.add).then_inc(S["xbo_ready"], 1)
                        if proj and not is_first(b):
                            split_q(nc.gpsimd, pool, n2)
                        if prev:
                            pool.wait_ge(S["mv_ready"], p1.count(QT, QT))
                            nc.gpsimd.tensor_tensor(var_eps[:, :], mean_var[:, :, 1], eps_t[:, :], ALU.add).then_inc(S["vareps_ready"], 1)
                            pool.wait_ge(S["vareps_ready"], p1.count(1, 1))
                            wait(pool, S["x1_ready"], p1.count(QT, 0))
                            nc.gpsimd.tensor_tensor(rstd[:, :], var_eps[:, :], neg_half[:, :], ALU.pow).then_inc(S["rstd_ready"], 1)
                        if proj and not is_first(b):
                            split_k(nc.gpsimd, pool, n2)
                        if prev2:
                            pool.wait_ge(S["place_out"], p2.count(1, 1))
                            pool.wait_ge(S["slot_step"], p2.count(8, 8))
                            pool.wait_ge(S["copied"], p2.count(1, 1))
                        if nxt:
                            split_max(n1, 0)
                        if prev2:
                            for w in range(2):
                                for t in range(QT):
                                    nc.gpsimd.indirect_dma_start(
                                        routed_d, bass.IndirectOffsetOnAxis(ap=slot_i[p2.parity][:, w, t:t + 1], axis=0),
                                        rows[p2.parity][w][:, t, :], None).then_inc(scattered[p2.parity], 16)

                    for k, (clear, n) in enumerate(((clear_q, 0), (ones_k, 0), (clear_q, 1), (ones_k, 1))):
                        clear(nc.gpsimd, n).then_inc(cleared_pool, 1)
                        pool.wait_ge(cleared_pool, k + 1)
                    schedule(pool, body)

                @block.sync
                def _(sp):
                    def body(b, cur, nxt, proj, prev, prev2):
                        n1, n2, p1, p2 = b + 1, b + 2, b + -1, b + -2

                        row_of = {n: sp.snap(n.row()) if not isinstance(n.i, int) else n.row() for n in (n2, b, p1)}

                        def tokens(dram, n):
                            return dram[bass.ds(row_of[n], T), :].rearrange("(t p) d -> p t d", p=P)

                        def max_rows(n, half):
                            sp.wait_ge(S["maxsplit_done"], n.count(2, half + 1))
                            for part in range(3):
                                sp.dma_start(q_stack[n.parity][MAX_ROW + part:MAX_ROW + part + 1, half * H // 2:(half + 1) * H // 2, :].rearrange("a h (t p) -> a (h t) p", p=P),
                                             max_parts[half][:, part, :]).then_inc(maxrow_loaded[half], 16)

                        def stacks(n, hg):
                            heads = slice(HG * hg, HG * hg + HG)
                            for slot, part, count in K_RUNS:
                                source = k_parts_d[n.parity][part * R:(part + 1) * R, heads, :].rearrange("(c r) h t -> c r h t", c=1)
                                sp.dma_start(k_stack[n.parity][slot * R:(slot + count) * R, heads, :],
                                             source.to_broadcast([count, R, HG, T])).then_inc(stack_loaded[hg], 16)
                            for slot, part, count in Q_RUNS:
                                sp.dma_start(q_stack[n.parity][slot * R:(slot + count) * R, heads, :],
                                             q_parts_d[n.parity][part * R:(part + count) * R, heads, :]).then_inc(stack_loaded[hg], 16)

                        if is_first(b):
                            sp.wait_ge(cleared, 1)
                            sp.wait_ge(cleared_pool, 2)
                        if is_first(p1):
                            sp.wait_ge(cleared, 2)
                            sp.wait_ge(cleared_pool, 4)
                        if proj and not is_first(b) and not is_first(p1):
                            wait(sp, S["xt_done"], b.count(1, 1))
                            sp.dma_start(x_in[n2.parity][:, :, :], tokens(x_rows, n2)).then_inc(x_loaded[n2.parity], 16)
                        if nxt:
                            wait(sp, S["sm_done"], b.count(32, 32))
                            stacks(n1, HG - 1)
                        if cur:
                            wait(sp, S["xbo_ready"], p1.count(1, 0))
                            sp.dma_start(x_res[b.parity][:, :, :], tokens(x_rows, b)).then_inc(xres_loaded[b.parity], 16)
                            max_rows(b, 1)
                        if proj:
                            for parts_d, parts, done in ((q_parts_d, q_parts, 1), (k_parts_d, k_parts, 2)):
                                sp.wait_ge(S["split_done"], n2.count(2, done))
                                sp.dma_start(parts_d[n2.parity].rearrange("(s r) h t -> s (r h) t", r=R).rearrange("s p t -> p s t"),
                                             parts[:, :, :]).then_inc(S["parts_stored"], 16)
                        if prev:
                            sp.wait_ge(S["x1_ready"], p1.count(QT, QT))
                            sp.dma_start(tokens(x1_d, p1), rows[p1.parity][0][:, :, 0:D]).then_inc(x1_stored[p1.parity], 16)
                        if nxt:
                            max_rows(n1, 0)
                        if proj:
                            sp.wait_ge(S["parts_stored"], n2.count(32, 32))
                            stacks(n2, 0)
                            stacks(n2, 1)
                            wait(sp, S["sm_done"], n1.count(32, 24))
                            stacks(n2, 2)
                        if is_first(b):
                            for half in range(2):
                                some = slice(half * E // 2, (half + 1) * E // 2)
                                sp.dma_start(w1_n[:, some.start * HB:some.stop * HB, :], w1[some].rearrange("e (h p) d -> p (e h) d", p=P)).then_inc(experts_loaded[half], 16)
                                sp.dma_start(w2_n[:, some, :], w2[some].rearrange("e d h -> d e h")).then_inc(experts_loaded[half], 16)
                            sp.dma_start(experts[:, :, B2], b2.rearrange("(a e) d -> a e d", a=1).to_broadcast([P, E, D])).then_inc(b2_loaded, 16)


                    schedule(sp, body)
                    sp.wait_ge(b2_loaded, 16)
                    sp.wait_ge(table_step, 1)
                    for e in range(E):
                        end = sp.value_load(next_row_i[0:1, e:e + 1], min_val=e * CAP, max_val=e * CAP + B * T)
                        sp.dma_start(routed_d[bass.ds(end, P), :], pad_rows[:, :]).then_inc(pads_stored, 16)
                    sp.wait_ge(pads_stored, 16 + 16 * E)
                    for n in range(2):
                        sp.wait_ge(x1_stored[n], 16 * (B // 2))
                        sp.wait_ge(scattered[n], B // 2 * 8 * 16)

        moe, fin = ExitStack(), ExitStack()
        x1_sb = fin.enter_context(nc.sbuf_tensor("x1_sb", [P, B, QT, D], fp32))
        x1_back = sem("x1_back")
        with moe:
            def msb(name, shape, dt=fp32):
                return moe.enter_context(nc.sbuf_tensor(name, shape, dt))

            RING = 8
            W_AHEAD = 3
            x_rows_sb = [msb(f"x_rows_sb{n}", [P, ROW]) for n in range(RING)]
            xt_sb = [msb(f"xt_sb{n}", [P, P]) for n in range(2)]
            w_cur = [msb(f"w_cur{n}", [P, B2.stop]) for n in range(RING)]
            hidden = [msb(f"hidden{n}", [P, HB, P]) for n in range(4)]
            hidden_r = [msb(f"hidden_r{n}", [P, HB, P]) for n in range(4)]
            y_bias = [msb(f"y_bias{n}", [P, D]) for n in range(2)]
            weight = [msb(f"weight{n}", [P, 1]) for n in range(RING)]
            place = [msb(f"place{n}", [P, 1], i32) for n in range(RING)]
            y_out = [msb(f"y_out{n}", [P, D]) for n in range(RING)]
            up_ps = [moe.enter_context(nc.psum_tensor(f"up_ps{n}", [P, HID], fp32)) for n in range(4)]
            down_ps = [moe.enter_context(nc.psum_tensor(f"down_ps{n}", [P, D], fp32)) for n in range(2)]
            xt_ps = [moe.enter_context(nc.psum_tensor(f"xt_ps{n}", [P, P], fp32)) for n in range(2)]

            names = "xt_done xt_out w_copied up_done biased relu_out down_done y_bias_done y_done"
            M = {n: sem("moe_" + n) for n in names.split()}
            rows_loaded = [sem(f"rows_loaded{n}") for n in range(RING)]
            y_scattered = [sem(f"y_scattered{n}") for n in range(RING)]

            def loop_tiles(engine, step):
                for u in range(RING):
                    step(0, u)
                with engine.Fori(1, TILES // RING - 1) as i:
                    for u in range(RING):
                        step(i, u)
                for u in range(RING):
                    step(TILES // RING - 1, u)

            def before_last(i, u):
                return (i, u - 2) if u >= 2 else (i - 1, u + RING - 2)

            with nc.Block() as block:
                @block.sync
                def _(sp):
                    def load(i, u):
                        row = sp.value_load(tile_row[0:1, bass.ds(i * RING + u, 1)], min_val=0, max_val=E * CAP)
                        wait(sp, M["xt_out"], i * RING + (u - 7))
                        sp.dma_start(x_rows_sb[u][:, :], routed_d[bass.ds(row, P), :]).then_inc(rows_loaded[u], 16)
                        if isinstance(i, int) and i:
                            per_tile = B // RING
                            for b in range(u * per_tile, (u + 1) * per_tile):
                                sp.dma_start(x1_sb[:, b, :, :], x1_d[b * T:(b + 1) * T, :].rearrange("(t p) d -> p t d", p=P)).then_inc(x1_back, 16)
                    loop_tiles(sp, load)
                    for n in range(RING):
                        sp.wait_ge(y_scattered[n], 16 * (TILES // RING))

                @block.tensor
                def _(pe):
                    def x_transpose(i, u):
                        pe.wait_ge(rows_loaded[u], i * 16 + 16)
                        nc.tensor.transpose(xt_ps[u % 2][:, :], x_rows_sb[u][:, 0:D], ident[:, :]).then_inc(M["xt_done"], 1)

                    def up(i, u):
                        pe.wait_ge(M["xt_out"], i * RING + (u + 1))
                        if isinstance(i, int) and i == 0 and u < W_AHEAD:
                            pe.wait_ge(M["w_copied"], u + 1)
                        for h in range(HB):
                            last = nc.tensor.matmul(up_ps[u % 4][:, h * P:(h + 1) * P], w_cur[u][:, h * P:(h + 1) * P], xt_sb[u % 2][:, :],
                                                    start=True, stop=True)
                        last.then_inc(M["up_done"], 1)

                    def down(i, u):
                        pe.wait_ge(M["relu_out"], i * RING + (u + 1))
                        for h in range(HB):
                            last = nc.tensor.matmul(down_ps[u % 2][:, :], hidden_r[u % 4][:, h, :],
                                                    w_cur[u][:, HID + h * D:HID + (h + 1) * D],
                                                    start=(h == 0), stop=(h == HB - 1))
                        last.then_inc(M["down_done"], 1)

                    def step(i, u):
                        pi, pu = before_last(i, u)
                        ni, nu = (i, u + 1) if u < RING - 1 else (i + 1, 0)
                        has_last = not (isinstance(i, int) and i == 0 and u < 2)
                        has_next = not (isinstance(i, int) and i == TILES // RING - 1 and u == RING - 1)
                        if has_next:
                            x_transpose(ni, nu)
                        up(i, u)
                        if has_last:
                            down(pi, pu)

                    x_transpose(0, 0)
                    loop_tiles(pe, step)
                    for u in (RING - 2, RING - 1):
                        pe.wait_ge(M["y_bias_done"], TILES - RING + u - 1)
                        down(TILES // RING - 1, u)

                @block.scalar
                def _(act):
                    def copy_w(i, u):
                        e = act.value_load(tile_expert[0:1, bass.ds(i * RING + u, 1)], min_val=0, max_val=E - 1)
                        wait(act, M["y_bias_done"], i * RING + (u - 7))
                        nc.scalar.activation(w_cur[u][:, :], experts[:, bass.ds(e, 1), :].rearrange("p a h -> p (a h)"),
                                             ACT.Copy).then_inc(M["w_copied"], 1)

                    def step(i, u):
                        if not (isinstance(i, int) and i == TILES // RING - 1 and u + W_AHEAD >= RING):
                            copy_w(*((i, u + W_AHEAD) if u + W_AHEAD < RING else (i + 1, u + W_AHEAD - RING)))
                        act.wait_ge(M["biased"], i * RING + (u + 1))
                        nc.scalar.activation(hidden_r[u % 4][:, :, :], hidden[u % 4][:, :, :], ACT.Relu).then_inc(M["relu_out"], 1)

                    for u in range(W_AHEAD):
                        copy_w(0, u)
                    loop_tiles(act, step)

                @block.vector
                def _(dve):
                    def x_out(i, u):
                        dve.wait_ge(M["xt_done"], i * RING + (u + 1))
                        wait(dve, y_scattered[u], i * 16)
                        nc.vector.tensor_copy(weight[u][:, :], x_rows_sb[u][:, D:D + 1])
                        nc.vector.tensor_copy(place[u][:, :], x_rows_sb[u][:, D + 1:ROW].bitcast(i32))
                        nc.vector.tensor_copy(xt_sb[u % 2][:, :], xt_ps[u % 2][:, :]).then_inc(M["xt_out"], 1)

                    def y(i, u):
                        dve.wait_ge(M["down_done"], i * RING + (u + 1))
                        wait(dve, M["y_done"], i * RING + (u - 1))
                        nc.vector.tensor_tensor(y_bias[u % 2][:, :], down_ps[u % 2][:, :], w_cur[u][:, B2],
                                                ALU.add).then_inc(M["y_bias_done"], 1)

                    def step(i, u):
                        pi, pu = before_last(i, u)
                        ni, nu = (i, u + 1) if u < RING - 1 else (i + 1, 0)
                        has_last = not (isinstance(i, int) and i == 0 and u < 2)
                        has_next = not (isinstance(i, int) and i == TILES // RING - 1 and u == RING - 1)
                        if has_next:
                            x_out(ni, nu)
                        dve.wait_ge(M["up_done"], i * RING + (u + 1))
                        nc.vector.tensor_tensor(hidden[u % 4][:, :, :], up_ps[u % 4][:, :].rearrange("p (h t) -> p h t", t=P),
                                                w_cur[u][:, B1].unsqueeze(2).to_broadcast([P, HB, P]),
                                                ALU.add).then_inc(M["biased"], 1)
                        if has_last:
                            y(pi, pu)

                    x_out(0, 0)
                    loop_tiles(dve, step)
                    for u in (RING - 2, RING - 1):
                        y(TILES // RING - 1, u)

                @block.gpsimd
                def _(pool):
                    def weigh(i, u):
                        pool.wait_ge(M["y_bias_done"], i * RING + (u + 1))
                        wait(pool, y_scattered[u], i * 16)
                        wait(pool, M["y_done"], i * RING + u)
                        nc.gpsimd.tensor_tensor(y_out[u][:, :], y_bias[u % 2][:, :], weight[u][:, :].to_broadcast([P, D]),
                                                ALU.mult).then_inc(M["y_done"], 1)

                    def scatter(u):
                        nc.gpsimd.indirect_dma_start(y_d, bass.IndirectOffsetOnAxis(ap=place[u][:, :], axis=0),
                                                     y_out[u][:, :], None, bounds_check=2 * B * T - 1, oob_is_err=False).then_inc(y_scattered[u], 16)

                    def step(i, u):
                        weigh(i, u)
                        if not (isinstance(i, int) and i == 0 and u == 0):
                            scatter((u - 1) % RING)

                    loop_tiles(pool, step)
                    pool.wait_ge(M["y_done"], TILES)
                    scatter(RING - 1)

        with fin:
            def fsb(name, shape, dt=fp32):
                return fin.enter_context(nc.sbuf_tensor(name, shape, dt))
            y_in = [[fsb(f"y_in{n}_{w}", [P, QT, D]) for w in range(2)] for n in range(4)]
            f_sum = [fsb(f"f_sum{n}", [P, QT, D]) for n in range(2)]
            f_res = [fsb(f"f_res{n}", [P, QT, D]) for n in range(4)]
            f_stats = fsb("f_stats", [P, QT, 6])
            f_mv = [fsb(f"f_mv{n}", [P, QT, 2]) for n in range(2)]
            f_ve = [fsb(f"f_ve{n}", [P, QT]) for n in range(2)]
            f_rstd = [fsb(f"f_rstd{n}", [P, QT]) for n in range(2)]
            f_shift = [fsb(f"f_shift{n}", [P, QT]) for n in range(2)]
            f_out = [fsb(f"f_out{n}", [P, QT, D]) for n in range(4)]
            F = {n: sem("fin_" + n) for n in "sum res stats mv ve rstd shift out".split()}
            f_loaded = [sem(f"f_loaded{n}") for n in range(4)]
            f_stored = [sem(f"f_stored{n}") for n in range(4)]

            def loop_batches(engine, step):
                for u in range(4):
                    step(0, u)
                with engine.Fori(1, B // 4 - 1) as i:
                    for u in range(4):
                        step(i, u)
                for u in range(4):
                    step(B // 4 - 1, u)

            def last_batch(i, u):
                if u:
                    return i, u - 1
                return None if isinstance(i, int) and i == 0 else (i - 1, 3)

            def batch_rows(dram, first, engine):
                if not isinstance(first, int):
                    first = engine.snap(first)
                return dram[bass.ds(first, T), :].rearrange("(t p) d -> p t d", p=P)

            with nc.Block() as block:
                @block.sync
                def _(sp):
                    def load(i, u):
                        sources = [batch_rows(y_d, (i * 4 + u) * T + w * B * T, sp) for w in range(2)]
                        wait(sp, F["sum"], i * 4 + (u - 3))
                        for w in range(2):
                            sp.dma_start(y_in[u][w][:, :, :], sources[w]).then_inc(f_loaded[u], 16)
                    loop_batches(sp, load)

                @block.gpsimd
                def _(pool):
                    def rstd_of(i, u):
                        pool.wait_ge(F["mv"], (i * 4 + (u + 1)) * QT)
                        nc.gpsimd.tensor_tensor(f_ve[u % 2][:, :], f_mv[u % 2][:, :, 1], eps_t[:, :], ALU.add).then_inc(F["ve"], 1)
                        pool.wait_ge(F["ve"], i * 4 + (u + 1))
                        wait(pool, F["out"], (i * 4 + (u - 1)) * QT)
                        nc.gpsimd.tensor_tensor(f_rstd[u % 2][:, :], f_ve[u % 2][:, :], neg_half[:, :], ALU.pow).then_inc(F["rstd"], 1)

                    def step(i, u):
                        pool.wait_ge(f_loaded[u], i * 32 + 32)
                        wait(pool, F["res"], i * 4 + (u - 1))
                        nc.gpsimd.tensor_tensor(f_sum[u % 2][:, :, :], y_in[u][0][:, :, :], y_in[u][1][:, :, :], ALU.add).then_inc(F["sum"], 1)
                        if last_batch(i, u):
                            rstd_of(*last_batch(i, u))

                    loop_batches(pool, step)
                    rstd_of(B // 4 - 1, 3)

                @block.vector
                def _(dve):
                    def shift_of(i, u):
                        dve.wait_ge(F["rstd"], i * 4 + (u + 1))
                        wait(dve, F["out"], (i * 4 + (u - 1)) * QT)
                        wait(dve, F["shift"], i * 4 + u)
                        nc.vector.scalar_tensor_tensor(f_shift[u % 2][:, :], f_mv[u % 2][:, :, 0], -1.0, f_rstd[u % 2][:, :],
                                                       ALU.mult, ALU.mult).then_inc(F["shift"], 1)

                    def step(i, u):
                        dve.wait_ge(F["sum"], i * 4 + (u + 1))
                        wait(dve, F["out"], (i * 4 + (u - 3)) * QT)
                        rows = x1_sb[:, bass.ds(i * 4 + u, 1), :, :].rearrange("p b t d -> p (b t) d")
                        nc.vector.tensor_tensor(f_res[u][:, :, :], f_sum[u % 2][:, :, :], rows, ALU.add).then_inc(F["res"], 1)
                        dve.wait_ge(F["res"], i * 4 + (u + 1))
                        wait(dve, F["mv"], (i * 4 + u) * QT)
                        for t in range(QT):
                            nc.vector.bn_stats(f_stats[:, t, :], f_res[u][:, t, :]).then_inc(F["stats"], 1)
                        dve.wait_ge(F["stats"], (i * 4 + (u + 1)) * QT)
                        if last_batch(i, u):
                            shift_of(*last_batch(i, u))
                        for t in range(QT):
                            nc.vector.bn_aggr(f_mv[u % 2][:, t, :], f_stats[:, t, :]).then_inc(F["mv"], 1)

                    dve.wait_ge(x1_back, 16 * B)
                    loop_batches(dve, step)
                    shift_of(B // 4 - 1, 3)

                @block.scalar
                def _(act):
                    def store(i, u, rows):
                        act.wait_ge(F["out"], (i * 4 + (u + 1)) * QT)
                        act.dma_start(rows, f_out[u][:, :, :]).then_inc(f_stored[u], 16)

                    def step(i, u):
                        if last_batch(i, u):
                            last_i, last_u = last_batch(i, u)
                            rows = batch_rows(out_rows, (last_i * 4 + last_u) * T, act)
                        act.wait_ge(F["shift"], i * 4 + (u + 1))
                        wait(act, f_stored[u], i * 16)
                        for t in range(QT):
                            nc.scalar.activation(f_out[u][:, t, :], f_res[u][:, t, :], ACT.Identity, bias=f_shift[u % 2][:, t:t + 1],
                                                 scale=f_rstd[u % 2][:, t:t + 1]).then_inc(F["out"], 1)
                        if last_batch(i, u):
                            store(last_i, last_u, rows)

                    loop_batches(act, step)
                    store(B // 4 - 1, 3, batch_rows(out_rows, (B - 1) * T, act))
                    for n in range(4):
                        act.wait_ge(f_stored[n], 16 * (B // 4))


_INS = ["L0_attn_x", "L0_attn_Wq", "L0_attn_bq", "L0_attn_Wk", "L0_attn_bk", "L0_attn_Wv", "L0_attn_bv", "L0_attn_Wo",
        "L0_attn_bo", "L0_attn_U", "L0_attn_V", "L0_ffn_gate_w", "L0_ffn_w1", "L0_ffn_b1", "L0_ffn_w2", "L0_ffn_b2"]


def kernel(**inputs):
    import numpy as np
    import concourse.bacc as bacc
    from concourse.bass_utils import run_bass_kernel_spmd

    nc = bacc.Bacc("TRN2", target_bir_lowering=False, num_devices=1)
    arrays, args = {}, []
    for name in _INS:
        a = np.ascontiguousarray(inputs[name])
        arrays[name] = a
        args.append(nc.dram_tensor(name, a.shape, mybir.dt.from_np(a.dtype), kind="ExternalInput").ap())
    args.append(nc.dram_tensor("out", (B, T, D), mybir.dt.float32, kind="ExternalOutput").ap())
    build_layer(nc, *args)
    return run_bass_kernel_spmd(nc, [arrays], core_ids=[0]).results[0]["out"]
```
